# Optimizing a Trainium2 kernel written in Bass

```python
import numpy as np
import jax
import jax.numpy as jnp

def _softmax(x, axis=-1):
    return jax.nn.softmax(x, axis=axis)

def _gelu(x):
    return jax.nn.gelu(x, approximate=True)

def _silu(x):
    return jax.nn.silu(x)

def _sigmoid(x):
    return jax.nn.sigmoid(x)

def _layernorm(x, axis=-1, eps=1e-05):
    m = jnp.mean(x, axis=axis, keepdims=True)
    v = jnp.var(x, axis=axis, keepdims=True)
    return (x - m) / jnp.sqrt(v + eps)

def _scatter_add(tgt, idx, src, axis=0):
    return tgt.at[idx].add(src)

def _segment_sum(src, seg, n):
    return jax.ops.segment_sum(src, seg, n)
kernel_name = 'mk_flamingo_gated_d1_seqx_r4_81cfc3'

def setup_inputs(seed: int=0):
    np.random.seed(seed)
    _w = jnp.asarray

    def _rec_inputs():
        import jax
        import jax.numpy as jnp
        _rk = jax.random.key(seed)
        x = -0.0002928 + 1 * jax.random.normal(jax.random.fold_in(_rk, 1), (16, 256, 512), jnp.float32)
        _lenS = 256 - jax.random.randint(jax.random.fold_in(_rk, 7), (16,), 0, max(1, 256 // 4) + 1, jnp.int32)
        _lenS2 = 256 - jax.random.randint(jax.random.fold_in(_rk, 8), (16,), 0, max(1, 256 // 4) + 1, jnp.int32)
        _ctx_2048P = jax.random.normal(jax.random.fold_in(_rk, 11), (16, 16, 512), jnp.float32)
        _ctx_2048c = jax.random.dirichlet(jax.random.fold_in(_rk, 511), 0.3 * jnp.ones((16,), jnp.float32), (16, 256))
        _ctx_2048t = jnp.einsum('bsk,bkd->bsd', _ctx_2048c, _ctx_2048P)
        _ctx_2048t = _ctx_2048t * jax.lax.rsqrt(jnp.mean(jnp.square(_ctx_2048t)) + 1e-12) * 0.953939
        ctx_2048 = -1.39393e-06 + 0.999914 * (_ctx_2048t + 0.3 * jax.random.normal(jax.random.fold_in(_rk, 611), (16, 256, 512), jnp.float32))
        _g = jax.random.normal(jax.random.fold_in(_rk, 9001), (2, 1), jnp.float32)
        _g = jnp.sign(_g) * jnp.maximum(jnp.abs(_g), 1.0) + (_g == 0) * 1.0
        g_xattn = _g[0]
        g_ffn = _g[1]
        return (x, ctx_2048, g_xattn, g_ffn)
    x, ctx_2048, g_xattn, g_ffn = _rec_inputs()

    def _L0_xattn_setup():
        import jax, jax.numpy as jnp
        import numpy as np
        B, S, E, NH = (2, 256, 512, 16)
        DH = E // NH
        EPS = 1e-06

        def _mlstm_forward(q, k, v, Wi, bi, Wf, bf, ln_scale):
            b, s, e = q.shape
            nh = Wi.shape[1]
            dh = e // nh
            x = jnp.concatenate([q, k, v], axis=-1)
            ig = (x @ Wi + bi).transpose(0, 2, 1)[..., None]
            fg = (x @ Wf + bf).transpose(0, 2, 1)[..., None]
            split = lambda t: t.reshape(b, s, nh, dh).transpose(0, 2, 1, 3)
            qh, kh, vh = (split(q), split(k), split(v))
            log_f = jax.nn.log_sigmoid(fg)
            log_f_cum = jnp.concatenate([jnp.zeros((b, nh, 1, 1), q.dtype), jnp.cumsum(log_f, axis=2)], axis=2)
            fg_mat = log_f_cum - jnp.transpose(log_f_cum, (0, 1, 3, 2))
            ltr = jnp.tril(jnp.ones((s, s), dtype=bool))
            log_fg = jnp.where(ltr, fg_mat[:, :, 1:, 1:], -jnp.inf)
            log_D = log_fg + jnp.transpose(ig, (0, 1, 3, 2))
            max_log_D = jnp.max(log_D, axis=-1, keepdims=True)
            D = jnp.exp(log_D - max_log_D)
            qk = jnp.einsum('bhsd,bhtd->bhst', qh, kh) / jnp.sqrt(jnp.asarray(dh, q.dtype))
            C = qk * D
            normalizer = jnp.maximum(jnp.abs(C.sum(-1, keepdims=True)), jnp.exp(-max_log_D))
            Cn = C / (normalizer + EPS)
            h = jnp.einsum('bhst,bhtd->bhsd', Cn, vh)
            mu = h.mean(-1, keepdims=True)
            var = ((h - mu) ** 2).mean(-1, keepdims=True)
            hn = (h - mu) * jax.lax.rsqrt(var + EPS)
            hn = hn * ln_scale.reshape(1, nh, 1, dh)
            return hn.transpose(0, 2, 1, 3).reshape(b, s, e)
        key = jax.random.key(seed)
        ks = jax.random.split(key, 6)
        q = jax.random.normal(ks[0], (B, S, E), dtype=jnp.float32)
        k = jax.random.normal(ks[1], (B, S, E), dtype=jnp.float32)
        v = jax.random.normal(ks[2], (B, S, E), dtype=jnp.float32)
        Wi = jax.random.normal(ks[3], (3 * E, NH), dtype=jnp.float32) * 0.02
        bi = jax.random.normal(ks[4], (NH,), dtype=jnp.float32) * 0.1
        Wf = jax.random.normal(ks[5], (3 * E, NH), dtype=jnp.float32) * 0.02
        bf = jnp.linspace(3.0, 6.0, NH, dtype=jnp.float32)
        ln_scale = jnp.ones((E,), dtype=jnp.float32)
        return {'q': q, 'k': k, 'v': v, 'Wi': Wi, 'bi': bi, 'Wf': Wf, 'bf': bf, 'ln_scale': ln_scale}
    _L0_xattn_all = _L0_xattn_setup()
    _L0_xattn_in = {k: v for k, v in _L0_xattn_all.items() if k in ('Wi', 'bi', 'Wf', 'bf', 'ln_scale')}
    del _L0_xattn_all

    def _L0_ffn_setup():
        import jax, jax.numpy as jnp
        import numpy as np
        E = 16
        K = 2
        D = 512
        I = 352
        CAP = 256
        VOCAB = 32320
        key = jax.random.key(seed)
        ks = jax.random.split(key, 11)
        B, S = (4, 256)
        sd = 1.0 / np.sqrt(D)
        si = 1.0 / np.sqrt(I)
        return {'x': jax.random.normal(ks[0], (B, S, D), jnp.float32), 'input_ids': jax.random.randint(ks[1], (B, S), 0, VOCAB, dtype=jnp.int64), 'gate_w': jax.random.normal(ks[2], (E, D), jnp.float32) * sd, 'gate_b': jax.random.normal(ks[3], (E,), jnp.float32) * 0.01, 'W1': jax.random.normal(ks[4], (E, I, D), jnp.float32) * sd, 'W3': jax.random.normal(ks[5], (E, I, D), jnp.float32) * sd, 'W2': jax.random.normal(ks[6], (E, D, I), jnp.float32) * si, 'Ws1': jax.random.normal(ks[7], (I, D), jnp.float32) * sd, 'Ws3': jax.random.normal(ks[8], (I, D), jnp.float32) * sd, 'Ws2': jax.random.normal(ks[9], (D, I), jnp.float32) * si}
    _L0_ffn_all = _L0_ffn_setup()
    _L0_ffn_in = {k: v for k, v in _L0_ffn_all.items() if k in ('input_ids', 'gate_w', 'gate_b', 'W1', 'W3', 'W2', 'Ws1', 'Ws3', 'Ws2')}
    del _L0_ffn_all
    return {'x': x, 'ctx_2048': ctx_2048, 'g_xattn': g_xattn, 'g_ffn': g_ffn, 'L0_xattn_Wi': _L0_xattn_in['Wi'], 'L0_xattn_bi': _L0_xattn_in['bi'], 'L0_xattn_Wf': _L0_xattn_in['Wf'], 'L0_xattn_bf': _L0_xattn_in['bf'], 'L0_xattn_ln_scale': _L0_xattn_in['ln_scale'], 'L0_ffn_input_ids': _L0_ffn_in['input_ids'], 'L0_ffn_gate_w': _L0_ffn_in['gate_w'], 'L0_ffn_gate_b': _L0_ffn_in['gate_b'], 'L0_ffn_W1': _L0_ffn_in['W1'], 'L0_ffn_W3': _L0_ffn_in['W3'], 'L0_ffn_W2': _L0_ffn_in['W2'], 'L0_ffn_Ws1': _L0_ffn_in['Ws1'], 'L0_ffn_Ws3': _L0_ffn_in['Ws3'], 'L0_ffn_Ws2': _L0_ffn_in['Ws2']}

def reference(x, ctx_2048, g_xattn, g_ffn, L0_xattn_Wi, L0_xattn_bi, L0_xattn_Wf, L0_xattn_bf, L0_xattn_ln_scale, L0_ffn_input_ids, L0_ffn_gate_w, L0_ffn_gate_b, L0_ffn_W1, L0_ffn_W3, L0_ffn_W2, L0_ffn_Ws1, L0_ffn_Ws3, L0_ffn_Ws2):
    import jax
    import jax.numpy as jnp

    def _L0_xattn_ref(q, k, v, Wi, bi, Wf, bf, ln_scale):
        import jax, jax.numpy as jnp
        import numpy as np
        B, S, E, NH = (2, 256, 512, 16)
        DH = E // NH
        EPS = 1e-06

        def _mlstm_forward(q, k, v, Wi, bi, Wf, bf, ln_scale):
            b, s, e = q.shape
            nh = Wi.shape[1]
            dh = e // nh
            x = jnp.concatenate([q, k, v], axis=-1)
            ig = (x @ Wi + bi).transpose(0, 2, 1)[..., None]
            fg = (x @ Wf + bf).transpose(0, 2, 1)[..., None]
            split = lambda t: t.reshape(b, s, nh, dh).transpose(0, 2, 1, 3)
            qh, kh, vh = (split(q), split(k), split(v))
            log_f = jax.nn.log_sigmoid(fg)
            log_f_cum = jnp.concatenate([jnp.zeros((b, nh, 1, 1), q.dtype), jnp.cumsum(log_f, axis=2)], axis=2)
            fg_mat = log_f_cum - jnp.transpose(log_f_cum, (0, 1, 3, 2))
            ltr = jnp.tril(jnp.ones((s, s), dtype=bool))
            log_fg = jnp.where(ltr, fg_mat[:, :, 1:, 1:], -jnp.inf)
            log_D = log_fg + jnp.transpose(ig, (0, 1, 3, 2))
            max_log_D = jnp.max(log_D, axis=-1, keepdims=True)
            D = jnp.exp(log_D - max_log_D)
            qk = jnp.einsum('bhsd,bhtd->bhst', qh, kh) / jnp.sqrt(jnp.asarray(dh, q.dtype))
            C = qk * D
            normalizer = jnp.maximum(jnp.abs(C.sum(-1, keepdims=True)), jnp.exp(-max_log_D))
            Cn = C / (normalizer + EPS)
            h = jnp.einsum('bhst,bhtd->bhsd', Cn, vh)
            mu = h.mean(-1, keepdims=True)
            var = ((h - mu) ** 2).mean(-1, keepdims=True)
            hn = (h - mu) * jax.lax.rsqrt(var + EPS)
            hn = hn * ln_scale.reshape(1, nh, 1, dh)
            return hn.transpose(0, 2, 1, 3).reshape(b, s, e)
        return _mlstm_forward(q, k, v, Wi, bi, Wf, bf, ln_scale)

    def _L0_ffn_ref(x, input_ids, gate_w, gate_b, W1, W3, W2, Ws1, Ws3, Ws2):
        import jax, jax.numpy as jnp
        import numpy as np
        E = 16
        K = 2
        D = 512
        I = 352
        CAP = 256
        VOCAB = 32320
        shape = x.shape
        xt = x.reshape(-1, D)
        T = xt.shape[0]
        logits = xt.astype(jnp.float32) @ gate_w.astype(jnp.float32).T
        scores = jnp.sqrt(jax.nn.softplus(logits))
        _, idx = jax.lax.top_k(scores + gate_b, K)
        w = jnp.take_along_axis(scores, idx, axis=1)
        w = w / jnp.sum(w, axis=1, keepdims=True)
        e = idx.reshape(-1)
        onehot = jax.nn.one_hot(e, E, dtype=jnp.int32)
        pos = jnp.sum(onehot * (jnp.cumsum(onehot, axis=0) - 1), axis=1)
        valid = pos < CAP
        posc = jnp.where(valid, pos, 0)
        x_pairs = jnp.repeat(xt, K, axis=0)
        x_pairs = jnp.where(valid[:, None], x_pairs, 0.0)
        buf = jnp.zeros((E, CAP, D), xt.dtype).at[e, posc].add(x_pairs)
        g = jnp.einsum('ecd,eid->eci', buf, W1).astype(jnp.float32)
        u = jnp.einsum('ecd,eid->eci', buf, W3).astype(jnp.float32)
        h = (jax.nn.silu(g) * u).astype(xt.dtype)
        out = jnp.einsum('eci,edi->ecd', h, W2)
        y_pairs = out[e, posc] * (w.reshape(-1) * valid)[:, None]
        y = y_pairs.reshape(T, K, D).sum(axis=1)
        gs = jax.nn.silu((xt @ Ws1.T).astype(jnp.float32))
        us = (xt @ Ws3.T).astype(jnp.float32)
        shared = (gs * us).astype(xt.dtype) @ Ws2.T
        return (y + shared).astype(x.dtype).reshape(shape)
    x = x + jnp.tanh(g_xattn[0]) * _L0_xattn_ref(_layernorm(x, axis=-1), ctx_2048, ctx_2048, L0_xattn_Wi, L0_xattn_bi, L0_xattn_Wf, L0_xattn_bf, L0_xattn_ln_scale)
    x = x + jnp.tanh(g_ffn[0]) * _L0_ffn_ref(_layernorm(x, axis=-1), L0_ffn_input_ids, L0_ffn_gate_w, L0_ffn_gate_b, L0_ffn_W1, L0_ffn_W3, L0_ffn_W2, L0_ffn_Ws1, L0_ffn_Ws3, L0_ffn_Ws2)
    return x

_drawn_inputs = setup_inputs


def setup_inputs(seed=0):
    import zlib

    import numpy as np

    out = dict(_drawn_inputs(seed))
    spreads = {'L0_xattn_ln_scale': (1.0, 0.2)}
    factors = {'L0_xattn_bi': 64.0}
    for name, (base, spread) in spreads.items():
        noise = np.random.default_rng([zlib.crc32(name.encode()), seed]).standard_normal(out[name].shape)
        drawn = base * np.exp(spread * noise) if base else spread * noise
        out[name] = jnp.asarray(drawn.astype(out[name].dtype))
    for name, factor in factors.items():
        out[name] = (out[name] * factor).astype(out[name].dtype)
    return out
```

```python
from contextlib import ExitStack

import numpy as np

import concourse.bass as bass
from concourse import mybir

F32 = mybir.dt.float32
F32R = mybir.dt.float32r
BF16 = mybir.dt.bfloat16
U32 = mybir.dt.uint32
ACT = mybir.ActivationFunctionType
ALU = mybir.AluOpType
AX = mybir.AxisListType

P = 128
B, S, D = 16, 256, 512
NH, DH = 16, 32
NT = B * S // P
DC = D // P
E, FI, CAP = 16, 352, 256
FC = -(-FI // P)
FLAST = FI - (FC - 1) * P
HB = B // 2
LN_EPS, CELL_EPS = 1e-5, 1e-6
SCALE = float(DH) ** -0.5
MASKED = -1e30
SMALL_E = 0.01
NOWHERE = 1.0e6


class Chain:

    def __init__(self, eng, sem):
        self.eng, self.sem, self.n, self.base = eng, sem, 0, 0

    def link(self, ins):
        self.n += 1
        ins.then_inc(self.sem, 1)
        self.eng.wait_ge(self.sem, self.base + self.n)

    def enter(self, i, per):
        self.static = self.n + self.base
        self.base, self.n, self.per = i * per + self.static, 0, per

    def leave(self, rounds):
        assert self.n == self.per, (self.n, self.per)
        self.base, self.n = 0, self.static + self.per * rounds


class Pools:

    def __init__(self, nc, ctx):
        self.nc, self.ctx = nc, ctx

    def sb(self, name, shape, dt=F32):
        return self.ctx.enter_context(self.nc.sbuf_tensor(name, shape, dt))

    def ps(self, name, shape, dt=F32):
        return self.ctx.enter_context(self.nc.psum_tensor(name, shape, dt))

    def sem(self, name):
        return self.ctx.enter_context(self.nc.semaphore(name))


def setup_stage(nc, g, d):
    with ExitStack() as ctx:
        a = Pools(nc, ctx)
        zeros = a.sb("zeros", [P, D])
        wkv = a.sb("wkv", [P, 2, DC, 2 * NH])
        gt = a.sb("gt", [P, 2])
        loaded, zeroed, table_zeroed, const, th, ch = map(
            a.sem, ("s0_loaded", "s0_zeroed", "s0_table", "s0_const", "s0_tanh", "s0_chain"))
        block = ctx.enter_context(nc.Block())

        @block.sync
        def _(sp):
            loads = [
                (g.wg[:, :, :], d.wgate[0].rearrange("(c p) n -> p c n", p=P)),
                (wkv[:, 0, :, :], d.wgate[1].rearrange("(c p) n -> p c n", p=P)),
                (wkv[:, 1, :, :], d.wgate[2].rearrange("(c p) n -> p c n", p=P)),
                (g.wr[:, :, :], d.gate_wT.rearrange("(c p) n -> p c n", p=P)),
                (g.bias[:, :], d.gbias.to_broadcast([P, 2 * NH])),
                (g.coef[:, :], d.ln_scale.to_broadcast([P, D])),
                (g.gate_b[:, :], d.gate_b.to_broadcast([P, E])),
                (gt[:, 0:1], d.g_xattn.to_broadcast([P, 1])),
                (gt[:, 1:2], d.g_ffn.to_broadcast([P, 1])),
            ]
            for dst, src in loads:
                sp.dma_start(dst, src).then_inc(loaded, 16)
            sp.wait_ge(zeroed, 1)
            for t in range(NT):
                sp.dma_start(d.disp[t * P:(t + 1) * P, :], zeros[:, :]).then_inc(table_zeroed, 16)
            sp.wait_ge(table_zeroed, 16 * NT)
            sp.wait_ge(loaded, 16 * len(loads))

        @block.gpsimd
        def _(pool):
            c = Chain(pool, const)
            c.link(nc.gpsimd.memset(g.ident[:, :], 0.0))
            c.link(nc.gpsimd.affine_select(out=g.ident[:, :], in_=g.ident[:, :], compare_op=ALU.not_equal, fill=1.0,
                                           base=0, pattern=[[-1, P]], channel_multiplier=1))
            c.link(nc.gpsimd.tensor_copy(g.identb[:, :], g.ident[:, :]))
            c.link(nc.gpsimd.memset(g.causal[:, :, :], 0.0))
            c.link(nc.gpsimd.affine_select(out=g.causal[:, :, :], in_=g.causal[:, :, :], compare_op=ALU.is_ge,
                                           fill=MASKED, base=0, pattern=[[0, 4], [1, P]], channel_multiplier=-1))
            c.link(nc.gpsimd.memset(g.before[:, :], 1.0))
            c.link(nc.gpsimd.affine_select(out=g.before[:, :], in_=g.before[:, :], compare_op=ALU.is_gt,
                                           fill=0.0, base=0, pattern=[[1, P]], channel_multiplier=-1))
            c.link(nc.gpsimd.memset(g.onesb[:, :], 1.0))
            c.link(nc.gpsimd.memset(g.neghalf[:, :], -0.5))
            c.link(nc.gpsimd.iota(g.eiota[:, :], pattern=[[1, E]], base=0, channel_multiplier=0,
                                  allow_small_or_imprecise_dtypes=True))

        @block.scalar
        def _(act):
            act.wait_ge(loaded, 16 * 9)
            nc.scalar.activation(g.tanh[:, :], gt[:, :], ACT.Tanh).then_inc(th, 1)

        @block.vector
        def _(dve):
            nc.vector.memset(zeros[:, :], 0.0).then_inc(zeroed, 1)
            dve.wait_ge(loaded, 16 * 9)
            nc.vector.tensor_tensor(g.wc[:, :, :], wkv[:, 0, :, :], wkv[:, 1, :, :], ALU.add)
            dve.wait_ge(th, 1)
            nc.vector.tensor_scalar(g.coef[:, :], g.coef[:, :], g.tanh[:, 0:1], None, ALU.mult).then_inc(ch, 1)


def norm_project_stage(nc, g, d, first):
    tag = "g" if first else "r"
    width = 2 * NH if first else E
    with ExitStack() as ctx:
        a = Pools(nc, ctx)
        stats = a.sb(tag + "stats", [P, 2, 4, 6])
        mv = a.sb(tag + "mv", [P, 2, 4, 2])
        var = a.sb(tag + "var", [P, 2, 4])
        xn = a.sb(tag + "xn", [P, 2, 4, D])
        xT = [a.sb(f"{tag}xT{k}", [P, DC, S]) for k in range(2)]
        cT = [a.sb(f"{tag}cT{k}", [P, 2, DC, S]) for k in range(2)] if first else None
        psT = [a.ps(f"{tag}psT{k}", [P, DC, S]) for k in range(2)]
        psG = [a.ps(f"{tag}psG{k}", [P, 2, 256]) for k in range(2)]
        x_in = [a.sem(f"{tag}_x_in{k}") for k in range(2)]
        c_in = [a.sem(f"{tag}_c_in{k}") for k in range(2)]
        chain, var_ready, rs_ready, xn_ready, turned, xt_ready, projected, kept = map(
            a.sem, [f"{tag}_{n}" for n in
                    ("chain", "var_ready", "rs_ready", "xn_ready", "turned", "xt_ready", "projected", "kept")])
        block = ctx.enter_context(nc.Block())
        ROUNDS = B // 4

        if first:
            @block.sync
            def _(sp):
                with sp.Fori(0, ROUNDS) as i:
                    for s in range(2):
                        b0 = 4 * i + 2 * s
                        sp.wait_ge(projected, 4 * i + 2 * s + 2)
                        sp.dma_start(g.xres[:, bass.ds(2 * b0, 4), :],
                                     d.x[bass.ds(b0, 2)].rearrange("b (t p) d -> p (b t) d", p=P)).then_inc(x_in[s], 16)
                        sp.dma_start(cT[s][:, :, :, :],
                                     d.ctxT[bass.ds(b0, 2)].rearrange("b (c p) t -> p b c t", p=P)).then_inc(c_in[s], 16)

        @block.vector
        def _(dve):
            c = Chain(dve, chain)
            with dve.Fori(0, ROUNDS) as i:
                c.enter(i, 6)
                for s in range(2):
                    t0 = 8 * i + 4 * s
                    if first:
                        dve.wait_ge(x_in[s], 16 * i + 16)
                    for k in range(4):
                        last = nc.vector.bn_stats(stats[:, s, k, :], g.xres[:, bass.ds(t0 + k, 1), :].rearrange("p a d -> p (a d)"))
                    c.link(last)
                    nc.vector.memset(g.idle[:, 0:1], 0.0)
                    for k in range(4):
                        last = nc.vector.bn_aggr(mv[:, s, k, :], stats[:, s, k, :])
                    c.link(last)
                    nc.vector.tensor_copy(g.mu_all[:, bass.ds(t0, 4)], mv[:, s, :, 0])
                    c.link(nc.vector.tensor_scalar(var[:, s, :], mv[:, s, :, 1], LN_EPS, None, ALU.add))
                    nc.vector.sem_inc(var_ready, 1)
                    dve.wait_ge(rs_ready, 2 * i + s + 1)
                    nc.vector.tensor_copy(g.rs_all[:, bass.ds(t0, 4)], g.rs_stage[:, s, :])
                    dve.wait_ge(turned, 4 * i + 2 * s + 2)
                    for k in range(4):
                        last = nc.vector.tensor_scalar(xn[:, s, k, :], g.xres[:, bass.ds(t0 + k, 1), :].rearrange("p a d -> p (a d)"),
                                                       mv[:, s, k, 0:1], g.rs_stage[:, s, k:k + 1],
                                                       ALU.subtract, ALU.mult)
                    last.then_inc(xn_ready, 1)
                c.leave(ROUNDS)

        @block.gpsimd
        def _(pool):
            with pool.Fori(0, ROUNDS) as i:
                for s in range(2):
                    pool.wait_ge(var_ready, 2 * i + s + 1)
                    nc.gpsimd.tensor_tensor(g.rs_stage[:, s, :], var[:, s, :], g.neghalf[:, 0:4], ALU.pow).then_inc(rs_ready, 1)

        @block.tensor
        def _(pe):
            nc.tensor.sem_inc(turned, 4)
            nc.tensor.sem_inc(projected, 4)
            with pe.Fori(0, ROUNDS) as i:
                for s in range(2):
                    pe.wait_ge(xn_ready, 2 * i + s + 1)
                    for k in range(2):
                        n = 4 * i + 2 * s + k
                        pe.wait_ge(xt_ready, n + 1)
                        for c in range(DC):
                            for j in range(2):
                                last = nc.tensor.transpose(psT[k][:, c, j * P:(j + 1) * P],
                                                           xn[:, s, 2 * k + j, c * P:(c + 1) * P], g.ident[:, :])
                        last.then_inc(turned, 1)
                    for k in range(2):
                        n = 4 * i + 2 * s + k
                        pe.wait_ge(xt_ready, n + 3)
                        if first and k == 0:
                            pe.wait_ge(c_in[s], 16 * i + 16)
                        pe.wait_ge(kept, n + 1)
                        for j in range(2):
                            for c in range(DC):
                                last = nc.tensor.matmul(psG[k][:, j, 0:width], xT[k][:, c, j * P:(j + 1) * P],
                                                        (g.wg if first else g.wr)[:, c, :],
                                                        start=(c == 0), stop=(not first and c == DC - 1))
                            if first:
                                for c in range(DC):
                                    last = nc.tensor.matmul(psG[k][:, j, 0:width], cT[s][:, k, c, j * P:(j + 1) * P],
                                                            g.wc[:, c, :], start=False, stop=(c == DC - 1))
                        last.then_inc(projected, 1)

        @block.scalar
        def _(act):
            nc.scalar.sem_inc(xt_ready, 2)
            nc.scalar.sem_inc(kept, 2)
            with act.Fori(0, ROUNDS) as i:
                for s in range(2):
                    for k in range(2):
                        n = 4 * i + 2 * s + k
                        act.wait_ge(turned, n + 5)
                        act.wait_ge(projected, n + 3)
                        if first:
                            nc.scalar.activation(g.qT_all[:, bass.ds(n * DC, DC), :], psT[k][:, :, :], ACT.Copy)
                        nc.scalar.activation(xT[k][:, :, :], psT[k][:, :, :], ACT.Copy).then_inc(xt_ready, 1)
                    for k in range(2):
                        n = 4 * i + 2 * s + k
                        act.wait_ge(projected, n + 5)
                        for j in range(2):
                            if first:
                                out = g.gates[:, j, :, bass.ds(n * NH, NH)]
                                src = psG[k][:, j, 0:width].rearrange("p (a h) -> p a h", a=2)
                            else:
                                out = g.logits[:, bass.ds(2 * n + j, 1), :].rearrange("p a e -> p (a e)")
                                src = psG[k][:, j, 0:width]
                            last = nc.scalar.activation(out, src, ACT.Copy)
                        last.then_inc(kept, 1)


def log1p_exp(nc, c, e, log_u, poly, mask):
    c.link(nc.vector.tensor_scalar(poly, e, -0.25, 1.0 / 3.0, ALU.mult, ALU.add))
    c.link(nc.vector.scalar_tensor_tensor(out=poly, in0=poly, scalar=-1.0, in1=e, op0=ALU.mult, op1=ALU.mult))
    c.link(nc.vector.scalar_tensor_tensor(out=poly, in0=poly, scalar=0.5, in1=e, op0=ALU.add, op1=ALU.mult))
    c.link(nc.vector.scalar_tensor_tensor(out=poly, in0=poly, scalar=1.0, in1=e, op0=ALU.subtract, op1=ALU.mult))
    c.link(nc.vector.tensor_scalar(mask, e, SMALL_E, None, ALU.is_lt))
    c.link(nc.vector.scalar_tensor_tensor(out=poly, in0=poly, scalar=-1.0, in1=log_u, op0=ALU.mult, op1=ALU.subtract))
    c.link(nc.vector.tensor_tensor(poly, poly, mask, ALU.mult))
    c.link(nc.vector.tensor_tensor(log_u, log_u, poly, ALU.add))


def gate_stage(nc, g, d):
    with ExitStack() as ctx:
        a = Pools(nc, ctx)
        e = a.sb("ge", [P, 2, B * NH])
        lu = a.sb("glu", [P, 2, B * NH])
        poly = a.sb("gpoly", [P, 2, B * NH])
        mask = a.sb("gmask", [P, 2, B * NH])
        ones = a.sb("gones", [P, S])
        head = a.sb("ghead", [P, 2, 2, S])
        F = a.sb("gF", [P, 2, S])
        am = a.sb("gam", [P, 2, 2, S])
        M = a.sb("gM", [P, 2, S])
        m = a.sb("gm", [P, 2, S])
        ex = a.sb("gex", [P, 2, 4, P])
        rest = a.sb("grest", [P, 2, 2, S])
        parts = a.sb("gparts", [P, 2, 2, 3, S], BF16)
        psH = [a.ps(f"gpsH{k}", [P, 2, S]) for k in range(2)]
        psE = [a.ps(f"gpsE{k}", [P, 4, P]) for k in range(2)]
        chain, abs_ready, e_ready, lf_ready, heads, exps_go, exps, ex_turned, parts_ready, saved, pch = map(
            a.sem, ["gt_" + n for n in ("chain", "abs", "e", "lf", "heads", "exps_go", "exps", "ex_turned",
                                        "parts", "saved", "pool")])
        block = ctx.enter_context(nc.Block())

        @block.vector
        def _(dve):
            c = Chain(dve, chain)
            f = g.gates[:, :, 1, :]
            for j in range(2):
                gj = g.gates[:, j, :, :].rearrange("p a (b h) -> p a b h", h=NH)
                bias = g.bias[:, :].rearrange("p (a o h) -> p a o h", a=2, o=1).broadcast_to([P, 2, B, NH])
                last = nc.vector.tensor_tensor(gj, gj, bias, ALU.add)
            c.link(last)
            nc.vector.memset(ones[:, :], 1.0)
            nc.vector.scalar_tensor_tensor(out=poly[:, :, :], in0=f, scalar=-1.0, in1=f, op0=ALU.mult,
                                           op1=ALU.max).then_inc(abs_ready, 1)
            dve.wait_ge(e_ready, 2)
            log1p_exp(nc, c, e[:, :, :], lu[:, :, :], poly[:, :, :], mask[:, :, :])
            nc.vector.scalar_tensor_tensor(out=f, in0=f, scalar=0.0, in1=lu[:, :, :], op0=ALU.min,
                                           op1=ALU.subtract).then_inc(lf_ready, 1)
            for k in range(2):
                dve.wait_ge(heads, k + 1)
                c.link(nc.vector.tensor_copy(head[:, k, :, :], psH[k][:, :, :]))
                c.link(nc.vector.tensor_tensor_scan(F[:, k, :], ones[:, :], head[:, k, 1, :], 0.0, ALU.mult, ALU.add))
                c.link(nc.vector.tensor_tensor(am[:, k, 0, :], head[:, k, 0, :], F[:, k, :], ALU.subtract))
                c.link(nc.vector.tensor_tensor_scan(M[:, k, :], am[:, k, 0, :], am[:, k, 0, :], -3.0e38, ALU.max, ALU.max))
                nc.vector.tensor_scalar(am[:, k, 1, :], M[:, k, :], -1.0, None, ALU.mult)
                nc.vector.tensor_tensor(m[:, k, :], F[:, k, :], M[:, k, :], ALU.add).then_inc(exps_go, 1)
            for k in range(2):
                dve.wait_ge(ex_turned, k + 1)
                nc.vector.tensor_copy(g.tmE[:, :, k * P:(k + 1) * P], psE[k][:, :, :])

        @block.scalar
        def _(act):
            act.wait_ge(abs_ready, 1)
            nc.scalar.activation(e[:, :, :], poly[:, :, :], ACT.Exp, scale=-1.0).then_inc(e_ready, 1)
            act.wait_ge(e_ready, 1)
            nc.scalar.activation(lu[:, :, :], e[:, :, :], ACT.Ln, bias=1.0).then_inc(e_ready, 1)
            for k in range(2):
                act.wait_ge(exps_go, k + 1)
                nc.scalar.activation(ex[:, k, 0, :], am[:, k, 0, 0:P], ACT.Exp, bias=am[:, k, 1, P - 1:P])
                nc.scalar.activation(ex[:, k, 1, :], am[:, k, 1, P:S], ACT.Exp, bias=M[:, k, P - 1:P])
                nc.scalar.activation(ex[:, k, 2:4, :].rearrange("p a t -> p (a t)"), m[:, k, :], ACT.Exp,
                                     scale=-1.0).then_inc(exps, 1)

        @block.tensor
        def _(pe):
            pe.wait_ge(lf_ready, 1)
            for k in range(2):
                for gi in range(2):
                    for j in range(2):
                        last = nc.tensor.transpose(psH[k][:, gi, j * P:(j + 1) * P],
                                                   g.gates[:, j, gi, k * P:(k + 1) * P], g.ident[:, :])
                last.then_inc(heads, 1)
            for k in range(2):
                pe.wait_ge(exps, k + 1)
                for q in range(4):
                    last = nc.tensor.transpose(psE[k][:, q, :], ex[:, k, q, :], g.ident[:, :])
                last.then_inc(ex_turned, 1)

        @block.gpsimd
        def _(pool):
            c = Chain(pool, pch)
            pool.wait_ge(exps_go, 2)
            for q in range(3):
                src = am if q == 0 else rest
                c.link(nc.gpsimd.tensor_copy(parts[:, :, :, q, :], src[:, :, :, :]))
                if q < 2:
                    c.link(nc.gpsimd.tensor_tensor(rest[:, :, :, :], src[:, :, :, :], parts[:, :, :, q, :], ALU.subtract))
            nc.gpsimd.sem_inc(parts_ready, 1)

        @block.sync
        def _(sp):
            sp.wait_ge(parts_ready, 1)
            for k in range(2):
                for w in range(2):
                    sp.dma_start(d.am[w].rearrange("q b h t -> (b h) q t")[k * P:(k + 1) * P], parts[:, k, w, :, :]).then_inc(saved, 16)
            sp.wait_ge(saved, 64)


def attention_stage(nc, g, d):
    with ExitStack() as ctx:
        a = Pools(nc, ctx)
        ctxs = a.sb("ctxs", [P, 2, D])
        kT = [a.sb(f"kT{k}", [P, DC, S]) for k in range(2)]
        vaug = [a.sb(f"vaug{k}", [P, 2, NH, DH + 1]) for k in range(2)]
        kkw = a.sb("kkw", [P, NH, DH])
        qst = [a.sb(f"qst{k}", [P, DC, S]) for k in range(2)]
        aml = a.sb("aml", [38, NH, P], BF16)
        amr = a.sb("amr", [38, NH, P], BF16)
        dec = [a.sb(f"dec{k}", [P, 4, 4, P]) for k in range(2)]
        state = a.sb("state", [P, DC, 4, DH + 1])
        num = [a.sb(f"num{k}", [P, NH, DH + 1]) for k in range(2)]
        cen = [a.sb(f"cen{k}", [P, NH, DH]) for k in range(4)]
        sm = a.sb("sm", [P, 4, 8, NH])
        psQ = a.ps("psQ", [P, 4, 512])
        psL = [a.ps(f"psL{k}", [P, 4, P]) for k in range(2)]
        psO = a.ps("psO", [P, 2, 512])
        (chain, am_done, dec_ready, qk_done, c_done, pv_done, si_done, si_evac, num_ready, cen_ready, sq_ready,
         ve_ready, hn_ready, x_done, v_ready, kk_ready, qs_ready, pch, ones_set, state_zero) = map(
            a.sem, ["at_" + n for n in (
                "chain", "am_done", "dec_ready", "qk_done", "c_done", "pv_done", "si_done", "si_evac", "num_ready",
                "cen_ready", "sq_ready", "ve_ready", "hn_ready", "x_done", "v_ready", "kk_ready", "qs_ready", "pool",
                "ones_set", "state_zero")])
        ctx_in = a.sem("at_ctx_in")
        kT_in = [a.sem(f"at_kT_in{k}") for k in range(2)]
        am_in = [a.sem(f"at_am_in{k}") for k in range(2)]
        block = ctx.enter_context(nc.Block())
        R0, RPL, LOOPS = 3, 4, 7
        assert R0 + RPL * LOOPS + 1 == NT

        def run(eng, chain_obj, per, step, drain):
            for r in range(R0):
                step(0, r, False)
            with eng.Fori(0, LOOPS) as i:
                if chain_obj:
                    chain_obj.enter(i, per)
                for r in range(R0, R0 + RPL):
                    step(i, r, False)
                if chain_obj:
                    chain_obj.leave(LOOPS)
            step(LOOPS, R0, True)
            drain(LOOPS, R0)

        @block.sync
        def _(sp):
            def load_ctx(b):
                sp.dma_start(ctxs[:, :, :], d.ctx[bass.ds(b, 1)].rearrange("b (t p) d -> p (b t) d", p=P)).then_inc(ctx_in, 16)

            def load_keys(b, u):
                sp.dma_start(kT[u][:, :, :], d.ctxT[bass.ds(b, 1)].rearrange("b (c p) t -> p (b c) t", p=P)).then_inc(kT_in[u], 16)

            def load_decay(b, c):
                lo = 32 * c
                sp.dma_start(aml[lo + 3:lo + 6, :, :], d.am[0][:, bass.ds(b, 1), :, c * P:(c + 1) * P].rearrange(
                    "q b h t -> q (b h) t")).then_inc(am_in[c], 16)
                sp.dma_start(amr[lo:lo + 3, :, :], d.am[1][:, bass.ds(b, 1), :, c * P:(c + 1) * P].rearrange(
                    "q b h t -> q (b h) t")).then_inc(am_in[c], 16)
            sp.wait_ge(ones_set, 1)
            load_decay(0, 0)
            load_keys(0, 0)
            load_ctx(0)
            load_decay(0, 1)

            def load(b, u, earlier):
                sp.wait_ge(am_done, 8 * b - 4)
                load_decay(b, 0)
                if earlier:
                    sp.wait_ge(qk_done, 2 * b - 2)
                load_keys(b, u)
                sp.wait_ge(v_ready, b)
                sp.wait_ge(kk_ready, b)
                load_ctx(b)
                sp.wait_ge(am_done, 8 * b)
                load_decay(b, 1)
            load(1, 1, False)
            with sp.Fori(0, B // 2 - 1) as i:
                load(2 * i + 2, 0, True)
                load(2 * i + 3, 1, True)

        @block.tensor
        def _(pe):
            def decay(i, r):
                n = 4 * i + r
                u, c = (r // 2) % 2, r % 2
                pe.wait_ge(am_in[c], 64 * i + 32 * (r // 2 + 1))
                for k in range(4):
                    if 4 * r + k >= 2:
                        pe.wait_ge(dec_ready, 4 * n + k - 1)
                    for gg in range(4):
                        h = 4 * gg + k
                        nc.tensor.matmul(psL[k % 2][:, gg, :], aml[32 * c:32 * c + 6, h, :],
                                                amr[32 * c:32 * c + 6, h, :], start=(gg == 0), stop=(gg == 3), skip_group_check=True)
                    nc.tensor.matmul(psL[k % 2][:, :, :], g.identb[:, :], g.causal[:, :, :], start=False, stop=True,
                                     skip_group_check=True).then_inc(am_done, 1)

            def scores(i, r):
                n = 4 * i + r
                u, c = (r // 2) % 2, r % 2
                if c == 0:
                    pe.wait_ge(kT_in[u], 16 * i + 16 * (r // 4 + 1))
                    pe.wait_ge(qs_ready, 2 * i + r // 2 + 1)
                if r >= 1:
                    pe.wait_ge(c_done, 4 * n)
                for gg in range(4):
                    for k in range(4):
                        last = nc.tensor.matmul(psQ[:, k, gg * P:(gg + 1) * P], kT[u][32 * k:32 * k + 32, gg, c * P:(c + 1) * P],
                                                qst[u][32 * k:32 * k + 32, gg, c * P:(c + 1) * P], start=True, stop=True)
                last.then_inc(qk_done, 1)

            def values(i, r):
                n = 4 * i + r
                u, c = (r // 2) % 2, r % 2
                pe.wait_ge(c_done, 4 * n + 4)
                pe.wait_ge(si_evac, n + 1)
                for h in range(NH):
                    last = nc.tensor.matmul(psO[:, h // 8, (h % 8) * 33:(h % 8) * 33 + 33], dec[c][:, h % 4, h // 4, :],
                                            vaug[u][:, c, h, :], start=True, stop=True)
                last.then_inc(pv_done, 1)

            def carry(i, r):
                n = 4 * i + r
                u, c = (r // 2) % 2, r % 2
                if r >= 1:
                    pe.wait_ge(num_ready, n)
                if c == 0:
                    pe.wait_ge(kk_ready, 2 * i + r // 2 + 1)
                    pe.wait_ge(v_ready, 2 * i + r // 2 + 1)
                    for gg in range(4):
                        last = nc.tensor.matmul(psO[:, gg // 2, (gg % 2) * 132:(gg % 2) * 132 + 132],
                                                kkw[:, 4 * gg:4 * gg + 4, :].rearrange("p h d -> p (h d)"),
                                                vaug[u][:, 0, 4 * gg:4 * gg + 4, :].rearrange("p h d -> p (h d)"),
                                                start=True, stop=True)
                else:
                    for gg in range(4):
                        last = nc.tensor.matmul(psO[:, gg // 2, (gg % 2) * 132:(gg % 2) * 132 + 132], qst[u][:, gg, P:S],
                                                state[:, gg, :, :].rearrange("p h d -> p (h d)"), start=True, stop=True)
                last.then_inc(si_done, 1)

            decay(0, 0)

            def step(i, r, is_last):
                scores(i, r)
                if r >= 1:
                    values(i, r - 1)
                if not is_last:
                    decay(i, r + 1)
                carry(i, r)
            run(pe, None, 0, step, values)

        @block.scalar
        def _(act):
            def exps(i, r):
                n = 4 * i + r
                c = r % 2
                for k in range(4):
                    act.wait_ge(am_done, 4 * n + k + 1)
                    if r >= 2 and k == 0:
                        act.wait_ge(pv_done, n - 1)
                    nc.scalar.activation(dec[c][:, k, :, :], psL[k % 2][:, :, :], ACT.Exp).then_inc(dec_ready, 1)

            def values(i, r):
                n, b, u = 4 * i + r, 2 * i + r // 2, (r // 2) % 2
                if r >= 4:
                    act.wait_ge(pv_done, n - 2)
                    act.wait_ge(si_done, n - 2)
                nc.scalar.activation(qst[u][:, :, :], g.qT_all[:, bass.ds(b * DC, DC), :], ACT.Copy).then_inc(qs_ready, 1)
                act.wait_ge(ctx_in, 32 * i + 16 * (r // 2 + 1))
                nc.scalar.activation(vaug[u][:, :, :, 0:DH], ctxs[:, :, :].rearrange("p t (h d) -> p t h d", d=DH),
                                     ACT.Copy).then_inc(v_ready, 1)

            def square(i, r):
                n = 4 * i + r
                act.wait_ge(cen_ready, n + 1)
                nc.scalar.activation(num[r % 2][:, :, 0:DH], cen[r % 4][:, :, :], ACT.Square).then_inc(sq_ready, 1)
            act.wait_ge(ones_set, 1)
            values(0, 0)
            exps(0, 0)

            def step(i, r, is_last):
                if not is_last:
                    exps(i, r + 1)
                if r % 2 == 1 and not is_last:
                    values(i, r + 1)
                if r >= 1:
                    square(i, r - 1)
            run(act, None, 0, step, square)

        @block.vector
        def _(dve):
            c_ = Chain(dve, chain)

            def weigh(i, r):
                n = 4 * i + r
                c = r % 2
                dve.wait_ge(qk_done, n + 1)
                for k in range(4):
                    dve.wait_ge(dec_ready, 4 * n + k + 1)
                    dk = dec[c][:, k, :, :].rearrange("p a t -> p (a t)")
                    nc.vector.scalar_tensor_tensor(out=dk, in0=psQ[:, k, :], scalar=SCALE, in1=dk,
                                                   op0=ALU.mult, op1=ALU.mult).then_inc(c_done, 1)

            def gather(i, r):
                n = 4 * i + r
                c = r % 2
                dve.wait_ge(pv_done, n + 1)
                o = psO[:, :, 0:264].rearrange("p a (h e) -> p a h e", e=33)
                nm = num[c][:, :, :].rearrange("p (a h) e -> p a h e", a=2)
                if c == 0:
                    c_.link(nc.vector.tensor_copy(nm, o))
                else:
                    c_.link(nc.vector.tensor_tensor(nm, num[1][:, :, :].rearrange("p (a h) e -> p a h e", a=2), o, ALU.add))
                nc.vector.sem_inc(num_ready, 1)

            def carry(i, r):
                n = 4 * i + r
                c = r % 2
                dve.wait_ge(si_done, n + 1)
                if c == 0:
                    for k in range(4):
                        src = psO[32 * k:32 * k + 32, :, 0:264].rearrange("p a (g h e) -> p a g h e", g=2, e=33)[:, :, :, k, :]
                        dst = state[32 * k:32 * k + 32, :, k, :].rearrange("p (a g) e -> p a g e", a=2)
                        last = nc.vector.tensor_scalar(dst, src, SCALE, None, ALU.mult)
                    last.then_inc(si_evac, 1)
                else:
                    o = psO[:, :, 0:264].rearrange("p a (h e) -> p a h e", e=33)
                    em = tm(1, i, r).rearrange("p (a h o) -> p a h o", a=2, o=1).broadcast_to([P, 2, 8, 33])
                    nc.vector.tensor_tensor(num[1][:, :, :].rearrange("p (a h) e -> p a h e", a=2), o, em,
                                            ALU.mult).then_inc(si_evac, 1)

            def tm(kind, i, r):
                return g.tmE[:, kind, bass.ds((2 * i + r // 2) * NH, NH)]

            def centre(i, r):
                n = 4 * i + r
                c, q = r % 2, r % 4
                v = sm[:, q]
                c_.link(nc.vector.tensor_reduce(v[:, 0, :], num[c][:, :, 0:DH], AX.X, ALU.add))
                c_.link(nc.vector.tensor_scalar(v[:, 1, :], v[:, 0, :], 1.0 / DH, None, ALU.mult))
                nc.vector.tensor_tensor(cen[q][:, :, :], num[c][:, :, 0:DH],
                                        v[:, 1, :].rearrange("p (h o) -> p h o", o=1).broadcast_to([P, NH, DH]),
                                        ALU.subtract).then_inc(cen_ready, 1)
                total = num[c][:, :, DH]
                c_.link(nc.vector.scalar_tensor_tensor(out=v[:, 2, :], in0=total, scalar=-1.0, in1=total,
                                                       op0=ALU.mult, op1=ALU.max))
                c_.link(nc.vector.tensor_tensor(v[:, 2, :], v[:, 2, :], tm(2 + c, i, r), ALU.max))
                c_.link(nc.vector.tensor_scalar(v[:, 2, :], v[:, 2, :], CELL_EPS, None, ALU.add))
                c_.link(nc.vector.reciprocal(v[:, 3, :], v[:, 2, :]))
                c_.link(nc.vector.tensor_tensor(v[:, 4, :], v[:, 3, :], v[:, 3, :], ALU.mult))

            def spread(i, r):
                n = 4 * i + r
                v = sm[:, r % 4]
                dve.wait_ge(sq_ready, n + 1)
                c_.link(nc.vector.tensor_reduce(v[:, 5, :], num[r % 2][:, :, 0:DH], AX.X, ALU.add))
                c_.link(nc.vector.scalar_tensor_tensor(out=v[:, 5, :], in0=v[:, 5, :], scalar=1.0 / DH, in1=v[:, 4, :],
                                                       op0=ALU.mult, op1=ALU.mult))
                nc.vector.tensor_scalar(v[:, 5, :], v[:, 5, :], CELL_EPS, None, ALU.add).then_inc(ve_ready, 1)

            def residual(i, r):
                n = 4 * i + r
                dve.wait_ge(hn_ready, n + 1)
                x = g.xres[:, bass.ds(n, 1), :].rearrange("p a d -> p (a d)")
                nc.vector.tensor_tensor(x, x, cen[r % 4][:, :, :].rearrange("p h d -> p (h d)"), ALU.add).then_inc(x_done, 1)

            nc.vector.memset(state[:, :, :, :], 0.0).then_inc(state_zero, 1)
            dve.wait_ge(state_zero, 1)

            def step(i, r, is_last):
                weigh(i, r)
                if r >= 2:
                    spread(i, r - 2)
                if r >= 1:
                    gather(i, r - 1)
                carry(i, r)
                if r >= 1:
                    centre(i, r - 1)
                if r >= 3:
                    residual(i, r - 3)

            def drain(i, r):
                spread(i, r - 1)
                gather(i, r)
                centre(i, r)
                residual(i, r - 2)
                spread(i, r)
                residual(i, r - 1)
                residual(i, r)
            run(dve, c_, 4 * 10, step, drain)

        @block.gpsimd
        def _(pool):
            c_ = Chain(pool, pch)
            nc.gpsimd.memset(aml[:, :, :], 1.0)
            nc.gpsimd.memset(amr[:, :, :], 1.0)
            for k in range(2):
                last = nc.gpsimd.memset(vaug[k][:, :, :, DH:DH + 1], 1.0)
            last.then_inc(ones_set, 1)

            def keys(i, r):
                n, b = 4 * i + r, 2 * i + r // 2
                pool.wait_ge(ctx_in, 32 * i + 16 * (r // 2 + 1))
                if r >= 2:
                    pool.wait_ge(si_done, n - 1)
                kw = g.tmE[:, 0, bass.ds(b * NH, NH)].rearrange("p (h o) -> p h o", o=1).broadcast_to([P, NH, DH])
                nc.gpsimd.tensor_tensor(kkw[:, :, :], ctxs[:, 0, :].rearrange("p (h d) -> p h d", d=DH), kw,
                                        ALU.mult).then_inc(kk_ready, 1)

            def normalise(i, r):
                n = 4 * i + r
                q = r % 4
                v = sm[:, q]
                pool.wait_ge(ve_ready, n + 1)
                c_.link(nc.gpsimd.tensor_tensor(v[:, 6, :], v[:, 5, :], g.neghalf[:, 0:NH], ALU.pow))
                c_.link(nc.gpsimd.tensor_tensor(v[:, 7, :], v[:, 6, :], v[:, 3, :], ALU.mult))
                c_.link(nc.gpsimd.tensor_tensor(cen[q][:, :, :], cen[q][:, :, :],
                                                v[:, 7, :].rearrange("p (h o) -> p h o", o=1).broadcast_to([P, NH, DH]),
                                                ALU.mult))
                flat = cen[q][:, :, :].rearrange("p h d -> p (h d)")
                nc.gpsimd.tensor_tensor(flat, flat, g.coef[:, :], ALU.mult).then_inc(hn_ready, 1)

            keys(0, 0)

            def step(i, r, is_last):
                if r >= 2:
                    normalise(i, r - 2)
                if r % 2 == 1 and not is_last:
                    keys(i, r + 1)

            def drain(i, r):
                normalise(i, r - 1)
                normalise(i, r)
            run(pool, c_, 4 * 4 - 4, step, drain)


def routing_stage(nc, g, d):
    with ExitStack() as ctx:
        a = Pools(nc, ctx)
        ab, e, lu, mask, sp, score, sel, tmp, pos = [a.sb("rt_" + n, [P, NT, E]) for n in
                                                     ("ab", "e", "lu", "mask", "sp", "score", "sel", "tmp", "pos")]
        oh = a.sb("rt_oh", [P, 2, NT, E])
        chosen = a.sb("rt_chosen", [P, NT, E], BF16)
        tot, keep, upto = [a.sb("rt_" + n, [P, E, NT]) for n in ("tot", "keep", "upto")]
        top = a.sb("rt_top", [P, NT, 8])
        topi = a.sb("rt_topi", [P, NT, 8], U32)
        idx, gk, pk, ok, slot = [a.sb("rt_" + n, [P, 2, NT]) for n in ("idx", "gk", "pk", "ok", "slot")]
        den = a.sb("rt_den", [P, NT])
        ps_before = a.ps("rt_before", [P, NT, E])
        ps_total = a.ps("rt_total", [P, NT, E])
        chain, abs_ready, e_ready, sp_ready, score_ready, chosen_ready, counted = map(
            a.sem, ["rt_" + n for n in ("chain", "abs", "e_ready", "sp_ready", "score_ready", "chosen_ready", "counted")])
        block = ctx.enter_context(nc.Block())

        @block.vector
        def _(dve):
            c = Chain(dve, chain)
            l = g.logits[:, :, :]
            nc.vector.scalar_tensor_tensor(out=ab[:, :, :], in0=l, scalar=-1.0, in1=l, op0=ALU.mult,
                                           op1=ALU.max).then_inc(abs_ready, 1)
            dve.wait_ge(e_ready, 2)
            log1p_exp(nc, c, e[:, :, :], lu[:, :, :], ab[:, :, :], mask[:, :, :])
            nc.vector.scalar_tensor_tensor(out=sp[:, :, :], in0=l, scalar=0.0, in1=lu[:, :, :], op0=ALU.max,
                                           op1=ALU.add).then_inc(sp_ready, 1)
            dve.wait_ge(score_ready, 1)
            bias = g.gate_b[:, :].rearrange("p (o e) -> p o e", o=1).broadcast_to([P, NT, E])
            c.link(nc.vector.tensor_tensor(sel[:, :, :], score[:, :, :], bias, ALU.add))
            for t in range(NT):
                last = nc.vector.max(top[:, t, :], sel[:, t, :])
            c.link(last)
            for t in range(NT):
                last = nc.vector.max_index(topi[:, t, :], top[:, t, :], sel[:, t, :])
            c.link(last)
            ids = g.eiota[:, :].rearrange("p (o e) -> p o e", o=1).broadcast_to([P, NT, E])
            for k in range(2):
                c.link(nc.vector.tensor_copy(idx[:, k, :], topi[:, :, k]))
                mine = idx[:, k, :].rearrange("p (t o) -> p t o", o=1).broadcast_to([P, NT, E])
                c.link(nc.vector.tensor_tensor(oh[:, k, :, :], ids, mine, ALU.is_equal))
            nc.vector.tensor_tensor(chosen[:, :, :], oh[:, 0, :, :], oh[:, 1, :, :], ALU.add).then_inc(chosen_ready, 1)
            for k in range(2):
                c.link(nc.vector.tensor_tensor(tmp[:, :, :], score[:, :, :], oh[:, k, :, :], ALU.mult))
                c.link(nc.vector.tensor_reduce(gk[:, k, :], tmp[:, :, :], AX.X, ALU.add))
            c.link(nc.vector.tensor_tensor(den[:, :], gk[:, 0, :], gk[:, 1, :], ALU.add))
            c.link(nc.vector.reciprocal(den[:, :], den[:, :]))
            c.link(nc.vector.tensor_tensor(gk[:, :, :], gk[:, :, :],
                                           den[:, :].rearrange("p (o t) -> p o t", o=1).broadcast_to([P, 2, NT]), ALU.mult))
            c.link(nc.vector.memset(keep[:, :, :], 1.0))
            c.link(nc.vector.memset(keep[:, :, 0:1], 0.0))
            dve.wait_ge(counted, 1)
            c.link(nc.vector.tensor_copy(tot[:, :, :], ps_total[:, :, :].rearrange("p t e -> p e t")))
            flat = lambda x: x[:, :, :].rearrange("p e t -> p (e t)")
            c.link(nc.vector.tensor_tensor_scan(flat(upto), flat(keep), flat(tot), 0.0, ALU.mult, ALU.add))
            c.link(nc.vector.tensor_tensor(upto[:, :, :], upto[:, :, :], tot[:, :, :], ALU.subtract))
            c.link(nc.vector.tensor_tensor(pos[:, :, :], upto[:, :, :].rearrange("p e t -> p t e"), ps_before[:, :, :], ALU.add))
            for k in range(2):
                c.link(nc.vector.tensor_tensor(tmp[:, :, :], pos[:, :, :], oh[:, k, :, :], ALU.mult))
                c.link(nc.vector.tensor_reduce(pk[:, k, :], tmp[:, :, :], AX.X, ALU.add))
            c.link(nc.vector.tensor_scalar(ok[:, :, :], pk[:, :, :], float(CAP), None, ALU.is_lt))
            c.link(nc.vector.scalar_tensor_tensor(out=g.weight[:, :, :], in0=gk[:, :, :], scalar=g.tanh[:, 1:2],
                                                  in1=ok[:, :, :], op0=ALU.mult, op1=ALU.mult))
            c.link(nc.vector.scalar_tensor_tensor(out=slot[:, :, :], in0=idx[:, :, :], scalar=float(CAP), in1=pk[:, :, :],
                                                  op0=ALU.mult, op1=ALU.add))
            c.link(nc.vector.tensor_scalar(ok[:, :, :], ok[:, :, :], -NOWHERE, NOWHERE, ALU.mult, ALU.add))
            c.link(nc.vector.tensor_tensor(slot[:, :, :], slot[:, :, :], ok[:, :, :], ALU.add))
            c.link(nc.vector.tensor_copy(g.slot[:, :, :], slot[:, :, :]))

        @block.scalar
        def _(act):
            act.wait_ge(abs_ready, 1)
            nc.scalar.activation(e[:, :, :], ab[:, :, :], ACT.Exp, scale=-1.0).then_inc(e_ready, 1)
            act.wait_ge(e_ready, 1)
            nc.scalar.activation(lu[:, :, :], e[:, :, :], ACT.Ln, bias=1.0).then_inc(e_ready, 1)
            act.wait_ge(sp_ready, 1)
            nc.scalar.activation(score[:, :, :], sp[:, :, :], ACT.Sqrt).then_inc(score_ready, 1)

        @block.tensor
        def _(pe):
            pe.wait_ge(chosen_ready, 1)
            ch = chosen[:, :, :].rearrange("p t e -> p (t e)")
            nc.tensor.matmul(ps_before[:, :, :].rearrange("p t e -> p (t e)"), g.before[:, :], ch, start=True, stop=True)
            nc.tensor.matmul(ps_total[:, :, :].rearrange("p t e -> p (t e)"), g.onesb[:, :], ch, start=True,
                             stop=True).then_inc(counted, 1)


def ffn_stage(nc, g, d, kind):
    shared, sending, collecting = kind != "experts", kind == "send", kind == "collect"
    COUNT = HB if shared else E
    FIRST = HB if collecting else 0
    tag = kind[0]
    WS = 1 if shared else 2
    rows = [P] * (FC - 1) + [FLAST]
    with ExitStack() as ctx:
        a = Pools(nc, ctx)
        raw13 = a.sb(tag + "raw13", [P, DC, 2 * FI])
        raw2 = a.sb(tag + "raw2", [P, FC, D])
        w13 = [[a.sb(f"{tag}w13{p}{k}", [P, DC, 2 * FI], F32R) for p in "hl"] for k in range(WS)]
        w2 = [[a.sb(f"{tag}w2{p}{k}", [P, FC, D], F32R) for p in "hl"] for k in range(WS)]
        xrows = [a.sb(f"{tag}xrows{k}", [P, 2, D]) for k in range(2)]
        xs = [[a.sb(f"{tag}x{p}{k}", [P, DC, S], F32R) for p in "hl"] for k in range(2)]
        hh = a.sb(tag + "hh", [P, FC, S])
        hs = [[a.sb(f"{tag}h{p}{k}", [P, FC, S], F32R) for p in "hl"] for k in range(2)]
        sg = a.sb(tag + "sg", [P, FC, S])
        ystage = None if shared else [a.sb(f"{tag}ystage{k}", [P, 2, D]) for k in range(2)]
        psT = a.ps(tag + "psT", [P, DC, S])
        psH = [a.ps(f"{tag}psH{m}", [P, 2, S]) for m in range(FC)]
        psY = [a.ps(f"{tag}psY{j}", [P, D]) for j in range(2)]
        names = ["turned", "h_done", "y_done", "xh_ready", "xl_ready", "sg_ready", "hh_done", "hh_high", "hl_ready",
                 "wh13", "wh2", "wl13", "wl2"] + (["x_rows", "y_taken"] if shared else ["y_staged"])
        names += ["sent_ready", "hold"] if sending else []
        names += ["idx_ready", "hold", "chain", "blank", "done"] if collecting else []
        s = {n: a.sem(f"{tag}_{n}") for n in names}
        piece = [a.sem(f"{tag}_w_in{k}") for k in range(DC + 2)]
        x_in = None if shared else [a.sem(f"{tag}_x_in{k}") for k in range(2)]
        y_out = None if shared else [a.sem(f"{tag}_y_out{k}") for k in range(2)]
        if sending:
            sent = [a.sb(f"{tag}sent{k}", [P, D]) for k in range(4)]
            sidx = a.sb(tag + "sidx", [P, 4, 2], U32)
            sent_out = [a.sem(f"{tag}_sent_out{k}") for k in range(4)]
        if collecting:
            got = [a.sb(f"{tag}got{k}", [P, 2, 2, D]) for k in range(2)]
            gidx = [a.sb(f"{tag}gidx{k}", [P, 2, 2], U32) for k in range(2)]
            got_in = [a.sem(f"{tag}_got_in{k}") for k in range(2)]
            out_done = [a.sem(f"{tag}_out_done{k}") for k in range(2)]
        block = ctx.enter_context(nc.Block())
        R0, LOOPS = 3, (COUNT - 4) // 2

        def run(eng, step, drain, chain=None, per=0):
            for r in range(R0):
                step(0, r, False)
            with eng.Fori(0, LOOPS) as i:
                if chain:
                    chain.enter(i, per)
                for r in range(R0, R0 + 2):
                    step(i, r, False)
                if chain:
                    chain.leave(LOOPS)
            step(LOOPS, R0, True)
            drain(LOOPS, R0 + 1)

        @block.sync
        def _(sp):
            src13 = lambda q, c: (d.ws13T[c * P:(c + 1) * P, :] if shared else
                                  d.w13T[bass.ds(q, 1), c * P:(c + 1) * P, :].rearrange("e p n -> p (e n)"))
            full = (FC - 1) * P

            def load13(q, wait):
                for c in range(DC):
                    if wait:
                        sp.wait_ge(s["wh13"], DC * q - DC + c + 1)
                        sp.wait_ge(s["wl13"], DC * q - DC + c + 1)
                    sp.dma_start(raw13[:, c, :], src13(q, c)).then_inc(piece[c], 16)

            def load2(q, wait):
                if shared:
                    two, one = d.ws2T[0:full, :].rearrange("(k p) n -> p k n", p=P), d.ws2T[full:FI, :]
                else:
                    two = d.w2T[bass.ds(q, 1), 0:full, :].rearrange("e (k p) n -> p (e k) n", p=P)
                    one = d.w2T[bass.ds(q, 1), full:FI, :].rearrange("e p n -> p (e n)")
                if wait:
                    sp.wait_ge(s["wh2"], 2 * q)
                    sp.wait_ge(s["wl2"], 2 * q)
                sp.dma_start(raw2[:, 0:FC - 1, :], two).then_inc(piece[DC], 16)
                sp.dma_start(raw2[0:FLAST, FC - 1, :], one).then_inc(piece[DC + 1], 16)

            def load_rows(q, r, wait):
                if wait:
                    sp.wait_ge(s["turned"], q - 1)
                sp.dma_start(xrows[r % 2][:, :, :], d.disp[bass.ds(q * CAP, CAP), :].rearrange(
                    "(j p) n -> p j n", p=P)).then_inc(x_in[r % 2], 16)

            def store(q, r):
                sp.wait_ge(s["y_staged"], 2 * q + 2)
                sp.dma_start(d.yexp[bass.ds(q * CAP, CAP), :].rearrange("(j p) n -> p j n", p=P),
                             ystage[r % 2][:, :, :]).then_inc(y_out[r % 2], 16)

            if shared:
                load13(0, False)
                load2(0, False)
                if collecting:
                    def leave(b, k, n):
                        sp.wait_ge(s["done"], n)
                        sp.dma_start(d.out[bass.ds(b, 1)].rearrange("a (j p) n -> p (a j) n", p=P),
                                     g.xres[:, bass.ds(2 * b, 2), :]).then_inc(out_done[k], 16)

                    def step(i, r, is_last):
                        q = 2 * i + r
                        if r >= 1:
                            leave(q + (FIRST - 1), 1, 2 * q)
                        leave(q, 0, 2 * q + 1)

                    def drain(i, r):
                        leave(2 * i + r + (FIRST - 1), 1, 2 * (2 * i + r))
                        for k in range(2):
                            sp.wait_ge(out_done[k], 16 * COUNT)
                    run(sp, step, drain)
            else:
                load13(0, False)
                load_rows(0, 0, False)
                load2(0, False)
                load_rows(1, 1, False)
                load13(1, True)

                def ahead(q, r, results):
                    load_rows(q + 2, r, True)
                    load13(q + 2, True)
                    load2(q + 1, True)
                    if results:
                        store(q - 1, r - 1)
                ahead(0, 0, False)
                ahead(1, 1, True)
                with sp.Fori(0, (COUNT - 4) // 2) as i:
                    for r in range(2, 4):
                        ahead(2 * i + r, r, True)
                load2(COUNT - 1, True)
                store(COUNT - 3, COUNT - 3)
                store(COUNT - 2, COUNT - 2)
                store(COUNT - 1, COUNT - 1)
                for k in range(2):
                    sp.wait_ge(y_out[k], 8 * COUNT)

        @block.tensor
        def _(pe):
            def turn(i, r):
                q = 2 * i + r
                if shared:
                    pe.wait_ge(s["x_rows"], q + 1)
                else:
                    pe.wait_ge(x_in[r % 2], 16 * i + 16 * (r // 2 + 1))
                if r >= 1:
                    pe.wait_ge(s["xl_ready"], q)
                for c in range(DC):
                    for j in range(2):
                        last = nc.tensor.transpose(psT[:, c, j * P:(j + 1) * P], xrows[r % 2][:, j, c * P:(c + 1) * P],
                                                   g.ident[:, :])
                last.then_inc(s["turned"], 1)

            def hidden(i, r, m):
                q, n = 2 * i + r, rows[m]
                w, x = w13[r % WS], xs[r % 2]
                if m == 0:
                    pe.wait_ge(s["xl_ready"], q + 1)
                    if shared:
                        pe.wait_ge(s["wl13"], DC)
                        pe.wait_ge(s["wh13"], DC)
                    else:
                        pe.wait_ge(s["wl13"], DC * q + DC)
                        pe.wait_ge(s["wh13"], DC * q + DC)
                if r >= 1:
                    pe.wait_ge(s["hh_done"], 3 * q - 2 + m)
                for v in range(2):
                    for c in range(DC):
                        col = v * FI + m * P
                        for p, (wp, xp) in enumerate(((0, 0), (0, 1), (1, 0))):
                            last = nc.tensor.matmul(psH[m][0:n, v, :], w[wp][:, c, col:col + n], x[xp][:, c, :],
                                                    start=(c == 0 and p == 0), stop=(c == DC - 1 and p == 2))
                last.then_inc(s["h_done"], 1)

            def back(i, r):
                q = 2 * i + r
                w, h = w2[r % WS], hs[r % 2]
                pe.wait_ge(s["hl_ready"], 3 * q + 3)
                if shared:
                    pe.wait_ge(s["wl2"], 2)
                    pe.wait_ge(s["wh2"], 2)
                else:
                    pe.wait_ge(s["wl2"], 2 * q + 2)
                    pe.wait_ge(s["wh2"], 2 * q + 2)
                for j in range(2):
                    if r >= 1:
                        pe.wait_ge(s["y_taken" if shared else "y_staged"], 2 * q - 1 + j)
                    for k in range(FC):
                        n = rows[k]
                        for p, (hp, wp) in enumerate(((0, 0), (0, 1), (1, 0))):
                            last = nc.tensor.matmul(psY[j][:, :], h[hp][0:n, k, j * P:(j + 1) * P], w[wp][0:n, k, :],
                                                    start=(k == 0 and p == 0), stop=(k == FC - 1 and p == 2))
                    last.then_inc(s["y_done"], 1)
            turn(0, 0)

            def step(i, r, is_last):
                hidden(i, r, 0)
                hidden(i, r, 1)
                if not is_last:
                    turn(i, r + 1)
                hidden(i, r, 2)
                if r >= 1:
                    back(i, r - 1)
            run(pe, step, lambda i, r: back(i, r - 1))

        @block.scalar
        def _(act):
            def split_x(i, r):
                q = 2 * i + r
                act.wait_ge(s["turned"], q + 1)
                nc.scalar.activation(xs[r % 2][0][:, :, :], psT[:, :, :], ACT.Copy).then_inc(s["xh_ready"], 1)

            def split13(i, r):
                for c in range(DC):
                    act.wait_ge(piece[c], 16 if shared else 32 * i + 16 * (r + 1))
                    nc.scalar.activation(w13[r % WS][0][:, c, :], raw13[:, c, :], ACT.Copy).then_inc(s["wh13"], 1)

            def split2(i, r):
                act.wait_ge(piece[DC], 16 if shared else 32 * i + 16 * (r + 1))
                nc.scalar.activation(w2[r % WS][0][:, 0:FC - 1, :], raw2[:, 0:FC - 1, :], ACT.Copy).then_inc(s["wh2"], 1)
                act.wait_ge(piece[DC + 1], 16 if shared else 32 * i + 16 * (r + 1))
                nc.scalar.activation(w2[r % WS][0][0:FLAST, FC - 1, :], raw2[0:FLAST, FC - 1, :], ACT.Copy).then_inc(s["wh2"], 1)

            def silu(i, r, m):
                q, n = 2 * i + r, rows[m]
                act.wait_ge(s["h_done"], 3 * q + m + 1)
                if r >= 1:
                    act.wait_ge(s["hh_done"], 3 * q - 2 + m)
                nc.scalar.activation(sg[0:n, m, :], psH[m][0:n, 0, :], ACT.Silu).then_inc(s["sg_ready"], 1)

            def high(i, r, m):
                q, n = 2 * i + r, rows[m]
                act.wait_ge(s["hh_done"], 3 * q + m + 1)
                nc.scalar.activation(hs[r % 2][0][0:n, m, :], hh[0:n, m, :], ACT.Copy).then_inc(s["hh_high"], 1)

            def stage(i, r):
                q = 2 * i + r
                if r >= 2:
                    act.wait_ge(y_out[r % 2], 16 * i + 16 * (r // 2))
                for j in range(2):
                    act.wait_ge(s["y_done"], 2 * q + j + 1)
                    nc.scalar.activation(ystage[r % 2][:, j, :], psY[j][:, :], ACT.Copy).then_inc(s["y_staged"], 1)

            split13(0, 0)
            split_x(0, 0)

            def step(i, r, is_last):
                silu(i, r, 0)
                silu(i, r, 1)
                high(i, r, 0)
                if not is_last:
                    split_x(i, r + 1)
                if not shared and not is_last:
                    split13(i, r + 1)
                silu(i, r, 2)
                high(i, r, 1)
                high(i, r, 2)
                if not shared or r == 0 and not is_last:
                    split2(i, r)
                if not shared and r >= 1:
                    stage(i, r - 1)
            run(act, step, lambda i, r: None if shared else stage(i, r - 1))

        @block.vector
        def _(dve):
            ch = Chain(dve, s["chain"]) if collecting else None
            row = lambda t: g.xres[:, bass.ds(t, 1), :].rearrange("p a n -> p (a n)")

            def normed(out, t):
                return nc.vector.tensor_scalar(out, row(t), g.mu_all[:, bass.ds(t, 1)], g.rs_all[:, bass.ds(t, 1)],
                                               ALU.subtract, ALU.mult)

            def fetch(i, r):
                q = 2 * i + r
                if r >= 2:
                    dve.wait_ge(s["turned"], q - 1)
                for j in range(2):
                    last = normed(xrows[r % 2][:, j, :], 2 * q + (2 * FIRST + j))
                last.then_inc(s["x_rows"], 1)

            def split_x(i, r):
                q = 2 * i + r
                dve.wait_ge(s["xh_ready"], q + 1)
                nc.vector.tensor_tensor(xs[r % 2][1][:, :, :], psT[:, :, :], xs[r % 2][0][:, :, :].bitcast(F32),
                                        ALU.subtract).then_inc(s["xl_ready"], 1)

            def split13(i, r, c):
                q = 2 * i + r
                dve.wait_ge(s["wh13"], DC * q + c + 1)
                nc.vector.tensor_tensor(w13[r % WS][1][:, c, :], raw13[:, c, :], w13[r % WS][0][:, c, :].bitcast(F32),
                                        ALU.subtract).then_inc(s["wl13"], 1)

            def split2(i, r):
                q = 2 * i + r
                h, l = w2[r % WS]
                dve.wait_ge(s["wh2"], 2 * q + 1)
                nc.vector.tensor_tensor(l[:, 0:FC - 1, :], raw2[:, 0:FC - 1, :], h[:, 0:FC - 1, :].bitcast(F32),
                                        ALU.subtract).then_inc(s["wl2"], 1)
                dve.wait_ge(s["wh2"], 2 * q + 2)
                nc.vector.tensor_tensor(l[0:FLAST, FC - 1, :], raw2[0:FLAST, FC - 1, :], h[0:FLAST, FC - 1, :].bitcast(F32),
                                        ALU.subtract).then_inc(s["wl2"], 1)

            def gated(i, r, m):
                q, n = 2 * i + r, rows[m]
                dve.wait_ge(s["sg_ready"], 3 * q + m + 1)
                if r >= 1:
                    dve.wait_ge(s["hl_ready"], 3 * q - 2 + m)
                nc.vector.tensor_tensor(hh[0:n, m, :], sg[0:n, m, :], psH[m][0:n, 1, :], ALU.mult).then_inc(s["hh_done"], 1)

            def add(i, r):
                q = 2 * i + r
                for j in range(2):
                    dve.wait_ge(s["y_done"], 2 * q + j + 1)
                    x = row(2 * q + (2 * FIRST + j))
                    nc.vector.scalar_tensor_tensor(out=x, in0=psY[j][:, :], scalar=g.tanh[:, 1:2], in1=x, op0=ALU.mult,
                                                   op1=ALU.add).then_inc(s["y_taken"], 1)

            def send(i, r):
                q = 2 * i + r
                for k in range(4):
                    if r >= 1:
                        dve.wait_ge(sent_out[k], 32 * q)
                    normed(sent[k][:, :], 4 * q + k)
                    nc.vector.tensor_copy(sidx[:, k, :], g.slot[:, :, bass.ds(4 * q + k, 1)].rearrange(
                        "p k o -> p (k o)")).then_inc(s["sent_ready"], 1)

            def index(b, k):
                nc.vector.tensor_copy(gidx[k][:, :, :], g.slot[:, :, bass.ds(2 * b, 2)]).then_inc(s["idx_ready"], 1)

            def collect(b, k, n):
                dve.wait_ge(got_in[k], 64 * n)
                for e in range(2):
                    for j in range(2):
                        x = row(2 * b + j)
                        last = nc.vector.scalar_tensor_tensor(out=x, in0=got[k][:, e, j, :],
                                                              scalar=g.weight[:, e, bass.ds(2 * b + j, 1)], in1=x,
                                                              op0=ALU.mult, op1=ALU.add)
                    if e == 0:
                        ch.link(last)
                last.then_inc(s["done"], 1)

            if collecting:
                for k in range(2):
                    last = nc.vector.memset(got[k][:, :, :, :], 0.0)
                last.then_inc(s["blank"], 1)
                index(0, 0)
                index(FIRST, 1)
            if shared:
                fetch(0, 0)
            for c in range(DC):
                split13(0, 0, c)
            split_x(0, 0)

            def step(i, r, is_last):
                q = 2 * i + r
                if shared and not is_last:
                    fetch(i, r + 1)
                if sending:
                    send(i, r)
                gated(i, r, 0)
                gated(i, r, 1)
                if not is_last:
                    split_x(i, r + 1)
                if not shared and not is_last:
                    for c in range(DC):
                        split13(i, r + 1, c)
                gated(i, r, 2)
                if not shared or r == 0 and not is_last:
                    split2(i, r)
                if shared and r >= 1:
                    add(i, r - 1)
                if collecting:
                    if r >= 1:
                        dve.wait_ge(s["y_taken"], 2 * q)
                        collect(q + (FIRST - 1), 1, q)
                        index(q + FIRST, 1)
                    collect(q, 0, q + 1)
                    if not is_last:
                        index(q + 1, 0)

            def drain(i, r):
                q = 2 * i + r
                if shared:
                    add(i, r - 1)
                if collecting:
                    dve.wait_ge(s["y_taken"], 2 * q)
                    collect(q + (FIRST - 1), 1, q)
            run(dve, step, drain, ch if collecting else None, 2 * 2)

        @block.gpsimd
        def _(pool):
            last_row = pool.to_reg(E * CAP - 1) if shared else None
            hold = Chain(pool, s["hold"]) if shared else None

            def held():
                if not (isinstance(hold.base, int) and hold.base + hold.n == 0):
                    pool.wait_ge(s["hold"], hold.base + hold.n)
                hold.n += 1
                nc.gpsimd.tensor_tensor(g.idle[:, 1:2], g.neghalf[:, 0:1], g.neghalf[:, 1:2], ALU.mult).then_inc(s["hold"], 1)

            def rest(i, r, m):
                q, n = 2 * i + r, rows[m]
                pool.wait_ge(s["hh_high"], 3 * q + m + 1)
                nc.gpsimd.tensor_tensor(hs[r % 2][1][0:n, m, :], hh[0:n, m, :], hs[r % 2][0][0:n, m, :].bitcast(F32),
                                        ALU.subtract).then_inc(s["hl_ready"], 1)

            def scatter(i, r, k):
                q = 2 * i + r
                pool.wait_ge(s["sent_ready"], 4 * q + k + 1)
                held()
                for e in range(2):
                    nc.gpsimd.indirect_dma_start(
                        out=d.disp[:, :], out_offset=bass.IndirectOffsetOnAxis(ap=sidx[:, k, e:e + 1], axis=0),
                        in_=sent[k][:, :], in_offset=None, bounds_check=last_row, oob_is_err=False).then_inc(sent_out[k], 16)

            def gather(k, n):
                pool.wait_ge(s["idx_ready"], n)
                held()
                for e in range(2):
                    for j in range(2):
                        nc.gpsimd.indirect_dma_start(
                            out=got[k][:, e, j, :], out_offset=None, in_=d.yexp[:, :],
                            in_offset=bass.IndirectOffsetOnAxis(ap=gidx[k][:, e, j:j + 1], axis=0),
                            bounds_check=last_row, oob_is_err=False).then_inc(got_in[k], 16)

            def step(i, r, is_last):
                q = 2 * i + r
                for m in range(FC):
                    rest(i, r, m)
                    if sending:
                        scatter(i, r, m)
                        if m == 2:
                            scatter(i, r, 3)
                if collecting:
                    if r >= 1:
                        gather(1, 2 * q + 2)
                    if not is_last:
                        gather(0, 2 * q + 3)

            if collecting:
                gather(0, 1)
                gather(1, 2)

            def drain(i, r):
                if sending:
                    for k in range(4):
                        pool.wait_ge(sent_out[k], 32 * COUNT)
            run(pool, step, drain, hold, 8 if sending else 4 if collecting else 0)


def build(nc, d):
    with ExitStack() as ctx:
        a = Pools(nc, ctx)

        class g:
            xres = a.sb("xres", [P, NT, D])
            ident = a.sb("ident", [P, P])
            identb = a.sb("identb", [P, P], BF16)
            causal = a.sb("causal", [P, 4, P], BF16)
            before = a.sb("before", [P, P], BF16)
            onesb = a.sb("onesb", [P, P], BF16)
            neghalf = a.sb("neghalf", [P, NH])
            eiota = a.sb("eiota", [P, E])
            wr = a.sb("wr", [P, DC, E])
            bias = a.sb("bias", [P, 2 * NH])
            coef = a.sb("coef", [P, D])
            gate_b = a.sb("gate_b_rows", [P, E])
            tanh = a.sb("tanh", [P, 2])
            mu_all = a.sb("mu_all", [P, NT])
            rs_all = a.sb("rs_all", [P, NT])
            idle = a.sb("idle", [P, 2])
            rs_stage = a.sb("rs_stage", [P, 2, 4])

        with ExitStack() as cell:
            c = Pools(nc, cell)
            g.qT_all = c.sb("qT_all", [P, B * DC, S])
            g.tmE = c.sb("tmE", [P, 4, B * NH])
            with ExitStack() as gates:
                t = Pools(nc, gates)
                g.gates = t.sb("gates", [P, 2, 2, B * NH])
                g.wg = t.sb("wg", [P, DC, 2 * NH])
                g.wc = t.sb("wc", [P, DC, 2 * NH])
                setup_stage(nc, g, d)
                norm_project_stage(nc, g, d, True)
                gate_stage(nc, g, d)
            attention_stage(nc, g, d)
        g.weight = a.sb("weight", [P, 2, NT])
        g.slot = a.sb("slot", [P, 2, NT], U32)
        with ExitStack() as router:
            g.logits = Pools(nc, router).sb("logits", [P, NT, E])
            norm_project_stage(nc, g, d, False)
            routing_stage(nc, g, d)
        for kind in ("send", "experts", "collect"):
            ffn_stage(nc, g, d, kind)


def kernel(**inputs):
    import numpy as _np
    import concourse.bacc as _bacc
    from concourse import mybir as _mybir
    from concourse.bass_utils import run_bass_kernel_spmd as _run

    nc = _bacc.Bacc("TRN2", target_bir_lowering=False, num_devices=1)
    v = {k: _np.asarray(x) for k, x in inputs.items()}
    cat = lambda *xs: _np.concatenate(xs, axis=-1)
    w1, w3, w2 = v["L0_ffn_W1"], v["L0_ffn_W3"], v["L0_ffn_W2"]
    arrays = {
        "x": v["x"], "ctx": v["ctx_2048"], "ctxT": v["ctx_2048"].transpose(0, 2, 1),
        "g_xattn": v["g_xattn"].reshape(1, 1), "g_ffn": v["g_ffn"].reshape(1, 1),
        "wgate": cat(v["L0_xattn_Wi"], v["L0_xattn_Wf"]).reshape(3, D, 2 * NH),
        "gbias": cat(v["L0_xattn_bi"], v["L0_xattn_bf"]).reshape(1, 2 * NH),
        "ln_scale": v["L0_xattn_ln_scale"].reshape(1, D),
        "gate_wT": v["L0_ffn_gate_w"].T, "gate_b": v["L0_ffn_gate_b"].reshape(1, E),
        "w13T": cat(w1.transpose(0, 2, 1), w3.transpose(0, 2, 1)), "w2T": w2.transpose(0, 2, 1),
        "ws13T": cat(v["L0_ffn_Ws1"].T, v["L0_ffn_Ws3"].T), "ws2T": v["L0_ffn_Ws2"].T,
    }
    arrays = {k: _np.ascontiguousarray(a) for k, a in arrays.items()}

    ins = {name: nc.dram_tensor(name, a.shape, _mybir.dt.from_np(a.dtype), kind="ExternalInput").ap()
           for name, a in arrays.items()}
    program(nc, ins)
    r = _run(nc, [arrays], core_ids=[0])
    return r.results[0]["out"]


class Dram:

    def __init__(self, ins, out, am, disp, yexp):
        self.x, self.ctx, self.ctxT = ins["x"], ins["ctx"], ins["ctxT"]
        self.g_xattn, self.g_ffn, self.wgate, self.gbias = ins["g_xattn"], ins["g_ffn"], ins["wgate"], ins["gbias"]
        self.ln_scale, self.gate_wT, self.gate_b = ins["ln_scale"], ins["gate_wT"], ins["gate_b"]
        self.w13T, self.w2T, self.ws13T, self.ws2T = ins["w13T"], ins["w2T"], ins["ws13T"], ins["ws2T"]
        self.out, self.am, self.disp, self.yexp = out, am, disp, yexp


def program(nc, ins):
    out = nc.dram_tensor("out", (B, S, D), F32, kind="ExternalOutput").ap()
    am = nc.dram_tensor("am", (2, 3, B, NH, S), BF16, kind="Internal").ap()
    disp = nc.dram_tensor("disp", (E * CAP, D), F32, kind="Internal").ap()
    yexp = nc.dram_tensor("yexp", (E * CAP, D), F32, kind="Internal").ap()
    build(nc, Dram(ins, out, am, disp, yexp))
```

```python
from contextlib import ExitStack

import numpy as np

import concourse.bass as bass
from concourse import mybir

F32 = mybir.dt.float32
F32R = mybir.dt.float32r
BF16 = mybir.dt.bfloat16
U32 = mybir.dt.uint32
ACT = mybir.ActivationFunctionType
ALU = mybir.AluOpType
AX = mybir.AxisListType

P = 128
B, S, D = 16, 256, 512
NH, DH = 16, 32
NT = B * S // P
DC = D // P
E, FI, CAP = 16, 352, 256
FC = -(-FI // P)
FLAST = FI - (FC - 1) * P
HB = B // 2
LN_EPS, CELL_EPS = 1e-5, 1e-6
SCALE = float(DH) ** -0.5
MASKED = -1e30
SMALL_E = 0.01
NOWHERE = 1.0e6


class Chain:

    def __init__(self, eng, sem):
        self.eng, self.sem, self.n, self.base = eng, sem, 0, 0

    def link(self, ins):
        self.n += 1
        ins.then_inc(self.sem, 1)
        self.eng.wait_ge(self.sem, self.base + self.n)

    def enter(self, i, per):
        self.static = self.n + self.base
        self.base, self.n, self.per = i * per + self.static, 0, per

    def leave(self, rounds):
        assert self.n == self.per, (self.n, self.per)
        self.base, self.n = 0, self.static + self.per * rounds


class Pools:

    def __init__(self, nc, ctx):
        self.nc, self.ctx = nc, ctx

    def sb(self, name, shape, dt=F32):
        return self.ctx.enter_context(self.nc.sbuf_tensor(name, shape, dt))

    def ps(self, name, shape, dt=F32):
        return self.ctx.enter_context(self.nc.psum_tensor(name, shape, dt))

    def sem(self, name):
        return self.ctx.enter_context(self.nc.semaphore(name))


def setup_stage(nc, g, d):
    with ExitStack() as ctx:
        a = Pools(nc, ctx)
        wkv = a.sb("wkv", [P, 2, DC, 2 * NH])
        gt = a.sb("gt", [P, 2])
        loaded, const, th, ch = map(a.sem, ("s0_loaded", "s0_const", "s0_tanh", "s0_chain"))
        block = ctx.enter_context(nc.Block())

        @block.sync
        def _(sp):
            loads = [
                (g.wg[:, :, :], d.wgate[0].rearrange("(c p) n -> p c n", p=P)),
                (wkv[:, 0, :, :], d.wgate[1].rearrange("(c p) n -> p c n", p=P)),
                (wkv[:, 1, :, :], d.wgate[2].rearrange("(c p) n -> p c n", p=P)),
                (g.wr[:, :, :], d.gate_wT.rearrange("(c p) n -> p c n", p=P)),
                (g.bias[:, :], d.gbias.to_broadcast([P, 2 * NH])),
                (g.coef[:, :], d.ln_scale.to_broadcast([P, D])),
                (g.gate_b[:, :], d.gate_b.to_broadcast([P, E])),
                (gt[:, 0:1], d.g_xattn.to_broadcast([P, 1])),
                (gt[:, 1:2], d.g_ffn.to_broadcast([P, 1])),
            ]
            for dst, src in loads:
                sp.dma_start(dst, src).then_inc(loaded, 16)
            sp.wait_ge(loaded, 16 * len(loads))

        @block.gpsimd
        def _(pool):
            c = Chain(pool, const)
            c.link(nc.gpsimd.memset(g.ident[:, :], 0.0))
            c.link(nc.gpsimd.affine_select(out=g.ident[:, :], in_=g.ident[:, :], compare_op=ALU.not_equal, fill=1.0,
                                           base=0, pattern=[[-1, P]], channel_multiplier=1))
            c.link(nc.gpsimd.tensor_copy(g.identb[:, :], g.ident[:, :]))
            c.link(nc.gpsimd.memset(g.causal[:, :, :], 0.0))
            c.link(nc.gpsimd.affine_select(out=g.causal[:, :, :], in_=g.causal[:, :, :], compare_op=ALU.is_ge,
                                           fill=MASKED, base=0, pattern=[[0, 4], [1, P]], channel_multiplier=-1))
            c.link(nc.gpsimd.memset(g.before[:, :], 1.0))
            c.link(nc.gpsimd.affine_select(out=g.before[:, :], in_=g.before[:, :], compare_op=ALU.is_gt,
                                           fill=0.0, base=0, pattern=[[1, P]], channel_multiplier=-1))
            c.link(nc.gpsimd.memset(g.onesb[:, :], 1.0))
            c.link(nc.gpsimd.memset(g.neghalf[:, :], -0.5))
            c.link(nc.gpsimd.iota(g.eiota[:, :], pattern=[[1, E]], base=0, channel_multiplier=0,
                                  allow_small_or_imprecise_dtypes=True))

        @block.scalar
        def _(act):
            act.wait_ge(loaded, 16 * 9)
            nc.scalar.activation(g.tanh[:, :], gt[:, :], ACT.Tanh).then_inc(th, 1)

        @block.vector
        def _(dve):
            dve.wait_ge(loaded, 16 * 9)
            nc.vector.tensor_tensor(g.wc[:, :, :], wkv[:, 0, :, :], wkv[:, 1, :, :], ALU.add)
            dve.wait_ge(th, 1)
            nc.vector.tensor_scalar(g.coef[:, :], g.coef[:, :], g.tanh[:, 0:1], None, ALU.mult).then_inc(ch, 1)


def norm_project_stage(nc, g, d, first):
    tag = "g" if first else "r"
    width = 2 * NH if first else E
    with ExitStack() as ctx:
        a = Pools(nc, ctx)
        stats = a.sb(tag + "stats", [P, 2, 4, 6])
        mv = a.sb(tag + "mv", [P, 2, 4, 2])
        var = a.sb(tag + "var", [P, 2, 4])
        xn = a.sb(tag + "xn", [P, 2, 4, D])
        xT = [a.sb(f"{tag}xT{k}", [P, DC, S]) for k in range(2)]
        cT = [a.sb(f"{tag}cT{k}", [P, 2, DC, S]) for k in range(2)] if first else None
        psT = [a.ps(f"{tag}psT{k}", [P, DC, S]) for k in range(2)]
        psG = [a.ps(f"{tag}psG{k}", [P, 2, 256]) for k in range(2)]
        x_in = [a.sem(f"{tag}_x_in{k}") for k in range(2)]
        c_in = [a.sem(f"{tag}_c_in{k}") for k in range(2)]
        chain, var_ready, rs_ready, xn_ready, turned, xt_ready, projected, kept = map(
            a.sem, [f"{tag}_{n}" for n in
                    ("chain", "var_ready", "rs_ready", "xn_ready", "turned", "xt_ready", "projected", "kept")])
        if not first:
            zeros = a.sb("zeros", [P, D])
            zeroed, tables = a.sem("r_zeroed"), a.sem("r_tables")
        block = ctx.enter_context(nc.Block())
        ROUNDS = B // 4

        if first:
            @block.sync
            def _(sp):
                with sp.Fori(0, ROUNDS) as i:
                    for s in range(2):
                        b0 = 4 * i + 2 * s
                        sp.wait_ge(projected, 4 * i + 2 * s + 2)
                        sp.dma_start(g.xres[:, bass.ds(2 * b0, 4), :],
                                     d.x[bass.ds(b0, 2)].rearrange("b (t p) d -> p (b t) d", p=P)).then_inc(x_in[s], 16)
                        sp.dma_start(cT[s][:, :, :, :],
                                     d.ctxT[bass.ds(b0, 2)].rearrange("b (c p) t -> p b c t", p=P)).then_inc(c_in[s], 16)

        if not first:
            @block.sync
            def _(sp):
                load_weights(sp, g, d, None)
                sp.wait_ge(zeroed, 1)
                for t in range(NT // 8):
                    sp.dma_start(d.disp[t * 8 * P:(t + 1) * 8 * P, :].rearrange("(p r) n -> p r n", p=P),
                                 zeros[:, :].rearrange("p (o n) -> p o n", o=1).broadcast_to([P, 8, D])).then_inc(tables, 16)
                sp.wait_ge(tables, 16 * (NT // 8))

        @block.vector
        def _(dve):
            c = Chain(dve, chain)
            if not first:
                nc.vector.memset(zeros[:, :], 0.0).then_inc(zeroed, 1)
            with dve.Fori(0, ROUNDS) as i:
                c.enter(i, 6)
                for s in range(2):
                    t0 = 8 * i + 4 * s
                    if first:
                        dve.wait_ge(x_in[s], 16 * i + 16)
                    for k in range(4):
                        last = nc.vector.bn_stats(stats[:, s, k, :], g.xres[:, bass.ds(t0 + k, 1), :].rearrange("p a d -> p (a d)"))
                    c.link(last)
                    nc.vector.memset(g.idle[:, 0:1], 0.0)
                    for k in range(4):
                        last = nc.vector.bn_aggr(mv[:, s, k, :], stats[:, s, k, :])
                    c.link(last)
                    nc.vector.tensor_copy(g.mu_all[:, bass.ds(t0, 4)], mv[:, s, :, 0])
                    c.link(nc.vector.tensor_scalar(var[:, s, :], mv[:, s, :, 1], LN_EPS, None, ALU.add))
                    nc.vector.sem_inc(var_ready, 1)
                    dve.wait_ge(rs_ready, 2 * i + s + 1)
                    nc.vector.tensor_copy(g.rs_all[:, bass.ds(t0, 4)], g.rs_stage[:, s, :])
                    dve.wait_ge(turned, 4 * i + 2 * s + 2)
                    for k in range(4):
                        last = nc.vector.tensor_scalar(xn[:, s, k, :], g.xres[:, bass.ds(t0 + k, 1), :].rearrange("p a d -> p (a d)"),
                                                       mv[:, s, k, 0:1], g.rs_stage[:, s, k:k + 1],
                                                       ALU.subtract, ALU.mult)
                    last.then_inc(xn_ready, 1)
                c.leave(ROUNDS)

        @block.gpsimd
        def _(pool):
            with pool.Fori(0, ROUNDS) as i:
                for s in range(2):
                    pool.wait_ge(var_ready, 2 * i + s + 1)
                    nc.gpsimd.tensor_tensor(g.rs_stage[:, s, :], var[:, s, :], g.neghalf[:, 0:4], ALU.pow).then_inc(rs_ready, 1)

        @block.tensor
        def _(pe):
            nc.tensor.sem_inc(turned, 4)
            nc.tensor.sem_inc(projected, 4)
            with pe.Fori(0, ROUNDS) as i:
                for s in range(2):
                    pe.wait_ge(xn_ready, 2 * i + s + 1)
                    for k in range(2):
                        n = 4 * i + 2 * s + k
                        pe.wait_ge(xt_ready, n + 1)
                        for c in range(DC):
                            for j in range(2):
                                last = nc.tensor.transpose(psT[k][:, c, j * P:(j + 1) * P],
                                                           xn[:, s, 2 * k + j, c * P:(c + 1) * P], g.ident[:, :])
                        last.then_inc(turned, 1)
                    for k in range(2):
                        n = 4 * i + 2 * s + k
                        pe.wait_ge(xt_ready, n + 3)
                        if first and k == 0:
                            pe.wait_ge(c_in[s], 16 * i + 16)
                        pe.wait_ge(kept, n + 1)
                        for j in range(2):
                            for c in range(DC):
                                last = nc.tensor.matmul(psG[k][:, j, 0:width], xT[k][:, c, j * P:(j + 1) * P],
                                                        (g.wg if first else g.wr)[:, c, :],
                                                        start=(c == 0), stop=(not first and c == DC - 1))
                            if first:
                                for c in range(DC):
                                    last = nc.tensor.matmul(psG[k][:, j, 0:width], cT[s][:, k, c, j * P:(j + 1) * P],
                                                            g.wc[:, c, :], start=False, stop=(c == DC - 1))
                        last.then_inc(projected, 1)

        @block.scalar
        def _(act):
            nc.scalar.sem_inc(xt_ready, 2)
            nc.scalar.sem_inc(kept, 2)
            with act.Fori(0, ROUNDS) as i:
                for s in range(2):
                    for k in range(2):
                        n = 4 * i + 2 * s + k
                        act.wait_ge(turned, n + 5)
                        act.wait_ge(projected, n + 3)
                        if first:
                            nc.scalar.activation(g.qT_all[:, bass.ds(n * DC, DC), :], psT[k][:, :, :], ACT.Copy)
                        nc.scalar.activation(xT[k][:, :, :], psT[k][:, :, :], ACT.Copy).then_inc(xt_ready, 1)
                    for k in range(2):
                        n = 4 * i + 2 * s + k
                        act.wait_ge(projected, n + 5)
                        for j in range(2):
                            if first:
                                out = g.gates[:, j, :, bass.ds(n * NH, NH)]
                                src = psG[k][:, j, 0:width].rearrange("p (a h) -> p a h", a=2)
                            else:
                                out = g.logits[:, bass.ds(2 * n + j, 1), :].rearrange("p a e -> p (a e)")
                                src = psG[k][:, j, 0:width]
                            last = nc.scalar.activation(out, src, ACT.Copy)
                        last.then_inc(kept, 1)


def log1p_exp(nc, c, e, log_u, poly, mask):
    c.link(nc.vector.tensor_scalar(poly, e, -0.25, 1.0 / 3.0, ALU.mult, ALU.add))
    c.link(nc.vector.scalar_tensor_tensor(out=poly, in0=poly, scalar=-1.0, in1=e, op0=ALU.mult, op1=ALU.mult))
    c.link(nc.vector.scalar_tensor_tensor(out=poly, in0=poly, scalar=0.5, in1=e, op0=ALU.add, op1=ALU.mult))
    c.link(nc.vector.scalar_tensor_tensor(out=poly, in0=poly, scalar=1.0, in1=e, op0=ALU.subtract, op1=ALU.mult))
    c.link(nc.vector.tensor_scalar(mask, e, SMALL_E, None, ALU.is_lt))
    c.link(nc.vector.scalar_tensor_tensor(out=poly, in0=poly, scalar=-1.0, in1=log_u, op0=ALU.mult, op1=ALU.subtract))
    c.link(nc.vector.tensor_tensor(poly, poly, mask, ALU.mult))
    c.link(nc.vector.tensor_tensor(log_u, log_u, poly, ALU.add))


def gate_stage(nc, g, d):
    with ExitStack() as ctx:
        a = Pools(nc, ctx)
        e = a.sb("ge", [P, 2, B * NH])
        lu = a.sb("glu", [P, 2, B * NH])
        poly = a.sb("gpoly", [P, 2, B * NH])
        mask = a.sb("gmask", [P, 2, B * NH])
        ones = a.sb("gones", [P, S])
        head = a.sb("ghead", [P, 2, 2, S])
        F = a.sb("gF", [P, 2, S])
        am = a.sb("gam", [P, 2, 2, S])
        M = a.sb("gM", [P, 2, S])
        m = a.sb("gm", [P, 2, S])
        ex = a.sb("gex", [P, 2, 4, P])
        rest = a.sb("grest", [P, 2, 2, S])
        parts = a.sb("gparts", [P, 2, 2, 3, S], BF16)
        psH = [a.ps(f"gpsH{k}", [P, 2, S]) for k in range(2)]
        psE = [a.ps(f"gpsE{k}", [P, 4, P]) for k in range(2)]
        chain, abs_ready, e_ready, lf_ready, heads, exps_go, exps, ex_turned, parts_ready, saved, pch = map(
            a.sem, ["gt_" + n for n in ("chain", "abs", "e", "lf", "heads", "exps_go", "exps", "ex_turned",
                                        "parts", "saved", "pool")])
        block = ctx.enter_context(nc.Block())

        @block.vector
        def _(dve):
            c = Chain(dve, chain)
            f = g.gates[:, :, 1, :]
            for j in range(2):
                gj = g.gates[:, j, :, :].rearrange("p a (b h) -> p a b h", h=NH)
                bias = g.bias[:, :].rearrange("p (a o h) -> p a o h", a=2, o=1).broadcast_to([P, 2, B, NH])
                last = nc.vector.tensor_tensor(gj, gj, bias, ALU.add)
            c.link(last)
            nc.vector.memset(ones[:, :], 1.0)
            nc.vector.scalar_tensor_tensor(out=poly[:, :, :], in0=f, scalar=-1.0, in1=f, op0=ALU.mult,
                                           op1=ALU.max).then_inc(abs_ready, 1)
            dve.wait_ge(e_ready, 2)
            log1p_exp(nc, c, e[:, :, :], lu[:, :, :], poly[:, :, :], mask[:, :, :])
            nc.vector.scalar_tensor_tensor(out=f, in0=f, scalar=0.0, in1=lu[:, :, :], op0=ALU.min,
                                           op1=ALU.subtract).then_inc(lf_ready, 1)
            for k in range(2):
                dve.wait_ge(heads, k + 1)
                c.link(nc.vector.tensor_copy(head[:, k, :, :], psH[k][:, :, :]))
                c.link(nc.vector.tensor_tensor_scan(F[:, k, :], ones[:, :], head[:, k, 1, :], 0.0, ALU.mult, ALU.add))
                c.link(nc.vector.tensor_tensor(am[:, k, 0, :], head[:, k, 0, :], F[:, k, :], ALU.subtract))
                c.link(nc.vector.tensor_tensor_scan(M[:, k, :], am[:, k, 0, :], am[:, k, 0, :], -3.0e38, ALU.max, ALU.max))
                nc.vector.tensor_scalar(am[:, k, 1, :], M[:, k, :], -1.0, None, ALU.mult)
                nc.vector.tensor_tensor(m[:, k, :], F[:, k, :], M[:, k, :], ALU.add).then_inc(exps_go, 1)
            for k in range(2):
                dve.wait_ge(ex_turned, k + 1)
                nc.vector.tensor_copy(g.tmE[:, :, k * P:(k + 1) * P], psE[k][:, :, :])

        @block.scalar
        def _(act):
            act.wait_ge(abs_ready, 1)
            nc.scalar.activation(e[:, :, :], poly[:, :, :], ACT.Exp, scale=-1.0).then_inc(e_ready, 1)
            act.wait_ge(e_ready, 1)
            nc.scalar.activation(lu[:, :, :], e[:, :, :], ACT.Ln, bias=1.0).then_inc(e_ready, 1)
            for k in range(2):
                act.wait_ge(exps_go, k + 1)
                nc.scalar.activation(ex[:, k, 0, :], am[:, k, 0, 0:P], ACT.Exp, bias=am[:, k, 1, P - 1:P])
                nc.scalar.activation(ex[:, k, 1, :], am[:, k, 1, P:S], ACT.Exp, bias=M[:, k, P - 1:P])
                nc.scalar.activation(ex[:, k, 2:4, :].rearrange("p a t -> p (a t)"), m[:, k, :], ACT.Exp,
                                     scale=-1.0).then_inc(exps, 1)

        @block.tensor
        def _(pe):
            pe.wait_ge(lf_ready, 1)
            for k in range(2):
                for gi in range(2):
                    for j in range(2):
                        last = nc.tensor.transpose(psH[k][:, gi, j * P:(j + 1) * P],
                                                   g.gates[:, j, gi, k * P:(k + 1) * P], g.ident[:, :])
                last.then_inc(heads, 1)
            for k in range(2):
                pe.wait_ge(exps, k + 1)
                for q in range(4):
                    last = nc.tensor.transpose(psE[k][:, q, :], ex[:, k, q, :], g.ident[:, :])
                last.then_inc(ex_turned, 1)

        @block.gpsimd
        def _(pool):
            c = Chain(pool, pch)
            pool.wait_ge(exps_go, 2)
            for q in range(3):
                src = am if q == 0 else rest
                c.link(nc.gpsimd.tensor_copy(parts[:, :, :, q, :], src[:, :, :, :]))
                if q < 2:
                    c.link(nc.gpsimd.tensor_tensor(rest[:, :, :, :], src[:, :, :, :], parts[:, :, :, q, :], ALU.subtract))
            nc.gpsimd.sem_inc(parts_ready, 1)

        @block.sync
        def _(sp):
            sp.wait_ge(parts_ready, 1)
            for k in range(2):
                for w in range(2):
                    sp.dma_start(d.am[w].rearrange("q b h t -> (b h) q t")[k * P:(k + 1) * P], parts[:, k, w, :, :]).then_inc(saved, 16)
            sp.wait_ge(saved, 64)


def attention_stage(nc, g, d):
    with ExitStack() as ctx:
        a = Pools(nc, ctx)
        ctxs = a.sb("ctxs", [P, 2, D])
        kT = [a.sb(f"kT{k}", [P, DC, S]) for k in range(2)]
        vaug = [a.sb(f"vaug{k}", [P, 2, NH, DH + 1]) for k in range(2)]
        kkw = a.sb("kkw", [P, NH, DH])
        qst = [a.sb(f"qst{k}", [P, DC, S]) for k in range(2)]
        aml = a.sb("aml", [38, NH, P], BF16)
        amr = a.sb("amr", [38, NH, P], BF16)
        dec = [a.sb(f"dec{k}", [P, 4, 4, P]) for k in range(2)]
        state = a.sb("state", [P, DC, 4, DH + 1])
        num = [a.sb(f"num{k}", [P, NH, DH + 1]) for k in range(2)]
        cen = [a.sb(f"cen{k}", [P, NH, DH]) for k in range(2)]
        sm = a.sb("sm", [P, 4, 8, NH])
        psQ = a.ps("psQ", [P, 4, 512])
        psL = a.ps("psL", [P, 4, P])
        psT = a.ps("psT", [P, DC, P])
        psO = a.ps("psO", [P, 2, 512])
        outT = a.sb("outT", [P, DC, P])
        sumT = a.sb("sumT", [P, P])
        pick = a.sb("pick", [P, DC, 32])
        (chain, am_done, dec_ready, qk_done, c_done, pv_done, si_done, si_evac, num_ready, cen_ready, sq_ready,
         ve_ready, hn_ready, x_done, v_ready, kk_ready, qs_ready, pch, ones_set, state_zero, out_copied, back_done,
         pick_set) = map(
            a.sem, ["at_" + n for n in (
                "chain", "am_done", "dec_ready", "qk_done", "c_done", "pv_done", "si_done", "si_evac", "num_ready",
                "cen_ready", "sq_ready", "ve_ready", "hn_ready", "x_done", "v_ready", "kk_ready", "qs_ready", "pool",
                "ones_set", "state_zero", "out_copied", "back_done", "pick_set")])
        ctx_in = a.sem("at_ctx_in")
        kT_in = [a.sem(f"at_kT_in{k}") for k in range(2)]
        am_in = [a.sem(f"at_am_in{k}") for k in range(2)]
        block = ctx.enter_context(nc.Block())
        R0, RPL, LOOPS = 3, 4, 7
        assert R0 + RPL * LOOPS + 1 == NT

        def run(eng, chain_obj, per, step, drain):
            for r in range(R0):
                step(0, r, False)
            with eng.Fori(0, LOOPS) as i:
                if chain_obj:
                    chain_obj.enter(i, per)
                for r in range(R0, R0 + RPL):
                    step(i, r, False)
                if chain_obj:
                    chain_obj.leave(LOOPS)
            step(LOOPS, R0, True)
            drain(LOOPS, R0)

        @block.sync
        def _(sp):
            def load_ctx(b):
                sp.dma_start(ctxs[:, :, :], d.ctx[bass.ds(b, 1)].rearrange("b (t p) d -> p (b t) d", p=P)).then_inc(ctx_in, 16)

            def load_keys(b, u):
                sp.dma_start(kT[u][:, :, :], d.ctxT[bass.ds(b, 1)].rearrange("b (c p) t -> p (b c) t", p=P)).then_inc(kT_in[u], 16)

            def load_decay(b, c):
                lo = 32 * c
                sp.dma_start(aml[lo + 3:lo + 6, :, :], d.am[0][:, bass.ds(b, 1), :, c * P:(c + 1) * P].rearrange(
                    "q b h t -> q (b h) t")).then_inc(am_in[c], 16)
                sp.dma_start(amr[lo:lo + 3, :, :], d.am[1][:, bass.ds(b, 1), :, c * P:(c + 1) * P].rearrange(
                    "q b h t -> q (b h) t")).then_inc(am_in[c], 16)
            sp.wait_ge(ones_set, 1)
            load_decay(0, 0)
            load_keys(0, 0)
            load_ctx(0)
            load_decay(0, 1)

            def load(b, u, earlier):
                sp.wait_ge(am_done, 8 * b - 4)
                load_decay(b, 0)
                if earlier:
                    sp.wait_ge(qk_done, 8 * b - 8)
                load_keys(b, u)
                sp.wait_ge(v_ready, b)
                sp.wait_ge(kk_ready, b)
                load_ctx(b)
                sp.wait_ge(am_done, 8 * b)
                load_decay(b, 1)
            load(1, 1, False)
            with sp.Fori(0, B // 2 - 1) as i:
                load(2 * i + 2, 0, True)
                load(2 * i + 3, 1, True)

        @block.tensor
        def _(pe):
            def scores(i, r, k):
                n = 4 * i + r
                u, c = (r // 2) % 2, r % 2
                if k == 0:
                    pe.wait_ge(am_in[c], 64 * i + 32 * (r // 2 + 1))
                if 4 * r + k >= 1:
                    pe.wait_ge(dec_ready, 4 * n + k)
                for gg in range(4):
                    h = 4 * gg + k
                    nc.tensor.matmul(psL[:, gg, :], aml[32 * c:32 * c + 6, h, :], amr[32 * c:32 * c + 6, h, :],
                                     start=(gg == 0), stop=(gg == 3), skip_group_check=True)
                nc.tensor.matmul(psL[:, :, :], g.identb[:, :], g.causal[:, :, :], start=False, stop=True,
                                 skip_group_check=True).then_inc(am_done, 1)
                if k == 0 and c == 0:
                    pe.wait_ge(kT_in[u], 16 * i + 16 * (r // 4 + 1))
                    pe.wait_ge(qs_ready, 2 * i + r // 2 + 1)
                if r >= 1:
                    pe.wait_ge(c_done, 4 * n - 3 + k)
                for gg in range(4):
                    last = nc.tensor.matmul(psQ[:, k, gg * P:(gg + 1) * P], kT[u][32 * k:32 * k + 32, gg, c * P:(c + 1) * P],
                                            qst[u][32 * k:32 * k + 32, gg, c * P:(c + 1) * P], start=True, stop=True)
                last.then_inc(qk_done, 1)

            def values(i, r):
                n = 4 * i + r
                u, c = (r // 2) % 2, r % 2
                pe.wait_ge(c_done, 4 * n + 4)
                if r >= 1:
                    pe.wait_ge(out_copied, n)
                for gg in range(4):
                    for k in range(4):
                        nc.tensor.matmul(psT[32 * k:32 * k + 32, gg, :], vaug[u][:, c, 4 * gg + k, 0:DH],
                                         dec[c][:, k, gg, :], start=True, stop=True)
                if r == 0:
                    pe.wait_ge(pick_set, 1)
                pe.wait_ge(si_evac, n + 1)
                for gg in range(4):
                    for k in range(4):
                        last = nc.tensor.matmul(psO[32 * k:32 * k + 32, 1, 0:P], pick[:, gg, :], dec[c][:, k, gg, :],
                                                start=(gg == 0), stop=(gg == 3), skip_group_check=True)
                last.then_inc(pv_done, 1)

            def back(i, r):
                n = 4 * i + r
                pe.wait_ge(out_copied, n + 1)
                for gg in range(4):
                    nc.tensor.transpose(psO[:, 0, gg * P:(gg + 1) * P], outT[:, gg, :], g.ident[:, :])
                nc.tensor.transpose(psO[:, 1, P:2 * P], sumT[:, :], g.ident[:, :]).then_inc(back_done, 1)

            def carry(i, r):
                n = 4 * i + r
                u, c = (r // 2) % 2, r % 2
                if r >= 1:
                    pe.wait_ge(num_ready, n)
                if c == 0:
                    pe.wait_ge(kk_ready, 2 * i + r // 2 + 1)
                    pe.wait_ge(v_ready, 2 * i + r // 2 + 1)
                    for gg in range(4):
                        last = nc.tensor.matmul(psO[:, gg // 2, (gg % 2) * 132:(gg % 2) * 132 + 132],
                                                kkw[:, 4 * gg:4 * gg + 4, :].rearrange("p h d -> p (h d)"),
                                                vaug[u][:, 0, 4 * gg:4 * gg + 4, :].rearrange("p h d -> p (h d)"),
                                                start=True, stop=True)
                else:
                    for gg in range(4):
                        last = nc.tensor.matmul(psO[:, gg // 2, (gg % 2) * 132:(gg % 2) * 132 + 132], qst[u][:, gg, P:S],
                                                state[:, gg, :, :].rearrange("p h d -> p (h d)"), start=True, stop=True)
                last.then_inc(si_done, 1)

            def step(i, r, is_last):
                if r >= 1:
                    values(i, r - 1)
                scores(i, r, 0)
                scores(i, r, 1)
                if r >= 1:
                    back(i, r - 1)
                scores(i, r, 2)
                scores(i, r, 3)
                carry(i, r)

            def drain(i, r):
                values(i, r)
                back(i, r)
            run(pe, None, 0, step, drain)

        @block.scalar
        def _(act):
            def exps(i, r, k):
                n = 4 * i + r
                c = r % 2
                act.wait_ge(am_done, 4 * n + k + 1)
                if r >= 2 and k == 0:
                    act.wait_ge(pv_done, n - 1)
                nc.scalar.activation(dec[c][:, k, :, :], psL[:, :, :], ACT.Exp).then_inc(dec_ready, 1)

            def copy_out(i, r):
                n = 4 * i + r
                act.wait_ge(pv_done, n + 1)
                if r >= 1:
                    act.wait_ge(back_done, n)
                nc.scalar.activation(sumT[:, :], psO[:, 1, 0:P], ACT.Copy)
                nc.scalar.activation(outT[:, :, :], psT[:, :, :], ACT.Copy).then_inc(out_copied, 1)

            def values(i, r):
                n, b, u = 4 * i + r, 2 * i + r // 2, (r // 2) % 2
                if r >= 4:
                    act.wait_ge(pv_done, n - 2)
                    act.wait_ge(si_done, n - 2)
                nc.scalar.activation(qst[u][:, :, :], g.qT_all[:, bass.ds(b * DC, DC), :], ACT.Copy).then_inc(qs_ready, 1)
                act.wait_ge(ctx_in, 32 * i + 16 * (r // 2 + 1))
                nc.scalar.activation(vaug[u][:, :, :, 0:DH], ctxs[:, :, :].rearrange("p t (h d) -> p t h d", d=DH),
                                     ACT.Copy).then_inc(v_ready, 1)

            def square(i, r):
                n = 4 * i + r
                act.wait_ge(cen_ready, n + 1)
                nc.scalar.activation(num[r % 2][:, :, 0:DH], cen[r % 2][:, :, :], ACT.Square).then_inc(sq_ready, 1)
            act.wait_ge(ones_set, 1)
            values(0, 0)

            def step(i, r, is_last):
                if r >= 1:
                    copy_out(i, r - 1)
                exps(i, r, 0)
                exps(i, r, 1)
                if r >= 2:
                    square(i, r - 2)
                exps(i, r, 2)
                exps(i, r, 3)
                if r % 2 == 1 and not is_last:
                    values(i, r + 1)

            def drain(i, r):
                copy_out(i, r)
                square(i, r - 1)
                square(i, r)
            run(act, None, 0, step, drain)

        @block.vector
        def _(dve):
            c_ = Chain(dve, chain)

            def weigh(i, r, k):
                n = 4 * i + r
                c = r % 2
                dve.wait_ge(dec_ready, 4 * n + k + 1)
                dve.wait_ge(qk_done, 4 * n + k + 1)
                dk = dec[c][:, k, :, :].rearrange("p a t -> p (a t)")
                nc.vector.scalar_tensor_tensor(out=dk, in0=psQ[:, k, :], scalar=SCALE, in1=dk,
                                               op0=ALU.mult, op1=ALU.mult).then_inc(c_done, 1)

            def gather(i, r):
                n = 4 * i + r
                c = r % 2
                dve.wait_ge(back_done, n + 1)
                o = psO[:, 0, :].rearrange("p (h e) -> p h e", e=DH)
                total = psO[:, 1, P:2 * P].rearrange("p (k x) -> p x k", x=32)[:, 0:4, :]
                to, tt = num[c][:, :, 0:DH], num[c][:, :, DH].rearrange("p (x k) -> p x k", k=4)
                if c == 0:
                    nc.vector.tensor_copy(to, o)
                    c_.link(nc.vector.tensor_copy(tt, total))
                else:
                    nc.vector.tensor_tensor(to, to, o, ALU.add)
                    c_.link(nc.vector.tensor_tensor(tt, tt, total, ALU.add))
                nc.vector.sem_inc(num_ready, 1)

            def carry(i, r):
                n = 4 * i + r
                c = r % 2
                dve.wait_ge(si_done, n + 1)
                if c == 0:
                    for k in range(4):
                        src = psO[32 * k:32 * k + 32, :, 0:264].rearrange("p a (g h e) -> p a g h e", g=2, e=33)[:, :, :, k, :]
                        dst = state[32 * k:32 * k + 32, :, k, :].rearrange("p (a g) e -> p a g e", a=2)
                        last = nc.vector.tensor_scalar(dst, src, SCALE, None, ALU.mult)
                    last.then_inc(si_evac, 1)
                else:
                    o = psO[:, :, 0:264].rearrange("p a (h e) -> p a h e", e=33)
                    em = tm(1, i, r).rearrange("p (a h o) -> p a h o", a=2, o=1).broadcast_to([P, 2, 8, 33])
                    nc.vector.tensor_tensor(num[1][:, :, :].rearrange("p (a h) e -> p a h e", a=2), o, em,
                                            ALU.mult).then_inc(si_evac, 1)

            def tm(kind, i, r):
                return g.tmE[:, kind, bass.ds((2 * i + r // 2) * NH, NH)]

            def centre(i, r):
                n = 4 * i + r
                c, q = r % 2, r % 4
                v = sm[:, q]
                c_.link(nc.vector.tensor_reduce(v[:, 0, :], num[c][:, :, 0:DH], AX.X, ALU.add))
                c_.link(nc.vector.tensor_scalar(v[:, 1, :], v[:, 0, :], 1.0 / DH, None, ALU.mult))
                nc.vector.tensor_tensor(cen[c][:, :, :], num[c][:, :, 0:DH],
                                        v[:, 1, :].rearrange("p (h o) -> p h o", o=1).broadcast_to([P, NH, DH]),
                                        ALU.subtract).then_inc(cen_ready, 1)
                total = num[c][:, :, DH]
                c_.link(nc.vector.scalar_tensor_tensor(out=v[:, 2, :], in0=total, scalar=-1.0, in1=total,
                                                       op0=ALU.mult, op1=ALU.max))
                c_.link(nc.vector.tensor_tensor(v[:, 2, :], v[:, 2, :], tm(2 + c, i, r), ALU.max))
                c_.link(nc.vector.tensor_scalar(v[:, 2, :], v[:, 2, :], CELL_EPS, None, ALU.add))
                c_.link(nc.vector.reciprocal(v[:, 3, :], v[:, 2, :]))
                c_.link(nc.vector.tensor_tensor(v[:, 4, :], v[:, 3, :], v[:, 3, :], ALU.mult))

            def spread(i, r):
                n = 4 * i + r
                v = sm[:, r % 4]
                dve.wait_ge(sq_ready, n + 1)
                c_.link(nc.vector.tensor_reduce(v[:, 5, :], num[r % 2][:, :, 0:DH], AX.X, ALU.add))
                c_.link(nc.vector.scalar_tensor_tensor(out=v[:, 5, :], in0=v[:, 5, :], scalar=1.0 / DH, in1=v[:, 4, :],
                                                       op0=ALU.mult, op1=ALU.mult))
                nc.vector.tensor_scalar(v[:, 5, :], v[:, 5, :], CELL_EPS, None, ALU.add).then_inc(ve_ready, 1)

            def residual(i, r):
                n = 4 * i + r
                dve.wait_ge(hn_ready, n + 1)
                x = g.xres[:, bass.ds(n, 1), :].rearrange("p a d -> p (a d)")
                nc.vector.tensor_tensor(x, x, cen[r % 2][:, :, :].rearrange("p h d -> p (h d)"), ALU.add).then_inc(x_done, 1)

            nc.vector.memset(state[:, :, :, :], 0.0).then_inc(state_zero, 1)
            dve.wait_ge(state_zero, 1)

            def step(i, r, is_last):
                if r >= 1:
                    carry(i, r - 1)
                if r >= 2:
                    centre(i, r - 2)
                weigh(i, r, 0)
                weigh(i, r, 1)
                if r >= 1:
                    gather(i, r - 1)
                if r >= 2:
                    spread(i, r - 2)
                weigh(i, r, 2)
                if r >= 3:
                    residual(i, r - 3)
                weigh(i, r, 3)

            def drain(i, r):
                carry(i, r)
                centre(i, r - 1)
                gather(i, r)
                spread(i, r - 1)
                residual(i, r - 2)
                centre(i, r)
                spread(i, r)
                residual(i, r - 1)
                residual(i, r)
            run(dve, c_, 4 * 10, step, drain)

        @block.gpsimd
        def _(pool):
            c_ = Chain(pool, pch)
            nc.gpsimd.memset(aml[:, :, :], 1.0)
            nc.gpsimd.memset(amr[:, :, :], 1.0)
            for k in range(2):
                last = nc.gpsimd.memset(vaug[k][:, :, :, DH:DH + 1], 1.0)
            last.then_inc(ones_set, 1)
            c_.link(nc.gpsimd.memset(pick[:, :, :], 0.0))
            for q in range(DC):
                last = nc.gpsimd.memset(pick[:, q, q:q + 1], 1.0)
            last.then_inc(pick_set, 1)

            def keys(i, r):
                n, b = 4 * i + r, 2 * i + r // 2
                pool.wait_ge(ctx_in, 32 * i + 16 * (r // 2 + 1))
                if r >= 2:
                    pool.wait_ge(si_done, n - 1)
                kw = g.tmE[:, 0, bass.ds(b * NH, NH)].rearrange("p (h o) -> p h o", o=1).broadcast_to([P, NH, DH])
                nc.gpsimd.tensor_tensor(kkw[:, :, :], ctxs[:, 0, :].rearrange("p (h d) -> p h d", d=DH), kw,
                                        ALU.mult).then_inc(kk_ready, 1)

            def normalise(i, r):
                n = 4 * i + r
                q = r % 4
                v = sm[:, q]
                pool.wait_ge(ve_ready, n + 1)
                c_.link(nc.gpsimd.tensor_tensor(v[:, 6, :], v[:, 5, :], g.neghalf[:, 0:NH], ALU.pow))
                c_.link(nc.gpsimd.tensor_tensor(v[:, 7, :], v[:, 6, :], v[:, 3, :], ALU.mult))
                c_.link(nc.gpsimd.tensor_tensor(cen[r % 2][:, :, :], cen[r % 2][:, :, :],
                                                v[:, 7, :].rearrange("p (h o) -> p h o", o=1).broadcast_to([P, NH, DH]),
                                                ALU.mult))
                flat = cen[r % 2][:, :, :].rearrange("p h d -> p (h d)")
                nc.gpsimd.tensor_tensor(flat, flat, g.coef[:, :], ALU.mult).then_inc(hn_ready, 1)

            keys(0, 0)

            def step(i, r, is_last):
                if r >= 2:
                    normalise(i, r - 2)
                if r % 2 == 1 and not is_last:
                    keys(i, r + 1)

            def drain(i, r):
                normalise(i, r - 1)
                normalise(i, r)
            run(pool, c_, 4 * 4 - 4, step, drain)


def routing_stage(nc, g, d):
    with ExitStack() as ctx:
        a = Pools(nc, ctx)
        ab, e, lu, mask, sp, score, sel, tmp, pos = [a.sb("rt_" + n, [P, NT, E]) for n in
                                                     ("ab", "e", "lu", "mask", "sp", "score", "sel", "tmp", "pos")]
        oh = a.sb("rt_oh", [P, 2, NT, E])
        chosen = a.sb("rt_chosen", [P, NT, E], BF16)
        tot, keep, upto = [a.sb("rt_" + n, [P, E, NT]) for n in ("tot", "keep", "upto")]
        top = a.sb("rt_top", [P, NT, 8])
        topi = a.sb("rt_topi", [P, NT, 8], U32)
        idx, gk, pk, ok, slot = [a.sb("rt_" + n, [P, 2, NT]) for n in ("idx", "gk", "pk", "ok", "slot")]
        den = a.sb("rt_den", [P, NT])
        ps_before = a.ps("rt_before", [P, NT, E])
        ps_total = a.ps("rt_total", [P, NT, E])
        chain, abs_ready, e_ready, sp_ready, score_ready, chosen_ready, counted = map(
            a.sem, ["rt_" + n for n in ("chain", "abs", "e_ready", "sp_ready", "score_ready", "chosen_ready", "counted")])
        block = ctx.enter_context(nc.Block())

        @block.vector
        def _(dve):
            c = Chain(dve, chain)
            l = g.logits[:, :, :]
            nc.vector.scalar_tensor_tensor(out=ab[:, :, :], in0=l, scalar=-1.0, in1=l, op0=ALU.mult,
                                           op1=ALU.max).then_inc(abs_ready, 1)
            dve.wait_ge(e_ready, 2)
            log1p_exp(nc, c, e[:, :, :], lu[:, :, :], ab[:, :, :], mask[:, :, :])
            nc.vector.scalar_tensor_tensor(out=sp[:, :, :], in0=l, scalar=0.0, in1=lu[:, :, :], op0=ALU.max,
                                           op1=ALU.add).then_inc(sp_ready, 1)
            dve.wait_ge(score_ready, 1)
            bias = g.gate_b[:, :].rearrange("p (o e) -> p o e", o=1).broadcast_to([P, NT, E])
            c.link(nc.vector.tensor_tensor(sel[:, :, :], score[:, :, :], bias, ALU.add))
            for t in range(NT):
                last = nc.vector.max(top[:, t, :], sel[:, t, :])
            c.link(last)
            for t in range(NT):
                last = nc.vector.max_index(topi[:, t, :], top[:, t, :], sel[:, t, :])
            c.link(last)
            ids = g.eiota[:, :].rearrange("p (o e) -> p o e", o=1).broadcast_to([P, NT, E])
            for k in range(2):
                c.link(nc.vector.tensor_copy(idx[:, k, :], topi[:, :, k]))
                mine = idx[:, k, :].rearrange("p (t o) -> p t o", o=1).broadcast_to([P, NT, E])
                c.link(nc.vector.tensor_tensor(oh[:, k, :, :], ids, mine, ALU.is_equal))
            nc.vector.tensor_tensor(chosen[:, :, :], oh[:, 0, :, :], oh[:, 1, :, :], ALU.add).then_inc(chosen_ready, 1)
            for k in range(2):
                c.link(nc.vector.tensor_tensor(tmp[:, :, :], score[:, :, :], oh[:, k, :, :], ALU.mult))
                c.link(nc.vector.tensor_reduce(gk[:, k, :], tmp[:, :, :], AX.X, ALU.add))
            c.link(nc.vector.tensor_tensor(den[:, :], gk[:, 0, :], gk[:, 1, :], ALU.add))
            c.link(nc.vector.reciprocal(den[:, :], den[:, :]))
            c.link(nc.vector.tensor_tensor(gk[:, :, :], gk[:, :, :],
                                           den[:, :].rearrange("p (o t) -> p o t", o=1).broadcast_to([P, 2, NT]), ALU.mult))
            c.link(nc.vector.memset(keep[:, :, :], 1.0))
            c.link(nc.vector.memset(keep[:, :, 0:1], 0.0))
            dve.wait_ge(counted, 1)
            c.link(nc.vector.tensor_copy(tot[:, :, :], ps_total[:, :, :].rearrange("p t e -> p e t")))
            flat = lambda x: x[:, :, :].rearrange("p e t -> p (e t)")
            c.link(nc.vector.tensor_tensor_scan(flat(upto), flat(keep), flat(tot), 0.0, ALU.mult, ALU.add))
            c.link(nc.vector.tensor_tensor(upto[:, :, :], upto[:, :, :], tot[:, :, :], ALU.subtract))
            c.link(nc.vector.tensor_tensor(pos[:, :, :], upto[:, :, :].rearrange("p e t -> p t e"), ps_before[:, :, :], ALU.add))
            for k in range(2):
                c.link(nc.vector.tensor_tensor(tmp[:, :, :], pos[:, :, :], oh[:, k, :, :], ALU.mult))
                c.link(nc.vector.tensor_reduce(pk[:, k, :], tmp[:, :, :], AX.X, ALU.add))
            c.link(nc.vector.tensor_scalar(ok[:, :, :], pk[:, :, :], float(CAP), None, ALU.is_lt))
            c.link(nc.vector.scalar_tensor_tensor(out=g.weight[:, :, :], in0=gk[:, :, :], scalar=g.tanh[:, 1:2],
                                                  in1=ok[:, :, :], op0=ALU.mult, op1=ALU.mult))
            c.link(nc.vector.scalar_tensor_tensor(out=slot[:, :, :], in0=idx[:, :, :], scalar=float(CAP), in1=pk[:, :, :],
                                                  op0=ALU.mult, op1=ALU.add))
            c.link(nc.vector.tensor_scalar(ok[:, :, :], ok[:, :, :], -NOWHERE, NOWHERE, ALU.mult, ALU.add))
            c.link(nc.vector.tensor_tensor(slot[:, :, :], slot[:, :, :], ok[:, :, :], ALU.add))
            c.link(nc.vector.tensor_copy(g.slot[:, :, :], slot[:, :, :]))

        @block.scalar
        def _(act):
            act.wait_ge(abs_ready, 1)
            nc.scalar.activation(e[:, :, :], ab[:, :, :], ACT.Exp, scale=-1.0).then_inc(e_ready, 1)
            act.wait_ge(e_ready, 1)
            nc.scalar.activation(lu[:, :, :], e[:, :, :], ACT.Ln, bias=1.0).then_inc(e_ready, 1)
            act.wait_ge(sp_ready, 1)
            nc.scalar.activation(score[:, :, :], sp[:, :, :], ACT.Sqrt).then_inc(score_ready, 1)

        @block.tensor
        def _(pe):
            pe.wait_ge(chosen_ready, 1)
            ch = chosen[:, :, :].rearrange("p t e -> p (t e)")
            nc.tensor.matmul(ps_before[:, :, :].rearrange("p t e -> p (t e)"), g.before[:, :], ch, start=True, stop=True)
            nc.tensor.matmul(ps_total[:, :, :].rearrange("p t e -> p (t e)"), g.onesb[:, :], ch, start=True,
                             stop=True).then_inc(counted, 1)


def load13(sp, g, d, expert, c):
    src = (d.ws13T[c * P:(c + 1) * P, :] if expert is None else
           d.w13T[bass.ds(expert, 1), c * P:(c + 1) * P, :].rearrange("e p n -> p (e n)"))
    sp.dma_start(g.raw13[:, c, :], src).then_inc(g.w_in[c], 16)


def load2(sp, g, d, expert):
    full = (FC - 1) * P
    if expert is None:
        two, one = d.ws2T[0:full, :].rearrange("(k p) n -> p k n", p=P), d.ws2T[full:FI, :]
    else:
        two = d.w2T[bass.ds(expert, 1), 0:full, :].rearrange("e (k p) n -> p (e k) n", p=P)
        one = d.w2T[bass.ds(expert, 1), full:FI, :].rearrange("e p n -> p (e n)")
    sp.dma_start(g.raw2[:, 0:FC - 1, :], two).then_inc(g.w_in[DC], 16)
    sp.dma_start(g.raw2[0:FLAST, FC - 1, :], one).then_inc(g.w_in[DC + 1], 16)


def load_weights(sp, g, d, expert):
    for c in range(DC):
        load13(sp, g, d, expert, c)
    load2(sp, g, d, expert)


def ffn_stage(nc, g, d, kind):
    shared, sending, collecting = kind != "experts", kind == "send", kind == "collect"
    COUNT = HB if shared else E
    FIRST = HB if collecting else 0
    tag = kind[0]
    WS = 1 if shared else 2
    rows = [P] * (FC - 1) + [FLAST]
    with ExitStack() as ctx:
        a = Pools(nc, ctx)
        raw13, raw2, piece = g.raw13, g.raw2, g.w_in
        BEFORE = {"send": 0, "experts": 16, "collect": 16 * (E + 1)}[kind]
        w13 = [[a.sb(f"{tag}w13{p}{k}", [P, DC, 2 * FI], F32R) for p in "hl"] for k in range(WS)]
        w2 = [[a.sb(f"{tag}w2{p}{k}", [P, FC, D], F32R) for p in "hl"] for k in range(WS)]
        xrows = [a.sb(f"{tag}xrows{k}", [P, 2, D]) for k in range(2)]
        xs = [[a.sb(f"{tag}x{p}{k}", [P, DC, S], F32R) for p in "hl"] for k in range(2)]
        hh = a.sb(tag + "hh", [P, FC, S])
        hs = [[a.sb(f"{tag}h{p}{k}", [P, FC, S], F32R) for p in "hl"] for k in range(2)]
        sg = a.sb(tag + "sg", [P, FC, S])
        ystage = None if shared else [a.sb(f"{tag}ystage{k}", [P, 2, D]) for k in range(2)]
        psT = a.ps(tag + "psT", [P, DC, S])
        psH = [a.ps(f"{tag}psH{m}", [P, 2, S]) for m in range(FC)]
        psY = [a.ps(f"{tag}psY{j}", [P, D]) for j in range(2)]
        names = ["turned", "h_done", "y_done", "xh_ready", "xl_ready", "sg_ready", "hh_done", "hh_high", "hl_ready",
                 "wh13", "wh2", "wl13", "wl2"] + (["x_rows", "y_taken"] if shared else ["y_staged"])
        names += ["sent_ready", "hold"] if sending else []
        names += ["idx_ready", "hold", "chain", "blank", "done"] if collecting else []
        s = {n: a.sem(f"{tag}_{n}") for n in names}
        x_in = None if shared else [a.sem(f"{tag}_x_in{k}") for k in range(2)]
        y_out = None if shared else [a.sem(f"{tag}_y_out{k}") for k in range(2)]
        if sending:
            sent = [a.sb(f"{tag}sent{k}", [P, D]) for k in range(4)]
            sidx = a.sb(tag + "sidx", [P, 4, 2], U32)
            sent_out = [a.sem(f"{tag}_sent_out{k}") for k in range(4)]
        if collecting:
            got = [a.sb(f"{tag}got{k}", [P, 2, 2, D]) for k in range(2)]
            gidx = [a.sb(f"{tag}gidx{k}", [P, 2, 2], U32) for k in range(2)]
            got_in = [a.sem(f"{tag}_got_in{k}") for k in range(2)]
            out_done = [a.sem(f"{tag}_out_done{k}") for k in range(2)]
        block = ctx.enter_context(nc.Block())
        R0, LOOPS = 3, (COUNT - 4) // 2

        def run(eng, step, drain, chain=None, per=0):
            for r in range(R0):
                step(0, r, False)
            with eng.Fori(0, LOOPS) as i:
                if chain:
                    chain.enter(i, per)
                for r in range(R0, R0 + 2):
                    step(i, r, False)
                if chain:
                    chain.leave(LOOPS)
            step(LOOPS, R0, True)
            drain(LOOPS, R0 + 1)

        @block.sync
        def _(sp):
            def next13(q):
                for c in range(DC):
                    sp.wait_ge(s["wh13"], DC * q - DC + c + 1)
                    sp.wait_ge(s["wl13"], DC * q - DC + c + 1)
                    load13(sp, g, d, q, c)

            def next2(q):
                sp.wait_ge(s["wh2"], 2 * q)
                sp.wait_ge(s["wl2"], 2 * q)
                load2(sp, g, d, q)

            def split_done():
                n = 1 if shared else COUNT
                for name, per in (("wh13", DC), ("wl13", DC), ("wh2", 2), ("wl2", 2)):
                    sp.wait_ge(s[name], per * n)

            def load_rows(q, r, wait):
                if wait:
                    sp.wait_ge(s["turned"], q - 1)
                sp.dma_start(xrows[r % 2][:, :, :], d.disp[bass.ds(q * CAP, CAP), :].rearrange(
                    "(j p) n -> p j n", p=P)).then_inc(x_in[r % 2], 16)

            def store(q, r):
                sp.wait_ge(s["y_staged"], 2 * q + 2)
                sp.dma_start(d.yexp[bass.ds(q * CAP, CAP), :].rearrange("(j p) n -> p j n", p=P),
                             ystage[r % 2][:, :, :]).then_inc(y_out[r % 2], 16)

            if shared:
                if sending:
                    split_done()
                    load_weights(sp, g, d, 0)
                if collecting:
                    def leave(b, k, n):
                        sp.wait_ge(s["done"], n)
                        sp.dma_start(d.out[bass.ds(b, 1)].rearrange("a (j p) n -> p (a j) n", p=P),
                                     g.xres[:, bass.ds(2 * b, 2), :]).then_inc(out_done[k], 16)

                    def step(i, r, is_last):
                        q = 2 * i + r
                        if r >= 2:
                            leave(q + (FIRST - 2), 1, 2 * q - 1)
                        leave(q, 0, 2 * q if r >= 2 else q + 1)

                    def drain(i, r):
                        q = 2 * i + r
                        leave(q + (FIRST - 2), 1, 2 * q - 1)
                        leave(q + (FIRST - 1), 1, 2 * q)
                        for k in range(2):
                            sp.wait_ge(out_done[k], 16 * COUNT)
                    run(sp, step, drain)
            else:
                load_rows(0, 0, False)
                load_rows(1, 1, False)
                next13(1)

                def ahead(q, r, results):
                    load_rows(q + 2, r, True)
                    next13(q + 2)
                    next2(q + 1)
                    if results:
                        store(q - 1, r - 1)
                ahead(0, 0, False)
                ahead(1, 1, True)
                with sp.Fori(0, (COUNT - 4) // 2) as i:
                    for r in range(2, 4):
                        ahead(2 * i + r, r, True)
                next2(COUNT - 1)
                store(COUNT - 3, COUNT - 3)
                store(COUNT - 2, COUNT - 2)
                split_done()
                load_weights(sp, g, d, None)
                store(COUNT - 1, COUNT - 1)
                for k in range(2):
                    sp.wait_ge(y_out[k], 8 * COUNT)

        @block.tensor
        def _(pe):
            def turn(i, r):
                q = 2 * i + r
                if shared:
                    pe.wait_ge(s["x_rows"], q + 1)
                else:
                    pe.wait_ge(x_in[r % 2], 16 * i + 16 * (r // 2 + 1))
                if r >= 1:
                    pe.wait_ge(s["xl_ready"], q)
                for c in range(DC):
                    for j in range(2):
                        last = nc.tensor.transpose(psT[:, c, j * P:(j + 1) * P], xrows[r % 2][:, j, c * P:(c + 1) * P],
                                                   g.ident[:, :])
                last.then_inc(s["turned"], 1)

            def hidden(i, r, m):
                q, n = 2 * i + r, rows[m]
                w, x = w13[r % WS], xs[r % 2]
                if m == 0:
                    pe.wait_ge(s["xl_ready"], q + 1)
                    if shared:
                        pe.wait_ge(s["wl13"], DC)
                        pe.wait_ge(s["wh13"], DC)
                    else:
                        pe.wait_ge(s["wl13"], DC * q + DC)
                        pe.wait_ge(s["wh13"], DC * q + DC)
                if r >= 1:
                    pe.wait_ge(s["hh_done"], 3 * q - 2 + m)
                for v in range(2):
                    for c in range(DC):
                        col = v * FI + m * P
                        for p, (wp, xp) in enumerate(((0, 0), (0, 1), (1, 0))):
                            last = nc.tensor.matmul(psH[m][0:n, v, :], w[wp][:, c, col:col + n], x[xp][:, c, :],
                                                    start=(c == 0 and p == 0), stop=(c == DC - 1 and p == 2))
                last.then_inc(s["h_done"], 1)

            def back(i, r):
                q = 2 * i + r
                w, h = w2[r % WS], hs[r % 2]
                pe.wait_ge(s["hl_ready"], 3 * q + 3)
                if shared:
                    pe.wait_ge(s["wl2"], 2)
                    pe.wait_ge(s["wh2"], 2)
                else:
                    pe.wait_ge(s["wl2"], 2 * q + 2)
                    pe.wait_ge(s["wh2"], 2 * q + 2)
                for j in range(2):
                    if r >= 1:
                        pe.wait_ge(s["y_taken" if shared else "y_staged"], 2 * q - 1 + j)
                    for k in range(FC):
                        n = rows[k]
                        for p, (hp, wp) in enumerate(((0, 0), (0, 1), (1, 0))):
                            last = nc.tensor.matmul(psY[j][:, :], h[hp][0:n, k, j * P:(j + 1) * P], w[wp][0:n, k, :],
                                                    start=(k == 0 and p == 0), stop=(k == FC - 1 and p == 2))
                    last.then_inc(s["y_done"], 1)
            turn(0, 0)

            def step(i, r, is_last):
                hidden(i, r, 0)
                hidden(i, r, 1)
                if not is_last:
                    turn(i, r + 1)
                hidden(i, r, 2)
                if r >= 1:
                    back(i, r - 1)
            run(pe, step, lambda i, r: back(i, r - 1))

        @block.scalar
        def _(act):
            def split_x(i, r):
                q = 2 * i + r
                act.wait_ge(s["turned"], q + 1)
                nc.scalar.activation(xs[r % 2][0][:, :, :], psT[:, :, :], ACT.Copy).then_inc(s["xh_ready"], 1)

            def split13(i, r):
                for c in range(DC):
                    act.wait_ge(piece[c], BEFORE + (16 if shared else 32 * i + 16 * (r + 1)))
                    nc.scalar.activation(w13[r % WS][0][:, c, :], raw13[:, c, :], ACT.Copy).then_inc(s["wh13"], 1)

            def split2(i, r):
                act.wait_ge(piece[DC], BEFORE + (16 if shared else 32 * i + 16 * (r + 1)))
                nc.scalar.activation(w2[r % WS][0][:, 0:FC - 1, :], raw2[:, 0:FC - 1, :], ACT.Copy).then_inc(s["wh2"], 1)
                act.wait_ge(piece[DC + 1], BEFORE + (16 if shared else 32 * i + 16 * (r + 1)))
                nc.scalar.activation(w2[r % WS][0][0:FLAST, FC - 1, :], raw2[0:FLAST, FC - 1, :], ACT.Copy).then_inc(s["wh2"], 1)

            def silu(i, r, m):
                q, n = 2 * i + r, rows[m]
                act.wait_ge(s["h_done"], 3 * q + m + 1)
                if r >= 1:
                    act.wait_ge(s["hh_done"], 3 * q - 2 + m)
                nc.scalar.activation(sg[0:n, m, :], psH[m][0:n, 0, :], ACT.Silu).then_inc(s["sg_ready"], 1)

            def high(i, r, m):
                q, n = 2 * i + r, rows[m]
                act.wait_ge(s["hh_done"], 3 * q + m + 1)
                nc.scalar.activation(hs[r % 2][0][0:n, m, :], hh[0:n, m, :], ACT.Copy).then_inc(s["hh_high"], 1)

            def stage(i, r):
                q = 2 * i + r
                if r >= 2:
                    act.wait_ge(y_out[r % 2], 16 * i + 16 * (r // 2))
                for j in range(2):
                    act.wait_ge(s["y_done"], 2 * q + j + 1)
                    nc.scalar.activation(ystage[r % 2][:, j, :], psY[j][:, :], ACT.Copy).then_inc(s["y_staged"], 1)

            split13(0, 0)
            split_x(0, 0)

            def step(i, r, is_last):
                silu(i, r, 0)
                silu(i, r, 1)
                high(i, r, 0)
                if not is_last:
                    split_x(i, r + 1)
                if not shared and not is_last:
                    split13(i, r + 1)
                silu(i, r, 2)
                high(i, r, 1)
                high(i, r, 2)
                if not shared or r == 0 and not is_last:
                    split2(i, r)
                if not shared and r >= 1:
                    stage(i, r - 1)
            run(act, step, lambda i, r: None if shared else stage(i, r - 1))

        @block.vector
        def _(dve):
            ch = Chain(dve, s["chain"]) if collecting else None
            row = lambda t: g.xres[:, bass.ds(t, 1), :].rearrange("p a n -> p (a n)")

            def normed(out, t):
                return nc.vector.tensor_scalar(out, row(t), g.mu_all[:, bass.ds(t, 1)], g.rs_all[:, bass.ds(t, 1)],
                                               ALU.subtract, ALU.mult)

            def fetch(i, r):
                q = 2 * i + r
                if r >= 2:
                    dve.wait_ge(s["turned"], q - 1)
                for j in range(2):
                    last = normed(xrows[r % 2][:, j, :], 2 * q + (2 * FIRST + j))
                last.then_inc(s["x_rows"], 1)

            def split_x(i, r):
                q = 2 * i + r
                dve.wait_ge(s["xh_ready"], q + 1)
                nc.vector.tensor_tensor(xs[r % 2][1][:, :, :], psT[:, :, :], xs[r % 2][0][:, :, :].bitcast(F32),
                                        ALU.subtract).then_inc(s["xl_ready"], 1)

            def split13(i, r, c):
                q = 2 * i + r
                dve.wait_ge(s["wh13"], DC * q + c + 1)
                nc.vector.tensor_tensor(w13[r % WS][1][:, c, :], raw13[:, c, :], w13[r % WS][0][:, c, :].bitcast(F32),
                                        ALU.subtract).then_inc(s["wl13"], 1)

            def split2(i, r):
                q = 2 * i + r
                h, l = w2[r % WS]
                dve.wait_ge(s["wh2"], 2 * q + 1)
                nc.vector.tensor_tensor(l[:, 0:FC - 1, :], raw2[:, 0:FC - 1, :], h[:, 0:FC - 1, :].bitcast(F32),
                                        ALU.subtract).then_inc(s["wl2"], 1)
                dve.wait_ge(s["wh2"], 2 * q + 2)
                nc.vector.tensor_tensor(l[0:FLAST, FC - 1, :], raw2[0:FLAST, FC - 1, :], h[0:FLAST, FC - 1, :].bitcast(F32),
                                        ALU.subtract).then_inc(s["wl2"], 1)

            def gated(i, r, m):
                q, n = 2 * i + r, rows[m]
                dve.wait_ge(s["sg_ready"], 3 * q + m + 1)
                if r >= 1:
                    dve.wait_ge(s["hl_ready"], 3 * q - 2 + m)
                nc.vector.tensor_tensor(hh[0:n, m, :], sg[0:n, m, :], psH[m][0:n, 1, :], ALU.mult).then_inc(s["hh_done"], 1)

            def add(i, r):
                q = 2 * i + r
                for j in range(2):
                    dve.wait_ge(s["y_done"], 2 * q + j + 1)
                    x = row(2 * q + (2 * FIRST + j))
                    nc.vector.scalar_tensor_tensor(out=x, in0=psY[j][:, :], scalar=g.tanh[:, 1:2], in1=x, op0=ALU.mult,
                                                   op1=ALU.add).then_inc(s["y_taken"], 1)

            def send(i, r, k):
                q = 2 * i + r
                if r >= 1:
                    dve.wait_ge(sent_out[k], 32 * q)
                normed(sent[k][:, :], 4 * q + k)
                nc.vector.tensor_copy(sidx[:, k, :], g.slot[:, :, bass.ds(4 * q + k, 1)].rearrange(
                    "p k o -> p (k o)")).then_inc(s["sent_ready"], 1)

            def index(b, k):
                nc.vector.tensor_copy(gidx[k][:, :, :], g.slot[:, :, bass.ds(2 * b, 2)]).then_inc(s["idx_ready"], 1)

            def collect(b, k, n):
                dve.wait_ge(got_in[k], 64 * n)
                for e in range(2):
                    for j in range(2):
                        x = row(2 * b + j)
                        last = nc.vector.scalar_tensor_tensor(out=x, in0=got[k][:, e, j, :],
                                                              scalar=g.weight[:, e, bass.ds(2 * b + j, 1)], in1=x,
                                                              op0=ALU.mult, op1=ALU.add)
                    if e == 0:
                        ch.link(last)
                last.then_inc(s["done"], 1)

            if collecting:
                for k in range(2):
                    last = nc.vector.memset(got[k][:, :, :, :], 0.0)
                last.then_inc(s["blank"], 1)
                index(0, 0)
                index(FIRST, 1)
            if shared:
                fetch(0, 0)
            for c in range(DC):
                split13(0, 0, c)
            split_x(0, 0)

            def step(i, r, is_last):
                q = 2 * i + r
                if shared and not is_last:
                    fetch(i, r + 1)
                if collecting and r >= 2:
                    dve.wait_ge(s["y_taken"], 2 * q - 2)
                    collect(q + (FIRST - 2), 1, q - 1)
                    index(q + (FIRST - 1), 1)
                gated(i, r, 0)
                if sending:
                    send(i, r, 0)
                gated(i, r, 1)
                if sending:
                    send(i, r, 1)
                if not is_last:
                    split_x(i, r + 1)
                if not shared and not is_last:
                    for c in range(DC):
                        split13(i, r + 1, c)
                if collecting:
                    collect(q, 0, q + 1)
                    index(q + FIRST if is_last else q + 1, 0)
                gated(i, r, 2)
                if sending:
                    send(i, r, 2)
                    send(i, r, 3)
                if not shared or r == 0 and not is_last:
                    split2(i, r)
                if shared and r >= 1:
                    add(i, r - 1)

            def drain(i, r):
                q = 2 * i + r
                if shared:
                    add(i, r - 1)
                if collecting:
                    dve.wait_ge(s["y_taken"], 2 * q)
                    collect(q + (FIRST - 2), 1, q - 1)
                    collect(q + (FIRST - 1), 0, q + 1)
            run(dve, step, drain, ch if collecting else None, 2 * 2)

        @block.gpsimd
        def _(pool):
            last_row = pool.to_reg(E * CAP - 1) if shared else None
            hold = Chain(pool, s["hold"]) if shared else None

            def held():
                if not (isinstance(hold.base, int) and hold.base + hold.n == 0):
                    pool.wait_ge(s["hold"], hold.base + hold.n)
                hold.n += 1
                nc.gpsimd.tensor_tensor(g.idle[:, 1:2], g.neghalf[:, 0:1], g.neghalf[:, 1:2], ALU.mult).then_inc(s["hold"], 1)

            def rest(i, r, m):
                q, n = 2 * i + r, rows[m]
                pool.wait_ge(s["hh_high"], 3 * q + m + 1)
                nc.gpsimd.tensor_tensor(hs[r % 2][1][0:n, m, :], hh[0:n, m, :], hs[r % 2][0][0:n, m, :].bitcast(F32),
                                        ALU.subtract).then_inc(s["hl_ready"], 1)

            def scatter(i, r, k):
                q = 2 * i + r
                pool.wait_ge(s["sent_ready"], 4 * q + k + 1)
                held()
                for e in range(2):
                    nc.gpsimd.indirect_dma_start(
                        out=d.disp[:, :], out_offset=bass.IndirectOffsetOnAxis(ap=sidx[:, k, e:e + 1], axis=0),
                        in_=sent[k][:, :], in_offset=None, bounds_check=last_row, oob_is_err=False).then_inc(sent_out[k], 16)

            def gather(k, n):
                pool.wait_ge(s["idx_ready"], n)
                held()
                for e in range(2):
                    for j in range(2):
                        nc.gpsimd.indirect_dma_start(
                            out=got[k][:, e, j, :], out_offset=None, in_=d.yexp[:, :],
                            in_offset=bass.IndirectOffsetOnAxis(ap=gidx[k][:, e, j:j + 1], axis=0),
                            bounds_check=last_row, oob_is_err=False).then_inc(got_in[k], 16)

            def step(i, r, is_last):
                q = 2 * i + r
                for m in range(FC):
                    rest(i, r, m)
                    if sending:
                        scatter(i, r, m)
                        if m == 2:
                            scatter(i, r, 3)
                    if collecting and r >= 2 and m == 0:
                        gather(1, 2 * q + 1)
                if collecting:
                    gather(0, 2 * q + 2 if r >= 2 else q + 3)

            if collecting:
                gather(0, 1)
                gather(1, 2)

            def drain(i, r):
                if sending:
                    for k in range(4):
                        pool.wait_ge(sent_out[k], 32 * COUNT)
            run(pool, step, drain, hold, 8 if sending else 4 if collecting else 0)


def build(nc, d):
    with ExitStack() as ctx:
        a = Pools(nc, ctx)

        class g:
            xres = a.sb("xres", [P, NT, D])
            ident = a.sb("ident", [P, P])
            identb = a.sb("identb", [P, P], BF16)
            causal = a.sb("causal", [P, 4, P], BF16)
            before = a.sb("before", [P, P], BF16)
            onesb = a.sb("onesb", [P, P], BF16)
            neghalf = a.sb("neghalf", [P, NH])
            eiota = a.sb("eiota", [P, E])
            wr = a.sb("wr", [P, DC, E])
            bias = a.sb("bias", [P, 2 * NH])
            coef = a.sb("coef", [P, D])
            gate_b = a.sb("gate_b_rows", [P, E])
            tanh = a.sb("tanh", [P, 2])
            mu_all = a.sb("mu_all", [P, NT])
            rs_all = a.sb("rs_all", [P, NT])
            idle = a.sb("idle", [P, 2])
            rs_stage = a.sb("rs_stage", [P, 2, 4])

        with ExitStack() as cell:
            c = Pools(nc, cell)
            g.qT_all = c.sb("qT_all", [P, B * DC, S])
            g.tmE = c.sb("tmE", [P, 4, B * NH])
            with ExitStack() as gates:
                t = Pools(nc, gates)
                g.gates = t.sb("gates", [P, 2, 2, B * NH])
                g.wg = t.sb("wg", [P, DC, 2 * NH])
                g.wc = t.sb("wc", [P, DC, 2 * NH])
                setup_stage(nc, g, d)
                norm_project_stage(nc, g, d, True)
                gate_stage(nc, g, d)
            attention_stage(nc, g, d)
        g.weight = a.sb("weight", [P, 2, NT])
        g.slot = a.sb("slot", [P, 2, NT], U32)
        g.raw13 = a.sb("raw13", [P, DC, 2 * FI])
        g.raw2 = a.sb("raw2", [P, FC, D])
        g.w_in = [a.sem(f"w_in{k}") for k in range(DC + 2)]
        with ExitStack() as router:
            g.logits = Pools(nc, router).sb("logits", [P, NT, E])
            norm_project_stage(nc, g, d, False)
            routing_stage(nc, g, d)
        for kind in ("send", "experts", "collect"):
            ffn_stage(nc, g, d, kind)


def kernel(**inputs):
    import numpy as _np
    import concourse.bacc as _bacc
    from concourse import mybir as _mybir
    from concourse.bass_utils import run_bass_kernel_spmd as _run

    nc = _bacc.Bacc("TRN2", target_bir_lowering=False, num_devices=1)
    v = {k: _np.asarray(x) for k, x in inputs.items()}
    cat = lambda *xs: _np.concatenate(xs, axis=-1)
    w1, w3, w2 = v["L0_ffn_W1"], v["L0_ffn_W3"], v["L0_ffn_W2"]
    arrays = {
        "x": v["x"], "ctx": v["ctx_2048"], "ctxT": v["ctx_2048"].transpose(0, 2, 1),
        "g_xattn": v["g_xattn"].reshape(1, 1), "g_ffn": v["g_ffn"].reshape(1, 1),
        "wgate": cat(v["L0_xattn_Wi"], v["L0_xattn_Wf"]).reshape(3, D, 2 * NH),
        "gbias": cat(v["L0_xattn_bi"], v["L0_xattn_bf"]).reshape(1, 2 * NH),
        "ln_scale": v["L0_xattn_ln_scale"].reshape(1, D),
        "gate_wT": v["L0_ffn_gate_w"].T, "gate_b": v["L0_ffn_gate_b"].reshape(1, E),
        "w13T": cat(w1.transpose(0, 2, 1), w3.transpose(0, 2, 1)), "w2T": w2.transpose(0, 2, 1),
        "ws13T": cat(v["L0_ffn_Ws1"].T, v["L0_ffn_Ws3"].T), "ws2T": v["L0_ffn_Ws2"].T,
    }
    arrays = {k: _np.ascontiguousarray(a) for k, a in arrays.items()}

    ins = {name: nc.dram_tensor(name, a.shape, _mybir.dt.from_np(a.dtype), kind="ExternalInput").ap()
           for name, a in arrays.items()}
    program(nc, ins)
    r = _run(nc, [arrays], core_ids=[0])
    return r.results[0]["out"]


class Dram:

    def __init__(self, ins, out, am, disp, yexp):
        self.x, self.ctx, self.ctxT = ins["x"], ins["ctx"], ins["ctxT"]
        self.g_xattn, self.g_ffn, self.wgate, self.gbias = ins["g_xattn"], ins["g_ffn"], ins["wgate"], ins["gbias"]
        self.ln_scale, self.gate_wT, self.gate_b = ins["ln_scale"], ins["gate_wT"], ins["gate_b"]
        self.w13T, self.w2T, self.ws13T, self.ws2T = ins["w13T"], ins["w2T"], ins["ws13T"], ins["ws2T"]
        self.out, self.am, self.disp, self.yexp = out, am, disp, yexp


def program(nc, ins):
    out = nc.dram_tensor("out", (B, S, D), F32, kind="ExternalOutput").ap()
    am = nc.dram_tensor("am", (2, 3, B, NH, S), BF16, kind="Internal").ap()
    disp = nc.dram_tensor("disp", (E * CAP, D), F32, kind="Internal").ap()
    yexp = nc.dram_tensor("yexp", (E * CAP, D), F32, kind="Internal").ap()
    build(nc, Dram(ins, out, am, disp, yexp))
```

```python
from contextlib import ExitStack

import numpy as np

import concourse.bass as bass
from concourse import mybir

F32 = mybir.dt.float32
F32R = mybir.dt.float32r
BF16 = mybir.dt.bfloat16
U32 = mybir.dt.uint32
ACT = mybir.ActivationFunctionType
ALU = mybir.AluOpType
AX = mybir.AxisListType

P = 128
B, S, D = 16, 256, 512
NH, DH = 16, 32
NT = B * S // P
DC = D // P
E, FI, CAP = 16, 352, 256
FC = -(-FI // P)
FLAST = FI - (FC - 1) * P
HB = B // 2
LN_EPS, CELL_EPS = 1e-5, 1e-6
SCALE = float(DH) ** -0.5
MASKED = -1e30
SMALL_E = 0.01
NOWHERE = 1.0e6


class Chain:

    def __init__(self, eng, sem):
        self.eng, self.sem, self.n, self.base = eng, sem, 0, 0

    def link(self, ins):
        self.n += 1
        ins.then_inc(self.sem, 1)
        self.eng.wait_ge(self.sem, self.base + self.n)

    def enter(self, i, per):
        self.static = self.n + self.base
        self.base, self.n, self.per = i * per + self.static, 0, per

    def leave(self, rounds):
        assert self.n == self.per, (self.n, self.per)
        self.base, self.n = 0, self.static + self.per * rounds


class Pools:

    def __init__(self, nc, ctx):
        self.nc, self.ctx = nc, ctx

    def sb(self, name, shape, dt=F32):
        return self.ctx.enter_context(self.nc.sbuf_tensor(name, shape, dt))

    def ps(self, name, shape, dt=F32):
        return self.ctx.enter_context(self.nc.psum_tensor(name, shape, dt))

    def sem(self, name):
        return self.ctx.enter_context(self.nc.semaphore(name))


def load_rows(eng, g, d, p, s):
    eng.dma_start(g.xres[:, bass.ds(4 * p, 4), :],
                  d.x[bass.ds(2 * p, 2)].rearrange("b (t p) d -> p (b t) d", p=P)).then_inc(g.x_in[s], 16)


def setup_stage(nc, g, d):
    with ExitStack() as ctx:
        a = Pools(nc, ctx)
        wkv = a.sb("wkv", [P, 2, DC, 2 * NH])
        loaded, const, ch = map(a.sem, ("s0_loaded", "s0_const", "s0_chain"))
        block = ctx.enter_context(nc.Block())

        @block.sync
        def _(sp):
            loads = [
                (g.wg[:, :, :], d.wgate[0].rearrange("(c p) n -> p c n", p=P)),
                (wkv[:, 0, :, :], d.wgate[1].rearrange("(c p) n -> p c n", p=P)),
                (wkv[:, 1, :, :], d.wgate[2].rearrange("(c p) n -> p c n", p=P)),
            ]
            for dst, src in loads:
                sp.dma_start(dst, src).then_inc(loaded, 16)
            sp.wait_ge(loaded, 16 * 3)

        @block.gpsimd
        def _(pool):
            c = Chain(pool, const)
            c.link(nc.gpsimd.memset(g.ident[:, :], 0.0))
            c.link(nc.gpsimd.affine_select(out=g.ident[:, :], in_=g.ident[:, :], compare_op=ALU.not_equal, fill=1.0,
                                           base=0, pattern=[[-1, P]], channel_multiplier=1))
            c.link(nc.gpsimd.tensor_copy(g.identb[:, :], g.ident[:, :]))
            c.link(nc.gpsimd.memset(g.causal[:, :, :], 0.0))
            c.link(nc.gpsimd.affine_select(out=g.causal[:, :, :], in_=g.causal[:, :, :], compare_op=ALU.is_ge,
                                           fill=MASKED, base=0, pattern=[[0, 4], [1, P]], channel_multiplier=-1))
            c.link(nc.gpsimd.memset(g.before[:, :], 1.0))
            c.link(nc.gpsimd.affine_select(out=g.before[:, :], in_=g.before[:, :], compare_op=ALU.is_gt,
                                           fill=0.0, base=0, pattern=[[1, P]], channel_multiplier=-1))
            c.link(nc.gpsimd.memset(g.fold[:, :], 0.0))
            for q in range(DC):
                c.link(nc.gpsimd.affine_select(out=g.fold[:, :], in_=g.fold[:, :], compare_op=ALU.not_equal, fill=1.0,
                                               base=-32 * q, pattern=[[-1, 32]], channel_multiplier=1))
            c.link(nc.gpsimd.memset(g.wr[:, :, E:32], 0.0))
            c.link(nc.gpsimd.memset(g.onesb[:, :], 1.0))
            c.link(nc.gpsimd.memset(g.neghalf[:, :], -0.5))
            c.link(nc.gpsimd.iota(g.eiota[:, :], pattern=[[1, E]], base=0, channel_multiplier=0,
                                  allow_small_or_imprecise_dtypes=True))

        @block.scalar
        def _(act):
            for p in range(2):
                load_rows(act, g, d, p, p)

        @block.vector
        def _(dve):
            dve.wait_ge(loaded, 16 * 3)
            nc.vector.tensor_tensor(g.wc[:, :, :], wkv[:, 0, :, :], wkv[:, 1, :, :], ALU.add).then_inc(ch, 1)


def norm_project_stage(nc, g, d, first):
    tag = "g" if first else "r"
    PAIRS = B // 2
    with ExitStack() as ctx:
        a = Pools(nc, ctx)
        stats = a.sb(tag + "stats", [P, 2, 4, 6])
        mv = a.sb(tag + "mv", [P, 2, 4, 2])
        var = a.sb(tag + "var", [P, 2, 4])
        xn = a.sb(tag + "xn", [P, 2, 4, D])
        part = [a.sb(f"{tag}part{k}", [P, S]) for k in range(2)]
        xT = [a.sb(f"{tag}xT{k}", [P, DC, S]) for k in range(2)]
        psT = [a.ps(f"{tag}psT{k}", [P, DC, S]) for k in range(2)]
        psG = [a.ps(f"{tag}psG{k}", [P, 512]) for k in range(2)]
        psF = [a.ps(f"{tag}psF{k}", [P, 512]) for k in range(2)]
        chain, var_ready, rs_ready, xn_ready, turned, xt_ready, projected, part_ready, folded, kept = map(
            a.sem, [f"{tag}_{n}" for n in ("chain", "var_ready", "rs_ready", "xn_ready", "turned", "xt_ready",
                                           "projected", "part_ready", "folded", "kept")])
        if first:
            cT = [a.sb(f"{tag}cT{k}", [P, 2, DC, S]) for k in range(2)]
            gst = [a.sb(f"{tag}gst{k}", [2 * NH, S]) for k in range(2)]
            x_in = g.x_in
            c_in = [a.sem(f"{tag}_c_in{k}") for k in range(2)]
            stored = [a.sem(f"{tag}_stored{k}") for k in range(2)]
            emptied = a.sem("g_emptied")
            later_in = a.sem("g_later_in")
        else:
            emptied = xt_ready
            zeros = a.sb("zeros", [P, D])
            zeroed, tables = a.sem("r_zeroed"), a.sem("r_tables")
        block = ctx.enter_context(nc.Block())
        R0, LOOPS = 3, (PAIRS - 4) // 2

        def run(eng, step, drain, chain=None, per=0):
            for r in range(R0):
                step(0, r, False)
            with eng.Fori(0, LOOPS) as i:
                if chain:
                    chain.enter(i, per)
                for r in range(R0, R0 + 2):
                    step(i, r, False)
                if chain:
                    chain.leave(LOOPS)
            step(LOOPS, R0, True)
            drain(LOOPS, R0)

        @block.sync
        def _(sp):
            if not first:
                load_weights(sp, g, d, None)
                sp.wait_ge(zeroed, 1)
                for t in range(NT // 8):
                    sp.dma_start(d.disp[t * 8 * P:(t + 1) * 8 * P, :].rearrange("(p r) n -> p r n", p=P),
                                 zeros[:, :].rearrange("p (o n) -> p o n", o=1).broadcast_to([P, 8, D])).then_inc(tables, 16)
                sp.wait_ge(tables, 16 * (NT // 8))
                return

            def load_x(p, s):
                load_rows(sp, g, d, p, s)

            def store(p):
                for k in range(2):
                    sp.wait_ge(kept, 2 * p + k + 1)
                    for w in range(2):
                        sp.dma_start(d.gt[w, bass.ds(2 * p + k, 1)].rearrange("b h t -> (b h) t"),
                                     gst[k][w * NH:(w + 1) * NH, :]).then_inc(stored[k], 16)

            def refill(p, s):
                sp.wait_ge(var_ready, p + 1)
                load_x(p + 2, s)
            later = [
                (g.wr[:, :, 0:E], d.gate_wT.rearrange("(c p) n -> p c n", p=P)),
                (g.coef[:, :], d.ln_scale.to_broadcast([P, D])),
                (g.gate_b[:, :], d.gate_b.to_broadcast([P, E])),
                (g.branch[:, 0:1], d.g_xattn.to_broadcast([P, 1])),
                (g.branch[:, 1:2], d.g_ffn.to_broadcast([P, 1])),
            ] + [(g.bias[b * NH:(b + 1) * NH, :], d.gbias) for b in range(HB)]
            refill(0, 0)
            refill(1, 1)
            for dst, src in later:
                sp.dma_start(dst, src).then_inc(later_in, 16)
            with sp.Fori(0, (PAIRS - 4) // 2) as i:
                for q in range(2):
                    refill(2 * i + q + 2, q)
                    store(2 * i + q)
            for p in range(PAIRS - 4, PAIRS):
                store(p)
            for k in range(2):
                sp.wait_ge(stored[k], 32 * PAIRS)
            sp.wait_ge(later_in, 16 * len(later))

        @block.vector
        def _(dve):
            ch = Chain(dve, chain)

            def measure(i, r):
                s, t0 = r % 2, 4 * (2 * i + r)
                if first:
                    dve.wait_ge(x_in[s], 16 * i + 16 * (r // 2 + 1))
                for k in range(4):
                    last = nc.vector.bn_stats(stats[:, s, k, :], g.xres[:, bass.ds(t0 + k, 1), :].rearrange("p a d -> p (a d)"))
                ch.link(last)
                nc.vector.memset(g.idle[:, 0:1], 0.0)
                for k in range(4):
                    last = nc.vector.bn_aggr(mv[:, s, k, :], stats[:, s, k, :])
                ch.link(last)
                nc.vector.tensor_copy(g.mu_all[:, bass.ds(t0, 4)], mv[:, s, :, 0])
                ch.link(nc.vector.tensor_scalar(var[:, s, :], mv[:, s, :, 1], LN_EPS, None, ALU.add))
                nc.vector.sem_inc(var_ready, 1)

            def norm(i, r):
                p, s, t0 = 2 * i + r, r % 2, 4 * (2 * i + r)
                dve.wait_ge(rs_ready, p + 1)
                nc.vector.tensor_copy(g.rs_all[:, bass.ds(t0, 4)], g.rs_stage[:, s, :])
                if r >= 2:
                    dve.wait_ge(turned, 2 * p - 2)
                for k in range(4):
                    last = nc.vector.tensor_scalar(xn[:, s, k, :], g.xres[:, bass.ds(t0 + k, 1), :].rearrange("p a d -> p (a d)"),
                                                   mv[:, s, k, 0:1], g.rs_stage[:, s, k:k + 1],
                                                   ALU.subtract, ALU.mult)
                last.then_inc(xn_ready, 1)
            if not first:
                nc.vector.memset(zeros[:, :], 0.0).then_inc(zeroed, 1)
            measure(0, 0)

            def step(i, r, is_last):
                if not is_last:
                    measure(i, r + 1)
                norm(i, r)
            run(dve, step, lambda i, r: None, ch, 2 * 3)

        @block.gpsimd
        def _(pool):
            def step(i, r, is_last):
                p, s = 2 * i + r, r % 2
                pool.wait_ge(var_ready, p + 1)
                if r >= 2:
                    pool.wait_ge(xn_ready, p - 1)
                nc.gpsimd.tensor_tensor(g.rs_stage[:, s, :], var[:, s, :], g.neghalf[:, 0:4], ALU.pow).then_inc(rs_ready, 1)
            run(pool, step, lambda i, r: None)

        @block.tensor
        def _(pe):
            def turn(i, r):
                p, s = 2 * i + r, r % 2
                pe.wait_ge(xn_ready, p + 1)
                for k in range(2):
                    if r >= 1:
                        pe.wait_ge(emptied, 2 * p + k - 1)
                    for c in range(DC):
                        for j in range(2):
                            last = nc.tensor.transpose(psT[k][:, c, j * P:(j + 1) * P],
                                                       xn[:, s, 2 * k + j, c * P:(c + 1) * P], g.ident[:, :])
                    last.then_inc(turned, 1)

            def project(i, r):
                p, s = 2 * i + r, r % 2
                for k in range(2):
                    n = 2 * p + k
                    pe.wait_ge(xt_ready, n + 1)
                    if first and k == 0:
                        pe.wait_ge(c_in[s], 16 * i + 16 * (r // 2 + 1))
                    if r >= 1:
                        pe.wait_ge(part_ready, n - 1)
                    for c in range(DC):
                        last = nc.tensor.matmul(psG[k][32 * c:32 * c + 32, 0:S], (g.wg if first else g.wr)[:, c, :],
                                                xT[k][:, c, :], start=True, stop=not first)
                    if first:
                        for c in range(DC):
                            last = nc.tensor.matmul(psG[k][32 * c:32 * c + 32, 0:S], g.wc[:, c, :], cT[s][:, k, c, :],
                                                    start=False, stop=True)
                    last.then_inc(projected, 1)

            def fold(i, r):
                p = 2 * i + r
                for k in range(2):
                    n = 2 * p + k
                    pe.wait_ge(part_ready, n + 1)
                    if r >= 1:
                        pe.wait_ge(kept, n - 1)
                    if first:
                        last = nc.tensor.matmul(psF[k][0:2 * NH, 0:S], g.fold[:, :], part[k][:, :], start=True, stop=True)
                    else:
                        for j in range(2):
                            last = nc.tensor.matmul(psF[k][:, j * E:(j + 1) * E], part[k][:, j * P:(j + 1) * P],
                                                    g.fold[:, 0:E], start=True, stop=True)
                    last.then_inc(folded, 1)

            def step(i, r, is_last):
                turn(i, r)
                if r >= 1:
                    fold(i, r - 1)
                project(i, r)
            run(pe, step, fold)

        @block.scalar
        def _(act):
            def load_c(p, s):
                act.dma_start(cT[s][:, :, :, :],
                             d.ctxT[bass.ds(2 * p, 2)].rearrange("b (c p) t -> p b c t", p=P)).then_inc(c_in[s], 16)

            def copy(i, r):
                p = 2 * i + r
                for k in range(2):
                    n = 2 * p + k
                    act.wait_ge(turned, n + 1)
                    if r >= 1:
                        act.wait_ge(projected, n - 1)
                    nc.scalar.activation(xT[k][:, :, :], psT[k][:, :, :], ACT.Copy).then_inc(xt_ready, 1)
                    if first:
                        nc.scalar.activation(g.qT_all[:, bass.ds(n * DC, DC), :], psT[k][:, :, :],
                                             ACT.Copy).then_inc(emptied, 1)

            def sums(i, r):
                p = 2 * i + r
                for k in range(2):
                    n = 2 * p + k
                    act.wait_ge(projected, n + 1)
                    if r >= 1:
                        act.wait_ge(folded, n - 1)
                    nc.scalar.activation(part[k][:, :], psG[k][:, 0:S], ACT.Copy).then_inc(part_ready, 1)

            def keep(i, r):
                p = 2 * i + r
                for k in range(2):
                    n = 2 * p + k
                    act.wait_ge(folded, n + 1)
                    if first:
                        if r >= 1:
                            act.wait_ge(stored[k], 32 * p)
                        out, src = gst[k][:, :], psF[k][0:2 * NH, 0:S]
                    else:
                        out, src = g.logits[:, bass.ds(2 * n, 2), :], psF[k][:, 0:2 * E].rearrange("p (j e) -> p j e", e=E)
                    nc.scalar.activation(out, src, ACT.Copy).then_inc(kept, 1)

            if first:
                load_c(0, 0)
                load_c(1, 1)

            def step(i, r, is_last):
                if first and r >= 1 and not is_last:
                    load_c(2 * i + r + 1, (r + 1) % 2)
                copy(i, r)
                if r >= 1:
                    keep(i, r - 1)
                sums(i, r)
            run(act, step, keep)


def log1p_exp(nc, c, e, log_u, poly, mask):
    nc.vector.tensor_scalar(mask, e, SMALL_E, None, ALU.is_lt)
    c.link(nc.vector.tensor_scalar(poly, e, -0.25, 1.0 / 3.0, ALU.mult, ALU.add))
    c.link(nc.vector.tensor_tensor(poly, poly, e, ALU.mult))
    c.link(nc.vector.scalar_tensor_tensor(out=poly, in0=poly, scalar=0.5, in1=e, op0=ALU.subtract, op1=ALU.mult))
    c.link(nc.vector.scalar_tensor_tensor(out=poly, in0=poly, scalar=1.0, in1=e, op0=ALU.add, op1=ALU.mult))
    c.link(nc.vector.copy_predicated(log_u, mask.bitcast(U32), poly))


def gate_stage(nc, g, d):
    with ExitStack() as ctx:
        a = Pools(nc, ctx)
        e, lu, poly, mask, f = [a.sb("g" + n, [P, 2, S]) for n in ("e", "lu", "poly", "mask", "f")]
        ones = a.sb("gones", [P, S])
        head = a.sb("ghead", [P, 2, 2, S])
        F = a.sb("gF", [P, 2, S])
        am = a.sb("gam", [P, 2, 2, S])
        M = a.sb("gM", [P, 2, S])
        m = a.sb("gm", [P, 2, S])
        ex = a.sb("gex", [P, 2, 4, P])
        rest = a.sb("grest", [P, 2, 2, S])
        parts = a.sb("gparts", [P, 2, 2, 3, S], BF16)
        psE = [a.ps(f"gpsE{k}", [P, 4, P]) for k in range(2)]
        chain, abs_ready, e_ready, exps_go, exps, ex_turned, saved = map(
            a.sem, ["gt_" + n for n in ("chain", "abs", "e", "exps_go", "exps", "ex_turned", "saved")])
        parts_ready, tanh_ready, part_made, rest_ready = map(a.sem, ("gt_parts", "gt_tanh", "gt_part_made", "gt_rest"))
        head_in = [a.sem(f"gt_head_in{k}") for k in range(2)]
        block = ctx.enter_context(nc.Block())

        @block.vector
        def _(dve):
            c = Chain(dve, chain)
            nc.vector.memset(ones[:, :], 1.0)
            dve.wait_ge(tanh_ready, 1)
            nc.vector.tensor_scalar(g.coef[:, :], g.coef[:, :], g.tanh[:, 0:1], None, ALU.mult)
            for k in range(2):
                dve.wait_ge(head_in[k], 16)
                last = nc.vector.tensor_scalar(f[:, k, :], head[:, k, 1, :], g.bias[:, 1:2], None, ALU.add)
            c.link(last)
            nc.vector.scalar_tensor_tensor(out=poly[:, :, :], in0=f[:, :, :], scalar=-1.0, in1=f[:, :, :], op0=ALU.mult,
                                           op1=ALU.max).then_inc(abs_ready, 1)
            dve.wait_ge(e_ready, 2)
            log1p_exp(nc, c, e[:, :, :], lu[:, :, :], poly[:, :, :], mask[:, :, :])
            c.link(nc.vector.scalar_tensor_tensor(out=f[:, :, :], in0=f[:, :, :], scalar=0.0, in1=lu[:, :, :],
                                                  op0=ALU.min, op1=ALU.subtract))
            for k in range(2):
                c.link(nc.vector.tensor_tensor_scan(F[:, k, :], ones[:, :], f[:, k, :], 0.0, ALU.mult, ALU.add))
                c.link(nc.vector.scalar_tensor_tensor(out=am[:, k, 0, :], in0=head[:, k, 0, :], scalar=g.bias[:, 0:1],
                                                      in1=F[:, k, :], op0=ALU.add, op1=ALU.subtract))
                c.link(nc.vector.tensor_tensor_scan(M[:, k, :], am[:, k, 0, :], am[:, k, 0, :], -3.0e38, ALU.max, ALU.max))
                nc.vector.tensor_scalar(am[:, k, 1, :], M[:, k, :], -1.0, None, ALU.mult)
                c.link(nc.vector.tensor_tensor(m[:, k, :], F[:, k, :], M[:, k, :], ALU.add))
                nc.vector.sem_inc(exps_go, 1)
                for q in range(3 if k == 1 else 0):
                    src = (am if q == 0 else rest)[:, k, :, :]
                    c.link(nc.vector.tensor_copy(parts[:, k, :, q, :], src))
                    if q < 2:
                        c.link(nc.vector.tensor_tensor(rest[:, k, :, :], src, parts[:, k, :, q, :], ALU.subtract))
            nc.vector.sem_inc(parts_ready, 1)
            for k in range(2):
                dve.wait_ge(ex_turned, k + 1)
                nc.vector.tensor_copy(g.tmE[:, :, k * P:(k + 1) * P], psE[k][:, :, :])

        @block.scalar
        def _(act):
            nc.scalar.activation(g.tanh[:, :], g.branch[:, :], ACT.Tanh).then_inc(tanh_ready, 1)
            act.wait_ge(abs_ready, 1)
            nc.scalar.activation(e[:, :, :], poly[:, :, :], ACT.Exp, scale=-1.0).then_inc(e_ready, 1)
            act.wait_ge(e_ready, 1)
            nc.scalar.activation(lu[:, :, :], e[:, :, :], ACT.Ln, bias=1.0).then_inc(e_ready, 1)
            for k in range(2):
                act.wait_ge(exps_go, k + 1)
                nc.scalar.activation(ex[:, k, 0, :], am[:, k, 0, 0:P], ACT.Exp, bias=am[:, k, 1, P - 1:P])
                nc.scalar.activation(ex[:, k, 1, :], am[:, k, 1, P:S], ACT.Exp, bias=M[:, k, P - 1:P])
                nc.scalar.activation(ex[:, k, 2:4, :].rearrange("p a t -> p (a t)"), m[:, k, :], ACT.Exp,
                                     scale=-1.0).then_inc(exps, 1)
                for q in range(3 if k == 0 else 0):
                    if q > 0:
                        act.wait_ge(rest_ready, q)
                    nc.scalar.activation(parts[:, 0, :, q, :], (am if q == 0 else rest)[:, 0, :, :],
                                         ACT.Copy).then_inc(part_made, 1)

        @block.tensor
        def _(pe):
            for k in range(2):
                pe.wait_ge(exps, k + 1)
                for q in range(4):
                    last = nc.tensor.transpose(psE[k][:, q, :], ex[:, k, q, :], g.ident[:, :])
                last.then_inc(ex_turned, 1)

        @block.gpsimd
        def _(pool):
            nc.gpsimd.memset(g.aml[:, :, :], 1.0)
            nc.gpsimd.memset(g.amr[:, :, :], 1.0)
            for q in range(2):
                pool.wait_ge(part_made, q + 1)
                nc.gpsimd.tensor_tensor(rest[:, 0, :, :], (am if q == 0 else rest)[:, 0, :, :], parts[:, 0, :, q, :],
                                        ALU.subtract).then_inc(rest_ready, 1)

        @block.sync
        def _(sp):
            for k in range(2):
                sp.dma_start(head[:, k, :, :], d.gt.rearrange("w b h t -> (b h) w t")[k * P:(k + 1) * P]).then_inc(head_in[k], 16)
            for k in range(2):
                if k == 0:
                    sp.wait_ge(part_made, 3)
                else:
                    sp.wait_ge(parts_ready, 1)
                for w in range(2):
                    sp.dma_start(d.am[w].rearrange("q b h t -> (b h) q t")[k * P:(k + 1) * P], parts[:, k, w, :, :]).then_inc(saved, 16)
            sp.wait_ge(saved, 64)


def attention_stage(nc, g, d):
    with ExitStack() as ctx:
        a = Pools(nc, ctx)
        ctxs = a.sb("ctxs", [P, 2, D])
        kT = [a.sb(f"kT{k}", [P, DC, S]) for k in range(2)]
        vaug = [a.sb(f"vaug{k}", [P, 2, NH, DH + 1]) for k in range(2)]
        kkw = a.sb("kkw", [P, NH, DH])
        qst = [a.sb(f"qst{k}", [P, DC, S]) for k in range(2)]
        aml, amr = g.aml, g.amr
        dec = [a.sb(f"dec{k}", [P, 4, 4, P]) for k in range(2)]
        state = a.sb("state", [P, DC, 4, DH + 1])
        num = [a.sb(f"num{k}", [P, NH, DH + 1]) for k in range(2)]
        cen = [a.sb(f"cen{k}", [P, NH, DH]) for k in range(2)]
        sm = a.sb("sm", [P, 4, 8, NH])
        psQ = a.ps("psQ", [P, 4, 512])
        psL = a.ps("psL", [P, 4, P])
        psT = a.ps("psT", [P, DC, P])
        psO = a.ps("psO", [P, 2, 512])
        outT = a.sb("outT", [P, DC, P])
        sumT = a.sb("sumT", [P, P])
        pick = a.sb("pick", [P, DC, 32])
        (chain, am_done, dec_ready, qk_done, c_done, pv_done, si_done, si_evac, num_ready, cen_ready, sq_ready,
         ve_ready, hn_ready, x_done, v_ready, kk_ready, qs_ready, pch, ones_set, state_zero, out_copied, back_done,
         pick_set) = map(
            a.sem, ["at_" + n for n in (
                "chain", "am_done", "dec_ready", "qk_done", "c_done", "pv_done", "si_done", "si_evac", "num_ready",
                "cen_ready", "sq_ready", "ve_ready", "hn_ready", "x_done", "v_ready", "kk_ready", "qs_ready", "pool",
                "ones_set", "state_zero", "out_copied", "back_done", "pick_set")])
        ctx_in = a.sem("at_ctx_in")
        kT_in = [a.sem(f"at_kT_in{k}") for k in range(2)]
        am_in = [a.sem(f"at_am_in{k}") for k in range(2)]
        block = ctx.enter_context(nc.Block())
        R0, RPL, LOOPS = 3, 4, 7
        assert R0 + RPL * LOOPS + 1 == NT

        def run(eng, chain_obj, per, step, drain):
            for r in range(R0):
                step(0, r, False)
            with eng.Fori(0, LOOPS) as i:
                if chain_obj:
                    chain_obj.enter(i, per)
                for r in range(R0, R0 + RPL):
                    step(i, r, False)
                if chain_obj:
                    chain_obj.leave(LOOPS)
            step(LOOPS, R0, True)
            drain(LOOPS, R0)

        @block.sync
        def _(sp):
            def load_ctx(b):
                sp.dma_start(ctxs[:, :, :], d.ctx[bass.ds(b, 1)].rearrange("b (t p) d -> p (b t) d", p=P)).then_inc(ctx_in, 16)

            def load_keys(b, u):
                sp.dma_start(kT[u][:, :, :], d.ctxT[bass.ds(b, 1)].rearrange("b (c p) t -> p (b c) t", p=P)).then_inc(kT_in[u], 16)

            def load_decay(b, c):
                lo = 32 * c
                sp.dma_start(aml[lo + 3:lo + 6, :, :], d.am[0][:, bass.ds(b, 1), :, c * P:(c + 1) * P].rearrange(
                    "q b h t -> q (b h) t")).then_inc(am_in[c], 16)
                sp.dma_start(amr[lo:lo + 3, :, :], d.am[1][:, bass.ds(b, 1), :, c * P:(c + 1) * P].rearrange(
                    "q b h t -> q (b h) t")).then_inc(am_in[c], 16)
            load_decay(0, 0)
            load_keys(0, 0)
            load_ctx(0)
            load_decay(0, 1)

            def load(b, u, earlier):
                sp.wait_ge(am_done, 8 * b - 4)
                load_decay(b, 0)
                if earlier:
                    sp.wait_ge(qk_done, 8 * b - 8)
                load_keys(b, u)
                sp.wait_ge(v_ready, b)
                sp.wait_ge(kk_ready, b)
                load_ctx(b)
                sp.wait_ge(am_done, 8 * b)
                load_decay(b, 1)
            load(1, 1, False)
            with sp.Fori(0, B // 2 - 1) as i:
                load(2 * i + 2, 0, True)
                load(2 * i + 3, 1, True)

        @block.tensor
        def _(pe):
            def scores(i, r, k):
                n = 4 * i + r
                u, c = (r // 2) % 2, r % 2
                if k == 0:
                    pe.wait_ge(am_in[c], 64 * i + 32 * (r // 2 + 1))
                if 4 * r + k >= 1:
                    pe.wait_ge(dec_ready, 4 * n + k)
                for gg in range(4):
                    h = 4 * gg + k
                    nc.tensor.matmul(psL[:, gg, :], aml[32 * c:32 * c + 6, h, :], amr[32 * c:32 * c + 6, h, :],
                                     start=(gg == 0), stop=(gg == 3), skip_group_check=True)
                nc.tensor.matmul(psL[:, :, :], g.identb[:, :], g.causal[:, :, :], start=False, stop=True,
                                 skip_group_check=True).then_inc(am_done, 1)
                if k == 0 and c == 0:
                    pe.wait_ge(kT_in[u], 16 * i + 16 * (r // 4 + 1))
                    pe.wait_ge(qs_ready, 2 * i + r // 2 + 1)
                if r >= 1:
                    pe.wait_ge(c_done, 4 * n - 3 + k)
                for gg in range(4):
                    last = nc.tensor.matmul(psQ[:, k, gg * P:(gg + 1) * P], kT[u][32 * k:32 * k + 32, gg, c * P:(c + 1) * P],
                                            qst[u][32 * k:32 * k + 32, gg, c * P:(c + 1) * P], start=True, stop=True)
                last.then_inc(qk_done, 1)

            def values(i, r):
                n = 4 * i + r
                u, c = (r // 2) % 2, r % 2
                pe.wait_ge(c_done, 4 * n + 4)
                if r >= 1:
                    pe.wait_ge(out_copied, n)
                for gg in range(4):
                    for k in range(4):
                        nc.tensor.matmul(psT[32 * k:32 * k + 32, gg, :], vaug[u][:, c, 4 * gg + k, 0:DH],
                                         dec[c][:, k, gg, :], start=True, stop=True)
                if r == 0:
                    pe.wait_ge(pick_set, 1)
                pe.wait_ge(si_evac, n + 1)
                for gg in range(4):
                    for k in range(4):
                        last = nc.tensor.matmul(psO[32 * k:32 * k + 32, 1, 0:P], pick[:, gg, :], dec[c][:, k, gg, :],
                                                start=(gg == 0), stop=(gg == 3), skip_group_check=True)
                last.then_inc(pv_done, 1)

            def back(i, r):
                n = 4 * i + r
                pe.wait_ge(out_copied, n + 1)
                for gg in range(4):
                    nc.tensor.transpose(psO[:, 0, gg * P:(gg + 1) * P], outT[:, gg, :], g.ident[:, :])
                nc.tensor.transpose(psO[:, 1, P:2 * P], sumT[:, :], g.ident[:, :]).then_inc(back_done, 1)

            def carry(i, r):
                n = 4 * i + r
                u, c = (r // 2) % 2, r % 2
                if r >= 1:
                    pe.wait_ge(num_ready, n)
                if c == 0:
                    pe.wait_ge(kk_ready, 2 * i + r // 2 + 1)
                    pe.wait_ge(v_ready, 2 * i + r // 2 + 1)
                    for gg in range(4):
                        last = nc.tensor.matmul(psO[:, gg // 2, (gg % 2) * 132:(gg % 2) * 132 + 132],
                                                kkw[:, 4 * gg:4 * gg + 4, :].rearrange("p h d -> p (h d)"),
                                                vaug[u][:, 0, 4 * gg:4 * gg + 4, :].rearrange("p h d -> p (h d)"),
                                                start=True, stop=True)
                else:
                    for gg in range(4):
                        last = nc.tensor.matmul(psO[:, gg // 2, (gg % 2) * 132:(gg % 2) * 132 + 132], qst[u][:, gg, P:S],
                                                state[:, gg, :, :].rearrange("p h d -> p (h d)"), start=True, stop=True)
                last.then_inc(si_done, 1)

            def step(i, r, is_last):
                if r >= 1:
                    values(i, r - 1)
                scores(i, r, 0)
                scores(i, r, 1)
                if r >= 1:
                    back(i, r - 1)
                scores(i, r, 2)
                scores(i, r, 3)
                carry(i, r)

            def drain(i, r):
                values(i, r)
                back(i, r)
            run(pe, None, 0, step, drain)

        @block.scalar
        def _(act):
            def exps(i, r, k):
                n = 4 * i + r
                c = r % 2
                act.wait_ge(am_done, 4 * n + k + 1)
                if r >= 2 and k == 0:
                    act.wait_ge(pv_done, n - 1)
                nc.scalar.activation(dec[c][:, k, :, :], psL[:, :, :], ACT.Exp).then_inc(dec_ready, 1)

            def copy_out(i, r):
                n = 4 * i + r
                act.wait_ge(pv_done, n + 1)
                if r >= 1:
                    act.wait_ge(back_done, n)
                nc.scalar.activation(sumT[:, :], psO[:, 1, 0:P], ACT.Copy)
                nc.scalar.activation(outT[:, :, :], psT[:, :, :], ACT.Copy).then_inc(out_copied, 1)

            def values(i, r):
                n, b, u = 4 * i + r, 2 * i + r // 2, (r // 2) % 2
                if r >= 4:
                    act.wait_ge(pv_done, n - 2)
                    act.wait_ge(si_done, n - 2)
                nc.scalar.activation(qst[u][:, :, :], g.qT_all[:, bass.ds(b * DC, DC), :], ACT.Copy).then_inc(qs_ready, 1)
                act.wait_ge(ctx_in, 32 * i + 16 * (r // 2 + 1))
                nc.scalar.activation(vaug[u][:, :, :, 0:DH], ctxs[:, :, :].rearrange("p t (h d) -> p t h d", d=DH),
                                     ACT.Copy).then_inc(v_ready, 1)

            def square(i, r):
                n = 4 * i + r
                act.wait_ge(cen_ready, n + 1)
                nc.scalar.activation(num[r % 2][:, :, 0:DH], cen[r % 2][:, :, :], ACT.Square).then_inc(sq_ready, 1)
            act.wait_ge(ones_set, 1)
            values(0, 0)

            def step(i, r, is_last):
                exps(i, r, 0)
                if r >= 1:
                    copy_out(i, r - 1)
                exps(i, r, 1)
                if r >= 2:
                    square(i, r - 2)
                exps(i, r, 2)
                exps(i, r, 3)
                if r % 2 == 1 and not is_last:
                    values(i, r + 1)

            def drain(i, r):
                copy_out(i, r)
                square(i, r - 1)
                square(i, r)
            run(act, None, 0, step, drain)

        @block.vector
        def _(dve):
            c_ = Chain(dve, chain)

            def weigh(i, r, k):
                n = 4 * i + r
                c = r % 2
                dve.wait_ge(dec_ready, 4 * n + k + 1)
                dve.wait_ge(qk_done, 4 * n + k + 1)
                dk = dec[c][:, k, :, :].rearrange("p a t -> p (a t)")
                nc.vector.scalar_tensor_tensor(out=dk, in0=psQ[:, k, :], scalar=SCALE, in1=dk,
                                               op0=ALU.mult, op1=ALU.mult).then_inc(c_done, 1)

            def gather(i, r):
                n = 4 * i + r
                c = r % 2
                dve.wait_ge(back_done, n + 1)
                o = psO[:, 0, :].rearrange("p (h e) -> p h e", e=DH)
                total = psO[:, 1, P:2 * P].rearrange("p (k x) -> p x k", x=32)[:, 0:4, :]
                to, tt = num[c][:, :, 0:DH], num[c][:, :, DH].rearrange("p (x k) -> p x k", k=4)
                if c == 0:
                    nc.vector.tensor_copy(to, o)
                    c_.link(nc.vector.tensor_copy(tt, total))
                else:
                    nc.vector.tensor_tensor(to, to, o, ALU.add)
                    c_.link(nc.vector.tensor_tensor(tt, tt, total, ALU.add))
                nc.vector.sem_inc(num_ready, 1)

            def carry(i, r):
                n = 4 * i + r
                c = r % 2
                dve.wait_ge(si_done, n + 1)
                if c == 0:
                    for k in range(4):
                        src = psO[32 * k:32 * k + 32, :, 0:264].rearrange("p a (g h e) -> p a g h e", g=2, e=33)[:, :, :, k, :]
                        dst = state[32 * k:32 * k + 32, :, k, :].rearrange("p (a g) e -> p a g e", a=2)
                        last = nc.vector.tensor_scalar(dst, src, SCALE, None, ALU.mult)
                    last.then_inc(si_evac, 1)
                else:
                    o = psO[:, :, 0:264].rearrange("p a (h e) -> p a h e", e=33)
                    em = tm(1, i, r).rearrange("p (a h o) -> p a h o", a=2, o=1).broadcast_to([P, 2, 8, 33])
                    nc.vector.tensor_tensor(num[1][:, :, :].rearrange("p (a h) e -> p a h e", a=2), o, em,
                                            ALU.mult).then_inc(si_evac, 1)

            def tm(kind, i, r):
                return g.tmE[:, kind, bass.ds((2 * i + r // 2) * NH, NH)]

            def centre(i, r):
                n = 4 * i + r
                c, q = r % 2, r % 4
                v = sm[:, q]
                total = num[c][:, :, DH]
                nc.vector.tensor_reduce(v[:, 0, :], num[c][:, :, 0:DH], AX.X, ALU.add)
                c_.link(nc.vector.scalar_tensor_tensor(out=v[:, 2, :], in0=total, scalar=-1.0, in1=total,
                                                       op0=ALU.mult, op1=ALU.max))
                nc.vector.tensor_scalar(v[:, 1, :], v[:, 0, :], 1.0 / DH, None, ALU.mult)
                c_.link(nc.vector.tensor_tensor(v[:, 2, :], v[:, 2, :], tm(2 + c, i, r), ALU.max))
                nc.vector.tensor_tensor(cen[c][:, :, :], num[c][:, :, 0:DH],
                                        v[:, 1, :].rearrange("p (h o) -> p h o", o=1).broadcast_to([P, NH, DH]),
                                        ALU.subtract).then_inc(cen_ready, 1)
                c_.link(nc.vector.tensor_scalar(v[:, 2, :], v[:, 2, :], CELL_EPS, None, ALU.add))
                c_.link(nc.vector.reciprocal(v[:, 3, :], v[:, 2, :]))
                c_.link(nc.vector.tensor_tensor(v[:, 4, :], v[:, 3, :], v[:, 3, :], ALU.mult))

            def spread(i, r):
                n = 4 * i + r
                v = sm[:, r % 4]
                dve.wait_ge(sq_ready, n + 1)
                c_.link(nc.vector.tensor_reduce(v[:, 5, :], num[r % 2][:, :, 0:DH], AX.X, ALU.add))
                c_.link(nc.vector.scalar_tensor_tensor(out=v[:, 5, :], in0=v[:, 5, :], scalar=1.0 / DH, in1=v[:, 4, :],
                                                       op0=ALU.mult, op1=ALU.mult))
                nc.vector.tensor_scalar(v[:, 5, :], v[:, 5, :], CELL_EPS, None, ALU.add).then_inc(ve_ready, 1)

            def residual(i, r):
                n = 4 * i + r
                dve.wait_ge(hn_ready, n + 1)
                x = g.xres[:, bass.ds(n, 1), :].rearrange("p a d -> p (a d)")
                nc.vector.tensor_tensor(x, x, cen[r % 2][:, :, :].rearrange("p h d -> p (h d)"), ALU.add).then_inc(x_done, 1)

            nc.vector.memset(state[:, :, :, :], 0.0).then_inc(state_zero, 1)
            dve.wait_ge(state_zero, 1)

            def step(i, r, is_last):
                if r >= 1:
                    carry(i, r - 1)
                if r >= 2:
                    centre(i, r - 2)
                weigh(i, r, 0)
                if r >= 3:
                    residual(i, r - 3)
                weigh(i, r, 1)
                if r >= 1:
                    gather(i, r - 1)
                if r >= 2:
                    spread(i, r - 2)
                weigh(i, r, 2)
                weigh(i, r, 3)

            def drain(i, r):
                carry(i, r)
                centre(i, r - 1)
                gather(i, r)
                spread(i, r - 1)
                residual(i, r - 2)
                centre(i, r)
                spread(i, r)
                residual(i, r - 1)
                residual(i, r)
            run(dve, c_, 4 * 8, step, drain)

        @block.gpsimd
        def _(pool):
            c_ = Chain(pool, pch)
            for k in range(2):
                last = nc.gpsimd.memset(vaug[k][:, :, :, DH:DH + 1], 1.0)
            last.then_inc(ones_set, 1)
            c_.link(nc.gpsimd.memset(pick[:, :, :], 0.0))
            for q in range(DC):
                last = nc.gpsimd.memset(pick[:, q, q:q + 1], 1.0)
            last.then_inc(pick_set, 1)

            def keys(i, r):
                n, b = 4 * i + r, 2 * i + r // 2
                pool.wait_ge(ctx_in, 32 * i + 16 * (r // 2 + 1))
                if r >= 2:
                    pool.wait_ge(si_done, n - 1)
                kw = g.tmE[:, 0, bass.ds(b * NH, NH)].rearrange("p (h o) -> p h o", o=1).broadcast_to([P, NH, DH])
                nc.gpsimd.tensor_tensor(kkw[:, :, :], ctxs[:, 0, :].rearrange("p (h d) -> p h d", d=DH), kw,
                                        ALU.mult).then_inc(kk_ready, 1)

            def normalise(i, r):
                n = 4 * i + r
                q = r % 4
                v = sm[:, q]
                pool.wait_ge(ve_ready, n + 1)
                c_.link(nc.gpsimd.tensor_tensor(v[:, 6, :], v[:, 5, :], g.neghalf[:, 0:NH], ALU.pow))
                c_.link(nc.gpsimd.tensor_tensor(v[:, 7, :], v[:, 6, :], v[:, 3, :], ALU.mult))
                c_.link(nc.gpsimd.tensor_tensor(cen[r % 2][:, :, :], cen[r % 2][:, :, :],
                                                v[:, 7, :].rearrange("p (h o) -> p h o", o=1).broadcast_to([P, NH, DH]),
                                                ALU.mult))
                flat = cen[r % 2][:, :, :].rearrange("p h d -> p (h d)")
                nc.gpsimd.tensor_tensor(flat, flat, g.coef[:, :], ALU.mult).then_inc(hn_ready, 1)

            keys(0, 0)

            def step(i, r, is_last):
                if r >= 2:
                    normalise(i, r - 2)
                if r % 2 == 1 and not is_last:
                    keys(i, r + 1)

            def drain(i, r):
                normalise(i, r - 1)
                normalise(i, r)
            run(pool, c_, 4 * 4 - 4, step, drain)


def routing_stage(nc, g, d):
    with ExitStack() as ctx:
        a = Pools(nc, ctx)
        ab, e, lu, mask, sp, score, sel, tmp, pos = [a.sb("rt_" + n, [P, NT, E]) for n in
                                                     ("ab", "e", "lu", "mask", "sp", "score", "sel", "tmp", "pos")]
        oh = a.sb("rt_oh", [P, 2, NT, E])
        chosen = a.sb("rt_chosen", [P, NT, E], BF16)
        tot, keep, upto = [a.sb("rt_" + n, [P, E, NT]) for n in ("tot", "keep", "upto")]
        top = a.sb("rt_top", [P, NT, 8])
        topi = a.sb("rt_topi", [P, NT, 8], U32)
        idx, gk, pk, ok, slot = [a.sb("rt_" + n, [P, 2, NT]) for n in ("idx", "gk", "pk", "ok", "slot")]
        den = a.sb("rt_den", [P, NT])
        ps_before = a.ps("rt_before", [P, NT, E])
        ps_total = a.ps("rt_total", [P, NT, E])
        chain, abs_ready, e_ready, sp_ready, score_ready, chosen_ready, counted = map(
            a.sem, ["rt_" + n for n in ("chain", "abs", "e_ready", "sp_ready", "score_ready", "chosen_ready", "counted")])
        w_high, gk_ready, pool_chain = a.sem("rt_w_high"), a.sem("rt_gk"), a.sem("rt_pool")
        picked = a.sb("rt_picked", [P, 2, NT, E])
        w_pieces = [(g.raw13[:, c, :], g.w13[0][:, c, :], g.w13[1][:, c, :]) for c in range(DC)]
        w_pieces += [(g.raw2[:, 0:FC - 1, :], g.w2[0][:, 0:FC - 1, :], g.w2[1][:, 0:FC - 1, :]),
                     tuple(w[0:FLAST, FC - 1, :] for w in (g.raw2, g.w2[0], g.w2[1]))]
        block = ctx.enter_context(nc.Block())

        @block.gpsimd
        def _(pool):
            for n, (whole, high, low) in enumerate(w_pieces):
                pool.wait_ge(w_high, n + 1)
                nc.gpsimd.tensor_tensor(low, whole, high.bitcast(F32), ALU.subtract)
            c = Chain(pool, pool_chain)
            pool.wait_ge(chosen_ready, 1)
            every = score[:, :, :].rearrange("p (o t) e -> p o t e", o=1).broadcast_to([P, 2, NT, E])
            c.link(nc.gpsimd.tensor_tensor(picked[:, :, :, :], every, oh[:, :, :, :], ALU.mult))
            n = E // 2
            while n > 1:
                c.link(nc.gpsimd.tensor_tensor(picked[:, :, :, 0:n], picked[:, :, :, 0:n], picked[:, :, :, n:2 * n], ALU.add))
                n //= 2
            nc.gpsimd.tensor_tensor(gk[:, :, :], picked[:, :, :, 0], picked[:, :, :, 1], ALU.add).then_inc(gk_ready, 1)

        @block.vector
        def _(dve):
            c = Chain(dve, chain)
            l = g.logits[:, :, :]
            nc.vector.scalar_tensor_tensor(out=ab[:, :, :], in0=l, scalar=-1.0, in1=l, op0=ALU.mult,
                                           op1=ALU.max).then_inc(abs_ready, 1)
            dve.wait_ge(e_ready, 2)
            log1p_exp(nc, c, e[:, :, :], lu[:, :, :], ab[:, :, :], mask[:, :, :])
            nc.vector.scalar_tensor_tensor(out=sp[:, :, :], in0=l, scalar=0.0, in1=lu[:, :, :], op0=ALU.max,
                                           op1=ALU.add).then_inc(sp_ready, 1)
            dve.wait_ge(score_ready, 1)
            bias = g.gate_b[:, :].rearrange("p (o e) -> p o e", o=1).broadcast_to([P, NT, E])
            c.link(nc.vector.tensor_tensor(sel[:, :, :], score[:, :, :], bias, ALU.add))
            for t in range(NT):
                last = nc.vector.max(top[:, t, :], sel[:, t, :])
            c.link(last)
            for t in range(NT):
                last = nc.vector.max_index(topi[:, t, :], top[:, t, :], sel[:, t, :])
            c.link(last)
            ids = g.eiota[:, :].rearrange("p (o e) -> p o e", o=1).broadcast_to([P, NT, E])
            for k in range(2):
                c.link(nc.vector.tensor_copy(idx[:, k, :], topi[:, :, k]))
                mine = idx[:, k, :].rearrange("p (t o) -> p t o", o=1).broadcast_to([P, NT, E])
                c.link(nc.vector.tensor_tensor(oh[:, k, :, :], ids, mine, ALU.is_equal))
            nc.vector.tensor_tensor(chosen[:, :, :], oh[:, 0, :, :], oh[:, 1, :, :], ALU.add).then_inc(chosen_ready, 1)
            c.link(nc.vector.memset(keep[:, :, :], 1.0))
            c.link(nc.vector.memset(keep[:, :, 0:1], 0.0))
            dve.wait_ge(counted, 1)
            c.link(nc.vector.tensor_copy(tot[:, :, :], ps_total[:, :, :].rearrange("p t e -> p e t")))
            flat = lambda x: x[:, :, :].rearrange("p e t -> p (e t)")
            c.link(nc.vector.tensor_tensor_scan(flat(upto), flat(keep), flat(tot), 0.0, ALU.mult, ALU.add))
            c.link(nc.vector.tensor_tensor(upto[:, :, :], upto[:, :, :], tot[:, :, :], ALU.subtract))
            c.link(nc.vector.tensor_tensor(pos[:, :, :], upto[:, :, :].rearrange("p e t -> p t e"), ps_before[:, :, :], ALU.add))
            for k in range(2):
                c.link(nc.vector.tensor_tensor(tmp[:, :, :], pos[:, :, :], oh[:, k, :, :], ALU.mult))
                c.link(nc.vector.tensor_reduce(pk[:, k, :], tmp[:, :, :], AX.X, ALU.add))
            c.link(nc.vector.tensor_scalar(ok[:, :, :], pk[:, :, :], float(CAP), None, ALU.is_lt))
            dve.wait_ge(gk_ready, 1)
            c.link(nc.vector.tensor_tensor(den[:, :], gk[:, 0, :], gk[:, 1, :], ALU.add))
            c.link(nc.vector.reciprocal(den[:, :], den[:, :]))
            c.link(nc.vector.tensor_tensor(gk[:, :, :], gk[:, :, :],
                                           den[:, :].rearrange("p (o t) -> p o t", o=1).broadcast_to([P, 2, NT]), ALU.mult))
            c.link(nc.vector.scalar_tensor_tensor(out=g.weight[:, :, :], in0=gk[:, :, :], scalar=g.tanh[:, 1:2],
                                                  in1=ok[:, :, :], op0=ALU.mult, op1=ALU.mult))
            c.link(nc.vector.scalar_tensor_tensor(out=slot[:, :, :], in0=idx[:, :, :], scalar=float(CAP), in1=pk[:, :, :],
                                                  op0=ALU.mult, op1=ALU.add))
            c.link(nc.vector.tensor_scalar(ok[:, :, :], ok[:, :, :], -NOWHERE, NOWHERE, ALU.mult, ALU.add))
            c.link(nc.vector.tensor_tensor(slot[:, :, :], slot[:, :, :], ok[:, :, :], ALU.add))
            c.link(nc.vector.tensor_copy(g.slot[:, :, :], slot[:, :, :]))

        @block.scalar
        def _(act):
            act.wait_ge(abs_ready, 1)
            nc.scalar.activation(e[:, :, :], ab[:, :, :], ACT.Exp, scale=-1.0).then_inc(e_ready, 1)
            act.wait_ge(e_ready, 1)
            nc.scalar.activation(lu[:, :, :], e[:, :, :], ACT.Ln, bias=1.0).then_inc(e_ready, 1)
            for n, (whole, high, low) in enumerate(w_pieces):
                act.wait_ge(g.w_in[n], 16)
                nc.scalar.activation(high, whole, ACT.Copy).then_inc(w_high, 1)
            act.wait_ge(sp_ready, 1)
            nc.scalar.activation(score[:, :, :], sp[:, :, :], ACT.Sqrt).then_inc(score_ready, 1)

        @block.tensor
        def _(pe):
            pe.wait_ge(chosen_ready, 1)
            ch = chosen[:, :, :].rearrange("p t e -> p (t e)")
            nc.tensor.matmul(ps_before[:, :, :].rearrange("p t e -> p (t e)"), g.before[:, :], ch, start=True, stop=True)
            nc.tensor.matmul(ps_total[:, :, :].rearrange("p t e -> p (t e)"), g.onesb[:, :], ch, start=True,
                             stop=True).then_inc(counted, 1)


def load13(sp, g, d, expert, c):
    src = (d.ws13T[c * P:(c + 1) * P, :] if expert is None else
           d.w13T[bass.ds(expert, 1), c * P:(c + 1) * P, :].rearrange("e p n -> p (e n)"))
    sp.dma_start(g.raw13[:, c, :], src).then_inc(g.w_in[c], 16)


def load2(sp, g, d, expert):
    full = (FC - 1) * P
    if expert is None:
        two, one = d.ws2T[0:full, :].rearrange("(k p) n -> p k n", p=P), d.ws2T[full:FI, :]
    else:
        two = d.w2T[bass.ds(expert, 1), 0:full, :].rearrange("e (k p) n -> p (e k) n", p=P)
        one = d.w2T[bass.ds(expert, 1), full:FI, :].rearrange("e p n -> p (e n)")
    sp.dma_start(g.raw2[:, 0:FC - 1, :], two).then_inc(g.w_in[DC], 16)
    sp.dma_start(g.raw2[0:FLAST, FC - 1, :], one).then_inc(g.w_in[DC + 1], 16)


def load_weights(sp, g, d, expert):
    for c in range(DC):
        load13(sp, g, d, expert, c)
    load2(sp, g, d, expert)


class FfnBuffers:

    def __init__(self, g, a):
        slots = range(2)
        self.w13 = [g.w13, [a.sb(f"f_w13{p}", [P, DC, 2 * FI], F32R) for p in "hl"]]
        self.w2 = [g.w2, [a.sb(f"f_w2{p}", [P, FC, D], F32R) for p in "hl"]]
        self.xrows = [a.sb(f"f_xrows{k}", [P, 2, D]) for k in slots]
        self.xs = [[a.sb(f"f_x{p}{k}", [P, DC, S], F32R) for p in "hl"] for k in slots]
        self.hh = a.sb("f_hh", [P, FC, S])
        self.hs = [[a.sb(f"f_h{p}{k}", [P, FC, S], F32R) for p in "hl"] for k in slots]
        self.sg = a.sb("f_sg", [P, FC, S])
        self.ystage = [a.sb(f"ystage{k}", [P, 2, D]) for k in slots]
        self.sent = [self.ystage[k // 2][:, k % 2, :] for k in range(4)]
        self.got = [self.w13[0][k][:, :, :].rearrange("p c n -> p (c n)")[:, 0:4 * D].bitcast(F32).rearrange(
            "p (e j n) -> p e j n", e=2, j=2) for k in slots]
        self.psT = a.ps("f_psT", [P, DC, S])
        self.psH = [a.ps(f"f_psH{m}", [P, 2, S]) for m in range(FC)]
        self.psY = [a.ps(f"f_psY{j}", [P, D]) for j in range(2)]


def ffn_part(nc, g, d, b, a, kind, prev):
    shared, sending, collecting = kind != "experts", kind == "send", kind == "collect"
    COUNT = HB if shared else E
    FIRST = HB if collecting else 0
    tag = kind[0]
    class part:
        pass

    wslot = lambda r: {"send": 0, "experts": (r + 1) % 2, "collect": 1}[kind]
    rows = [P] * (FC - 1) + [FLAST]
    raw13, raw2, piece = g.raw13, g.raw2, g.w_in
    BEFORE = {"send": 0, "experts": 16, "collect": 16 * (E + 1)}[kind]
    w13, w2, xrows, xs, hh, hs, sg, psT, psH, psY = b.w13, b.w2, b.xrows, b.xs, b.hh, b.hs, b.sg, b.psT, b.psH, b.psY
    got, sent, ystage = b.got, b.sent, b.ystage
    names = ["turned", "h_done", "y_done", "xh_ready", "xl_ready", "sg_ready", "hh_done", "hh_high", "hl_ready",
             "wh13", "wh2", "wl13", "wl2"] + (["x_rows", "y_taken"] if shared else ["y_staged"])
    names += ["sent_ready", "hold"] if sending else []
    names += ["idx_ready", "hold", "chain", "done"] if collecting else []
    s = {n: a.sem(f"{tag}_{n}") for n in names}
    x_in = None if shared else [a.sem(f"{tag}_x_in{k}") for k in range(2)]
    y_out = None if shared else [a.sem(f"{tag}_y_out{k}") for k in range(2)]
    if sending:
        sidx = a.sb(tag + "sidx", [P, 4, 2], U32)
        sent_out = [a.sem(f"{tag}_sent_out{k}") for k in range(4)]
    if collecting:
        gidx = [a.sb(f"{tag}gidx{k}", [P, 2, 2], U32) for k in range(2)]
        got_in = [a.sem(f"{tag}_got_in{k}") for k in range(2)]
        out_done = [a.sem(f"{tag}_out_done{k}") for k in range(2)]
    R0, LOOPS = 3, (COUNT - 4) // 2

    def run(eng, step, chain=None, per=0):
        for r in range(R0):
            step(0, r, False)
        with eng.Fori(0, LOOPS) as i:
            if chain:
                chain.enter(i, per)
            for r in range(R0, R0 + 2):
                step(i, r, False)
            if chain:
                chain.leave(LOOPS)
        step(LOOPS, R0, True)

    def split13_high(i, r):
        for c in range(DC):
            nc.scalar.wait_ge(piece[c], BEFORE + (16 if shared else 32 * i + 16 * (r + 1)))
            nc.scalar.activation(w13[wslot(r)][0][:, c, :], raw13[:, c, :], ACT.Copy).then_inc(s["wh13"], 1)

    def split13_rest(i, r, c):
        q = 2 * i + r
        nc.vector.wait_ge(s["wh13"], DC * q + c + 1)
        nc.vector.tensor_tensor(w13[wslot(r)][1][:, c, :], raw13[:, c, :], w13[wslot(r)][0][:, c, :].bitcast(F32),
                                ALU.subtract).then_inc(s["wl13"], 1)

    END = (LOOPS, R0 + 1)

    def sync(sp, finish):
        def next13(q):
            for c in range(DC):
                sp.wait_ge(s["wh13"], DC * q - DC + c + 1)
                sp.wait_ge(s["wl13"], DC * q - DC + c + 1)
                load13(sp, g, d, q, c)

        def next2(q):
            sp.wait_ge(s["wh2"], 2 * q)
            sp.wait_ge(s["wl2"], 2 * q)
            load2(sp, g, d, q)

        def split_done(per, high, low):
            sp.wait_ge(s[high], per * (1 if shared else COUNT))
            sp.wait_ge(s[low], per * (1 if shared else COUNT))

        def load_rows(q, r, wait):
            if wait:
                sp.wait_ge(s["turned"], q - 1)
            sp.dma_start(xrows[r % 2][:, :, :], d.disp[bass.ds(q * CAP, CAP), :].rearrange(
                "(j p) n -> p j n", p=P)).then_inc(x_in[r % 2], 16)

        def store(q, r):
            sp.wait_ge(s["y_staged"], 2 * q + 2)
            sp.dma_start(d.yexp[bass.ds(q * CAP, CAP), :].rearrange("(j p) n -> p j n", p=P),
                         ystage[r % 2][:, :, :]).then_inc(y_out[r % 2], 16)

        if shared:
            if sending:
                load_weights(sp, g, d, 0)
            if collecting:
                def leave(b, k, n):
                    sp.wait_ge(s["done"], n)
                    sp.dma_start(d.out[bass.ds(b, 1)].rearrange("a (j p) n -> p (a j) n", p=P),
                                 g.xres[:, bass.ds(2 * b, 2), :]).then_inc(out_done[k], 16)

                def step(i, r, is_last):
                    q = 2 * i + r
                    if r >= 2:
                        leave(q + (FIRST - 2), 1, 2 * q - 1)
                    leave(q, 0, 2 * q if r >= 2 else q + 1)

                run(sp, step)
                q = 2 * END[0] + END[1]
                leave(q + (FIRST - 2), 1, 2 * q - 1)
                leave(q + (FIRST - 1), 1, 2 * q)
                for k in range(2):
                    sp.wait_ge(out_done[k], 16 * COUNT)
        else:
            next13(1)
            for k in range(4):
                sp.wait_ge(prev.sent_out[k], 32 * prev.COUNT)
            for r in range(2):
                sp.wait_ge(prev.s["turned"], prev.COUNT - 1 + r)
                load_rows(r, r, False)

            def ahead(q, r, results):
                load_rows(q + 2, r, True)
                next13(q + 2)
                next2(q + 1)
                if results:
                    store(q - 1, r - 1)
            ahead(0, 0, False)
            ahead(1, 1, True)
            with sp.Fori(0, (COUNT - 4) // 2) as i:
                for r in range(2, 4):
                    ahead(2 * i + r, r, True)
            next2(COUNT - 1)
            split_done(DC, "wh13", "wl13")
            for c in range(DC):
                load13(sp, g, d, None, c)
            store(COUNT - 3, COUNT - 3)
            store(COUNT - 2, COUNT - 2)
            split_done(2, "wh2", "wl2")
            load2(sp, g, d, None)
            store(COUNT - 1, COUNT - 1)
            for k in range(2):
                sp.wait_ge(y_out[k], 8 * COUNT)

    def tensor(pe, finish):
        def turn(i, r):
            q = 2 * i + r
            if shared:
                pe.wait_ge(s["x_rows"], q + 1)
            else:
                pe.wait_ge(x_in[r % 2], 16 * i + 16 * (r // 2 + 1))
            if r >= 1:
                pe.wait_ge(s["xl_ready"], q)
            elif prev:
                pe.wait_ge(prev.s["xl_ready"], prev.COUNT)
            for c in range(DC):
                for j in range(2):
                    last = nc.tensor.transpose(psT[:, c, j * P:(j + 1) * P], xrows[r % 2][:, j, c * P:(c + 1) * P],
                                               g.ident[:, :])
            last.then_inc(s["turned"], 1)

        def hidden(i, r, m):
            q, n = 2 * i + r, rows[m]
            w, x = w13[wslot(r)], xs[r % 2]
            if m == 0:
                pe.wait_ge(s["xl_ready"], q + 1)
                if collecting:
                    pe.wait_ge(s["wl13"], DC)
                    pe.wait_ge(s["wh13"], DC)
                elif not sending:
                    pe.wait_ge(s["wl13"], DC * q + DC)
                    pe.wait_ge(s["wh13"], DC * q + DC)
            if r >= 1:
                pe.wait_ge(s["hh_done"], 3 * q - 2 + m)
            elif prev:
                pe.wait_ge(prev.s["hh_done"], 3 * prev.COUNT - 2 + m)
            for v in range(2):
                for c in range(DC):
                    col = v * FI + m * P
                    for p, (wp, xp) in enumerate(((0, 0), (0, 1), (1, 0))):
                        last = nc.tensor.matmul(psH[m][0:n, v, :], w[wp][:, c, col:col + n], x[xp][:, c, :],
                                                start=(c == 0 and p == 0), stop=(c == DC - 1 and p == 2))
            last.then_inc(s["h_done"], 1)

        def back(i, r):
            q = 2 * i + r
            w, h = w2[wslot(r)], hs[r % 2]
            pe.wait_ge(s["hl_ready"], 3 * q + 3)
            if collecting:
                pe.wait_ge(s["wl2"], 2)
                pe.wait_ge(s["wh2"], 2)
            elif not sending:
                pe.wait_ge(s["wl2"], 2 * q + 2)
                pe.wait_ge(s["wh2"], 2 * q + 2)
            for j in range(2):
                if r >= 1:
                    pe.wait_ge(s["y_taken" if shared else "y_staged"], 2 * q - 1 + j)
                elif prev:
                    pe.wait_ge(prev.s["y_taken" if prev.shared else "y_staged"], 2 * prev.COUNT - 1 + j)
                for k in range(FC):
                    n = rows[k]
                    for p, (hp, wp) in enumerate(((0, 0), (0, 1), (1, 0))):
                        last = nc.tensor.matmul(psY[j][:, :], h[hp][0:n, k, j * P:(j + 1) * P], w[wp][0:n, k, :],
                                                start=(k == 0 and p == 0), stop=(k == FC - 1 and p == 2))
                last.then_inc(s["y_done"], 1)
        if shared:
            turn(0, 0)
        finish()
        if not shared:
            turn(0, 0)

        def step(i, r, is_last):
            hidden(i, r, 0)
            hidden(i, r, 1)
            if not is_last:
                turn(i, r + 1)
            hidden(i, r, 2)
            if r >= 1:
                back(i, r - 1)
        run(pe, step)
        return lambda: back(END[0], END[1] - 1)

    def scalar(act, finish):
        def split_x(i, r):
            q = 2 * i + r
            act.wait_ge(s["turned"], q + 1)
            nc.scalar.activation(xs[r % 2][0][:, :, :], psT[:, :, :], ACT.Copy).then_inc(s["xh_ready"], 1)

        def split2(i, r):
            act.wait_ge(piece[DC], BEFORE + (16 if shared else 32 * i + 16 * (r + 1)))
            nc.scalar.activation(w2[wslot(r)][0][:, 0:FC - 1, :], raw2[:, 0:FC - 1, :], ACT.Copy).then_inc(s["wh2"], 1)
            act.wait_ge(piece[DC + 1], BEFORE + (16 if shared else 32 * i + 16 * (r + 1)))
            nc.scalar.activation(w2[wslot(r)][0][0:FLAST, FC - 1, :], raw2[0:FLAST, FC - 1, :], ACT.Copy).then_inc(s["wh2"], 1)

        def silu(i, r, m):
            q, n = 2 * i + r, rows[m]
            act.wait_ge(s["h_done"], 3 * q + m + 1)
            if r >= 1:
                act.wait_ge(s["hh_done"], 3 * q - 2 + m)
            nc.scalar.activation(sg[0:n, m, :], psH[m][0:n, 0, :], ACT.Silu).then_inc(s["sg_ready"], 1)

        def high(i, r, m):
            q, n = 2 * i + r, rows[m]
            act.wait_ge(s["hh_done"], 3 * q + m + 1)
            nc.scalar.activation(hs[r % 2][0][0:n, m, :], hh[0:n, m, :], ACT.Copy).then_inc(s["hh_high"], 1)

        def stage(i, r):
            q = 2 * i + r
            if r >= 2:
                act.wait_ge(y_out[r % 2], 16 * i + 16 * (r // 2))
            else:
                for k in range(4):
                    act.wait_ge(prev.sent_out[k], 32 * prev.COUNT)
            for j in range(2):
                act.wait_ge(s["y_done"], 2 * q + j + 1)
                nc.scalar.activation(ystage[r % 2][:, j, :], psY[j][:, :], ACT.Copy).then_inc(s["y_staged"], 1)

        if collecting:
            split13_high(0, 0)
        split_x(0, 0)
        finish()

        def step(i, r, is_last):
            if not shared and r == 0:
                act.wait_ge(prev.s["h_done"], 3 * prev.COUNT)
                split13_high(i, 1)
            silu(i, r, 0)
            silu(i, r, 1)
            high(i, r, 0)
            if sending and is_last:
                part.after.split13_high(0, 0)
            if not is_last:
                split_x(i, r + 1)
            if not shared and r >= 1 and not is_last:
                split13_high(i, r + 1)
            silu(i, r, 2)
            high(i, r, 1)
            high(i, r, 2)
            if not shared or collecting and r == 0 and not is_last:
                split2(i, r)
            if not shared and r >= 1:
                stage(i, r - 1)
        run(act, step)
        return (lambda: None) if shared else (lambda: stage(END[0], END[1] - 1))

    def vector(dve, finish):
        ch = Chain(dve, s["chain"]) if collecting else None
        row = lambda t: g.xres[:, bass.ds(t, 1), :].rearrange("p a n -> p (a n)")

        def normed(out, t):
            return nc.vector.tensor_scalar(out, row(t), g.mu_all[:, bass.ds(t, 1)], g.rs_all[:, bass.ds(t, 1)],
                                           ALU.subtract, ALU.mult)

        def fetch(i, r):
            q = 2 * i + r
            if r >= 2:
                dve.wait_ge(s["turned"], q - 1)
            elif prev:
                dve.wait_ge(prev.s["turned"], prev.COUNT - 1 + r)
            for j in range(2):
                last = normed(xrows[r % 2][:, j, :], 2 * q + (2 * FIRST + j))
            last.then_inc(s["x_rows"], 1)

        def split_x(i, r):
            q = 2 * i + r
            dve.wait_ge(s["xh_ready"], q + 1)
            nc.vector.tensor_tensor(xs[r % 2][1][:, :, :], psT[:, :, :], xs[r % 2][0][:, :, :].bitcast(F32),
                                    ALU.subtract).then_inc(s["xl_ready"], 1)

        def split2(i, r):
            q = 2 * i + r
            h, l = w2[wslot(r)]
            dve.wait_ge(s["wh2"], 2 * q + 1)
            nc.vector.tensor_tensor(l[:, 0:FC - 1, :], raw2[:, 0:FC - 1, :], h[:, 0:FC - 1, :].bitcast(F32),
                                    ALU.subtract).then_inc(s["wl2"], 1)
            dve.wait_ge(s["wh2"], 2 * q + 2)
            nc.vector.tensor_tensor(l[0:FLAST, FC - 1, :], raw2[0:FLAST, FC - 1, :], h[0:FLAST, FC - 1, :].bitcast(F32),
                                    ALU.subtract).then_inc(s["wl2"], 1)

        def gated(i, r, m):
            q, n = 2 * i + r, rows[m]
            dve.wait_ge(s["sg_ready"], 3 * q + m + 1)
            if r >= 1:
                dve.wait_ge(s["hl_ready"], 3 * q - 2 + m)
            elif prev:
                dve.wait_ge(prev.s["hl_ready"], 3 * prev.COUNT - 2 + m)
            nc.vector.tensor_tensor(hh[0:n, m, :], sg[0:n, m, :], psH[m][0:n, 1, :], ALU.mult).then_inc(s["hh_done"], 1)

        def add(i, r):
            q = 2 * i + r
            for j in range(2):
                dve.wait_ge(s["y_done"], 2 * q + j + 1)
                x = row(2 * q + (2 * FIRST + j))
                nc.vector.scalar_tensor_tensor(out=x, in0=psY[j][:, :], scalar=g.tanh[:, 1:2], in1=x, op0=ALU.mult,
                                               op1=ALU.add).then_inc(s["y_taken"], 1)

        def send(i, r, k):
            q = 2 * i + r
            if r >= 1:
                dve.wait_ge(sent_out[k], 32 * q)
            normed(sent[k], 4 * q + k)
            nc.vector.tensor_copy(sidx[:, k, :], g.slot[:, :, bass.ds(4 * q + k, 1)].rearrange(
                "p k o -> p (k o)")).then_inc(s["sent_ready"], 1)

        def index(b, k):
            nc.vector.tensor_copy(gidx[k][:, :, :], g.slot[:, :, bass.ds(2 * b, 2)]).then_inc(s["idx_ready"], 1)

        def collect(b, k, n):
            dve.wait_ge(got_in[k], 64 * n)
            for e in range(2):
                for j in range(2):
                    x = row(2 * b + j)
                    last = nc.vector.scalar_tensor_tensor(out=x, in0=got[k][:, e, j, :],
                                                          scalar=g.weight[:, e, bass.ds(2 * b + j, 1)], in1=x,
                                                          op0=ALU.mult, op1=ALU.add)
                if e == 0:
                    ch.link(last)
            last.then_inc(s["done"], 1)

        if collecting:
            index(0, 0)
            index(FIRST, 1)
        if shared:
            fetch(0, 0)
        for c in range(DC if collecting else 0):
            split13_rest(0, 0, c)
        split_x(0, 0)
        finish()

        def step(i, r, is_last):
            q = 2 * i + r
            if shared and not is_last:
                fetch(i, r + 1)
            if collecting and r >= 2:
                dve.wait_ge(s["y_taken"], 2 * q - 2)
                collect(q + (FIRST - 2), 1, q - 1)
                index(q + (FIRST - 1), 1)
            if not shared and r == 0:
                for c in range(DC):
                    split13_rest(i, 1, c)
            if sending:
                send(i, r, 0)
                send(i, r, 1)
            gated(i, r, 0)
            if sending:
                send(i, r, 2)
                send(i, r, 3)
            gated(i, r, 1)
            if sending and is_last:
                for c in range(DC):
                    part.after.split13_rest(0, 0, c)
            if not is_last:
                split_x(i, r + 1)
            if not shared and r >= 1 and not is_last:
                for c in range(DC):
                    split13_rest(i, r + 1, c)
            if r == 0:
                gated(i, r, 2)
            if collecting:
                collect(q, 0, q + 1)
                index(q + FIRST if is_last else q + 1, 0)
            if r >= 1:
                gated(i, r, 2)
            if not shared or collecting and r == 0 and not is_last:
                split2(i, r)
            if shared and r >= 1:
                add(i, r - 1)

        def drain():
            i, r = END
            q = 2 * i + r
            if shared:
                add(i, r - 1)
            if collecting:
                dve.wait_ge(s["y_taken"], 2 * q)
                collect(q + (FIRST - 2), 1, q - 1)
                collect(q + (FIRST - 1), 0, q + 1)
        run(dve, step, ch if collecting else None, 2 * 2)
        return drain

    def gpsimd(pool, finish):
        last_row = pool.to_reg(E * CAP - 1) if shared else None
        hold = Chain(pool, s["hold"]) if shared else None

        def held():
            if not (isinstance(hold.base, int) and hold.base + hold.n == 0):
                pool.wait_ge(s["hold"], hold.base + hold.n)
            hold.n += 1
            nc.gpsimd.tensor_tensor(g.idle[:, 1:2], g.neghalf[:, 0:1], g.neghalf[:, 1:2], ALU.mult).then_inc(s["hold"], 1)

        def rest(i, r, m):
            q, n = 2 * i + r, rows[m]
            pool.wait_ge(s["hh_high"], 3 * q + m + 1)
            nc.gpsimd.tensor_tensor(hs[r % 2][1][0:n, m, :], hh[0:n, m, :], hs[r % 2][0][0:n, m, :].bitcast(F32),
                                    ALU.subtract).then_inc(s["hl_ready"], 1)

        def scatter(i, r, k):
            q = 2 * i + r
            pool.wait_ge(s["sent_ready"], 4 * q + k + 1)
            held()
            for e in range(2):
                nc.gpsimd.indirect_dma_start(
                    out=d.disp[:, :], out_offset=bass.IndirectOffsetOnAxis(ap=sidx[:, k, e:e + 1], axis=0),
                    in_=sent[k], in_offset=None, bounds_check=last_row, oob_is_err=False).then_inc(sent_out[k], 16)

        def gather(k, n):
            pool.wait_ge(s["idx_ready"], n)
            held()
            for e in range(2):
                for j in range(2):
                    nc.gpsimd.indirect_dma_start(
                        out=got[k][:, e, j, :], out_offset=None, in_=d.yexp[:, :],
                        in_offset=bass.IndirectOffsetOnAxis(ap=gidx[k][:, e, j:j + 1], axis=0),
                        bounds_check=last_row, oob_is_err=False).then_inc(got_in[k], 16)

        def step(i, r, is_last):
            q = 2 * i + r
            for m in range(FC):
                if sending and m < 2:
                    scatter(i, r, 2 * m)
                    scatter(i, r, 2 * m + 1)
                rest(i, r, m)
                if collecting and r >= 2 and m == 0:
                    gather(1, 2 * q + 1)
            if collecting:
                gather(0, 2 * q + 2 if r >= 2 else q + 3)

        if collecting:
            pool.wait_ge(prev.prev.s["hold"], 4 * HB)
            for k in range(2):
                pool.wait_ge(prev.y_out[k], 8 * prev.COUNT)
            gather(0, 1)
            gather(1, 2)
        run(pool, step, hold, 8 if sending else 4 if collecting else 0)
        return lambda: None

    part.split13_high, part.split13_rest = split13_high, split13_rest
    part.s, part.COUNT, part.shared, part.prev = s, COUNT, shared, prev
    part.sent_out = sent_out if sending else None
    part.y_out = y_out
    part.sync, part.tensor, part.scalar, part.vector, part.gpsimd = sync, tensor, scalar, vector, gpsimd
    return part


def ffn_stage(nc, g, d):
    with ExitStack() as ctx:
        a = Pools(nc, ctx)
        b = FfnBuffers(g, a)
        send = ffn_part(nc, g, d, b, a, "send", None)
        experts = ffn_part(nc, g, d, b, a, "experts", send)
        parts = [send, experts, ffn_part(nc, g, d, b, a, "collect", experts)]
        send.after = experts
        block = ctx.enter_context(nc.Block())

        @block.sync
        def _(sp):
            for part in parts:
                part.sync(sp, None)

        @block.tensor
        def _(pe):
            finish = lambda: None
            for part in parts:
                finish = part.tensor(pe, finish)
            finish()

        @block.scalar
        def _(act):
            finish = lambda: None
            for part in parts:
                finish = part.scalar(act, finish)
            finish()

        @block.vector
        def _(dve):
            finish = lambda: None
            for part in parts:
                finish = part.vector(dve, finish)
            finish()

        @block.gpsimd
        def _(pool):
            finish = lambda: None
            for part in parts:
                finish = part.gpsimd(pool, finish)
            finish()


def build(nc, d):
    with ExitStack() as ctx:
        a = Pools(nc, ctx)

        class g:
            xres = a.sb("xres", [P, NT, D])
            ident = a.sb("ident", [P, P])
            identb = a.sb("identb", [P, P], BF16)
            causal = a.sb("causal", [P, 4, P], BF16)
            before = a.sb("before", [P, P], BF16)
            onesb = a.sb("onesb", [P, P], BF16)
            neghalf = a.sb("neghalf", [P, NH])
            eiota = a.sb("eiota", [P, E])
            wr = a.sb("wr", [P, DC, 32])
            fold = a.sb("fold", [P, 32])
            bias = a.sb("bias", [P, 2])
            coef = a.sb("coef", [P, D])
            gate_b = a.sb("gate_b_rows", [P, E])
            branch = a.sb("branch", [P, 2])
            tanh = a.sb("tanh", [P, 2])
            mu_all = a.sb("mu_all", [P, NT])
            rs_all = a.sb("rs_all", [P, NT])
            idle = a.sb("idle", [P, 2])
            rs_stage = a.sb("rs_stage", [P, 2, 4])
            x_in = [a.sem(f"x_in{k}") for k in range(2)]

        with ExitStack() as cell:
            c = Pools(nc, cell)
            g.qT_all = c.sb("qT_all", [P, B * DC, S])
            g.tmE = c.sb("tmE", [P, 4, B * NH])
            g.aml = c.sb("aml", [38, NH, P], BF16)
            g.amr = c.sb("amr", [38, NH, P], BF16)
            with ExitStack() as gates:
                t = Pools(nc, gates)
                g.wg = t.sb("wg", [P, DC, 2 * NH])
                g.wc = t.sb("wc", [P, DC, 2 * NH])
                setup_stage(nc, g, d)
                norm_project_stage(nc, g, d, True)
                gate_stage(nc, g, d)
            attention_stage(nc, g, d)
        g.weight = a.sb("weight", [P, 2, NT])
        g.slot = a.sb("slot", [P, 2, NT], U32)
        g.raw13 = a.sb("raw13", [P, DC, 2 * FI])
        g.raw2 = a.sb("raw2", [P, FC, D])
        g.w13 = [a.sb("w13" + p, [P, DC, 2 * FI], F32R) for p in "hl"]
        g.w2 = [a.sb("w2" + p, [P, FC, D], F32R) for p in "hl"]
        g.w_in = [a.sem(f"w_in{k}") for k in range(DC + 2)]
        with ExitStack() as router:
            g.logits = Pools(nc, router).sb("logits", [P, NT, E])
            norm_project_stage(nc, g, d, False)
            routing_stage(nc, g, d)
        ffn_stage(nc, g, d)


def kernel(**inputs):
    import numpy as _np
    import concourse.bacc as _bacc
    from concourse import mybir as _mybir
    from concourse.bass_utils import run_bass_kernel_spmd as _run

    nc = _bacc.Bacc("TRN2", target_bir_lowering=False, num_devices=1)
    v = {k: _np.asarray(x) for k, x in inputs.items()}
    cat = lambda *xs: _np.concatenate(xs, axis=-1)
    w1, w3, w2 = v["L0_ffn_W1"], v["L0_ffn_W3"], v["L0_ffn_W2"]
    arrays = {
        "x": v["x"], "ctx": v["ctx_2048"], "ctxT": v["ctx_2048"].transpose(0, 2, 1),
        "g_xattn": v["g_xattn"].reshape(1, 1), "g_ffn": v["g_ffn"].reshape(1, 1),
        "wgate": cat(v["L0_xattn_Wi"], v["L0_xattn_Wf"]).reshape(3, D, 2 * NH),
        "gbias": cat(v["L0_xattn_bi"][:, None], v["L0_xattn_bf"][:, None]),
        "ln_scale": v["L0_xattn_ln_scale"].reshape(1, D),
        "gate_wT": v["L0_ffn_gate_w"].T, "gate_b": v["L0_ffn_gate_b"].reshape(1, E),
        "w13T": cat(w1.transpose(0, 2, 1), w3.transpose(0, 2, 1)), "w2T": w2.transpose(0, 2, 1),
        "ws13T": cat(v["L0_ffn_Ws1"].T, v["L0_ffn_Ws3"].T), "ws2T": v["L0_ffn_Ws2"].T,
    }
    arrays = {k: _np.ascontiguousarray(a) for k, a in arrays.items()}

    ins = {name: nc.dram_tensor(name, a.shape, _mybir.dt.from_np(a.dtype), kind="ExternalInput").ap()
           for name, a in arrays.items()}
    program(nc, ins)
    r = _run(nc, [arrays], core_ids=[0])
    return r.results[0]["out"]


class Dram:

    def __init__(self, ins, out, gt, am, disp, yexp):
        self.x, self.ctx, self.ctxT = ins["x"], ins["ctx"], ins["ctxT"]
        self.g_xattn, self.g_ffn, self.wgate, self.gbias = ins["g_xattn"], ins["g_ffn"], ins["wgate"], ins["gbias"]
        self.ln_scale, self.gate_wT, self.gate_b = ins["ln_scale"], ins["gate_wT"], ins["gate_b"]
        self.w13T, self.w2T, self.ws13T, self.ws2T = ins["w13T"], ins["w2T"], ins["ws13T"], ins["ws2T"]
        self.out, self.gt, self.am, self.disp, self.yexp = out, gt, am, disp, yexp


def program(nc, ins):
    out = nc.dram_tensor("out", (B, S, D), F32, kind="ExternalOutput").ap()
    gt = nc.dram_tensor("gates", (2, B, NH, S), F32, kind="Internal").ap()
    am = nc.dram_tensor("am", (2, 3, B, NH, S), BF16, kind="Internal").ap()
    disp = nc.dram_tensor("disp", (E * CAP, D), F32, kind="Internal").ap()
    yexp = nc.dram_tensor("yexp", (E * CAP, D), F32, kind="Internal").ap()
    build(nc, Dram(ins, out, gt, am, disp, yexp))
```
